# Optimizing a Trainium2 kernel written in Bass

```python
import numpy as np
import jax
import jax.numpy as jnp

def _softmax(x, axis=-1):
    return jax.nn.softmax(x, axis=axis)

def _gelu(x):
    return jax.nn.gelu(x, approximate=True)

def _silu(x):
    return jax.nn.silu(x)

def _sigmoid(x):
    return jax.nn.sigmoid(x)

def _layernorm(x, axis=-1, eps=1e-05):
    m = jnp.mean(x, axis=axis, keepdims=True)
    v = jnp.var(x, axis=axis, keepdims=True)
    return (x - m) / jnp.sqrt(v + eps)

def _scatter_add(tgt, idx, src, axis=0):
    return tgt.at[idx].add(src)

def _segment_sum(src, seg, n):
    return jax.ops.segment_sum(src, seg, n)
kernel_name = 'mk_gnn_ffn_d1_gnn_r8_e6436f'

def setup_inputs(seed: int=0):
    np.random.seed(seed)
    _w = jnp.asarray

    def _rec_inputs():
        import jax
        import jax.numpy as jnp
        _gk = jax.random.key(seed)
        x = -0.000364 + 1 * jax.random.normal(jax.random.fold_in(_gk, 1), (1250, 768), jnp.float32)
        src = jax.random.randint(jax.random.fold_in(_gk, 2), (20000,), 0, 1250, jnp.int32)
        dst = jax.random.randint(jax.random.fold_in(_gk, 3), (20000,), 0, 1250, jnp.int32)
        _o = jnp.argsort(dst, stable=True)
        src = src[_o]
        dst = dst[_o]
        return (x, src, dst)
    x, src, dst = _rec_inputs()

    def _L0_gnn_setup():
        import jax, jax.numpy as jnp
        import numpy as np
        N = 2500
        E_RAND = 40000
        NEG_SLOPE = 0.2

        def gat_layer(x, W, a_src, a_dst, bias, src, dst, heads, out_c, concat):
            n = x.shape[0]
            h = (x @ W).reshape(n, heads, out_c)
            al_s = jnp.einsum('nhc,hc->nh', h, a_src)
            al_d = jnp.einsum('nhc,hc->nh', h, a_dst)
            e = jax.nn.leaky_relu(al_s[src] + al_d[dst], NEG_SLOPE)
            m = jax.ops.segment_max(e, dst, num_segments=n)
            ex = jnp.exp(e - m[dst])
            z = jax.ops.segment_sum(ex, dst, num_segments=n)
            alpha = ex / (z[dst] + 1e-16)
            msg = h[src] * alpha[:, :, None]
            out = jax.ops.segment_sum(msg, dst, num_segments=n)
            out = out.reshape(n, heads * out_c) if concat else out.mean(axis=1)
            return out + bias
        key = jax.random.key(seed)
        ks = jax.random.split(key, 10)
        x = jax.random.normal(ks[0], (N, 768), dtype=jnp.float32)
        src = jax.random.randint(ks[1], (E_RAND,), 0, N)
        dst = jax.random.randint(ks[2], (E_RAND,), 0, N)
        loop = jnp.arange(N)
        edge_index = jnp.stack([jnp.concatenate([src, loop]), jnp.concatenate([dst, loop])])
        s = 1.0 / np.sqrt(768.0)
        W1 = jax.random.normal(ks[3], (768, 768), dtype=jnp.float32) * s
        a_src1 = jax.random.normal(ks[4], (8, 96), dtype=jnp.float32) * 0.1
        a_dst1 = jax.random.normal(ks[5], (8, 96), dtype=jnp.float32) * 0.1
        b1 = jnp.zeros((768,), dtype=jnp.float32)
        W2 = jax.random.normal(ks[6], (768, 768), dtype=jnp.float32) * s
        a_src2 = jax.random.normal(ks[7], (1, 768), dtype=jnp.float32) * 0.1
        a_dst2 = jax.random.normal(ks[8], (1, 768), dtype=jnp.float32) * 0.1
        b2 = jnp.zeros((768,), dtype=jnp.float32)
        return {'x': x, 'edge_index': edge_index, 'W1': W1, 'a_src1': a_src1, 'a_dst1': a_dst1, 'b1': b1, 'W2': W2, 'a_src2': a_src2, 'a_dst2': a_dst2, 'b2': b2}
    _L0_gnn_all = _L0_gnn_setup()
    _L0_gnn_in = {k: v for k, v in _L0_gnn_all.items() if k in ('W1', 'a_src1', 'a_dst1', 'b1', 'W2', 'a_src2', 'a_dst2', 'b2')}
    del _L0_gnn_all

    def _L0_ffn_setup():
        import jax, jax.numpy as jnp
        import numpy as np
        D = 768
        M = 384
        G = 4
        E = 8
        KG = 2
        KE = 4
        EPS = 1e-06

        def _topk_gates(logits, k):
            top, idx = jax.lax.top_k(logits, k)
            gates = jax.nn.softmax(top, axis=-1)
            gates = jnp.where(gates >= EPS, gates, jnp.zeros_like(gates))
            return (gates, idx)
        key = jax.random.key(seed)
        ks = jax.random.split(key, 9)
        x = jax.random.normal(ks[0], (1, 1024, D), dtype=jnp.float32)
        Wg = jax.random.normal(ks[1], (D, G), dtype=jnp.float32) * 0.02
        bg = jax.random.normal(ks[2], (G,), dtype=jnp.float32) * 0.01
        We = jax.random.normal(ks[3], (G, D, E), dtype=jnp.float32) * 0.02
        be = jax.random.normal(ks[4], (G, E), dtype=jnp.float32) * 0.01
        W1 = jax.random.normal(ks[5], (G, E, D, M), dtype=jnp.float32) * 0.02
        b1 = jax.random.normal(ks[6], (G, E, M), dtype=jnp.float32) * 0.01
        W2 = jax.random.normal(ks[7], (G, E, M, D), dtype=jnp.float32) * 0.02
        b2 = jax.random.normal(ks[8], (G, E, D), dtype=jnp.float32) * 0.01
        return {'x': x, 'Wg': Wg, 'bg': bg, 'We': We, 'be': be, 'W1': W1, 'b1': b1, 'W2': W2, 'b2': b2}
    _L0_ffn_all = _L0_ffn_setup()
    _L0_ffn_in = {k: v for k, v in _L0_ffn_all.items() if k in ('Wg', 'bg', 'We', 'be', 'W1', 'b1', 'W2', 'b2')}
    del _L0_ffn_all
    return {'x': x, 'src': src, 'dst': dst, 'L0_gnn_W1': _L0_gnn_in['W1'], 'L0_gnn_a_src1': _L0_gnn_in['a_src1'], 'L0_gnn_a_dst1': _L0_gnn_in['a_dst1'], 'L0_gnn_b1': _L0_gnn_in['b1'], 'L0_gnn_W2': _L0_gnn_in['W2'], 'L0_gnn_a_src2': _L0_gnn_in['a_src2'], 'L0_gnn_a_dst2': _L0_gnn_in['a_dst2'], 'L0_gnn_b2': _L0_gnn_in['b2'], 'L0_ffn_Wg': _L0_ffn_in['Wg'], 'L0_ffn_bg': _L0_ffn_in['bg'], 'L0_ffn_We': _L0_ffn_in['We'], 'L0_ffn_be': _L0_ffn_in['be'], 'L0_ffn_W1': _L0_ffn_in['W1'], 'L0_ffn_b1': _L0_ffn_in['b1'], 'L0_ffn_W2': _L0_ffn_in['W2'], 'L0_ffn_b2': _L0_ffn_in['b2']}

def reference(x, src, dst, L0_gnn_W1, L0_gnn_a_src1, L0_gnn_a_dst1, L0_gnn_b1, L0_gnn_W2, L0_gnn_a_src2, L0_gnn_a_dst2, L0_gnn_b2, L0_ffn_Wg, L0_ffn_bg, L0_ffn_We, L0_ffn_be, L0_ffn_W1, L0_ffn_b1, L0_ffn_W2, L0_ffn_b2):
    import jax
    import jax.numpy as jnp

    def _L0_gnn_ref(x, edge_index, W1, a_src1, a_dst1, b1, W2, a_src2, a_dst2, b2):
        import jax, jax.numpy as jnp
        import numpy as np
        N = 2500
        E_RAND = 40000
        NEG_SLOPE = 0.2

        def gat_layer(x, W, a_src, a_dst, bias, src, dst, heads, out_c, concat):
            n = x.shape[0]
            h = (x @ W).reshape(n, heads, out_c)
            al_s = jnp.einsum('nhc,hc->nh', h, a_src)
            al_d = jnp.einsum('nhc,hc->nh', h, a_dst)
            e = jax.nn.leaky_relu(al_s[src] + al_d[dst], NEG_SLOPE)
            m = jax.ops.segment_max(e, dst, num_segments=n)
            ex = jnp.exp(e - m[dst])
            z = jax.ops.segment_sum(ex, dst, num_segments=n)
            alpha = ex / (z[dst] + 1e-16)
            msg = h[src] * alpha[:, :, None]
            out = jax.ops.segment_sum(msg, dst, num_segments=n)
            out = out.reshape(n, heads * out_c) if concat else out.mean(axis=1)
            return out + bias
        src, dst = (edge_index[0], edge_index[1])
        h = gat_layer(x, W1, a_src1, a_dst1, b1, src, dst, heads=8, out_c=96, concat=True)
        h = jax.nn.elu(h)
        out = gat_layer(h, W2, a_src2, a_dst2, b2, src, dst, heads=1, out_c=768, concat=False)
        return out

    def _L0_ffn_ref(x, Wg, bg, We, be, W1, b1, W2, b2):
        import jax, jax.numpy as jnp
        import numpy as np
        D = 768
        M = 384
        G = 4
        E = 8
        KG = 2
        KE = 4
        EPS = 1e-06

        def _topk_gates(logits, k):
            top, idx = jax.lax.top_k(logits, k)
            gates = jax.nn.softmax(top, axis=-1)
            gates = jnp.where(gates >= EPS, gates, jnp.zeros_like(gates))
            return (gates, idx)
        orig_shape = x.shape
        xf = x.reshape(-1, D)
        glog = xf @ Wg + bg
        ggates, gidx = _topk_gates(glog, KG)
        gw = jnp.einsum('nk,nkg->ng', ggates, jax.nn.one_hot(gidx, G, dtype=xf.dtype))
        elog = jnp.einsum('nd,gde->nge', xf, We) + be
        egates, eidx = _topk_gates(elog, KE)
        ew = jnp.einsum('ngk,ngke->nge', egates, jax.nn.one_hot(eidx, E, dtype=xf.dtype))
        combine = gw[:, :, None] * ew
        y = jnp.zeros_like(xf)
        for g in range(G):
            h = jax.nn.gelu(jnp.einsum('nd,edm->enm', xf, W1[g]) + b1[g][:, None, :], approximate=False)
            o = jnp.einsum('enm,emd->end', h, W2[g]) + b2[g][:, None, :]
            y = y + jnp.einsum('end,ne->nd', o, combine[:, g, :])
        return y.reshape(orig_shape)
    edge_index = jnp.stack([src, dst])
    x = x + _L0_gnn_ref(_layernorm(x, axis=-1), edge_index, L0_gnn_W1, L0_gnn_a_src1, L0_gnn_a_dst1, L0_gnn_b1, L0_gnn_W2, L0_gnn_a_src2, L0_gnn_a_dst2, L0_gnn_b2)
    x = x + _L0_ffn_ref(_layernorm(x, axis=-1)[None], L0_ffn_Wg, L0_ffn_bg, L0_ffn_We, L0_ffn_be, L0_ffn_W1, L0_ffn_b1, L0_ffn_W2, L0_ffn_b2)[0]
    return x

_drawn_inputs = setup_inputs


def setup_inputs(seed=0):
    import zlib

    import numpy as np

    out = dict(_drawn_inputs(seed))
    spreads = {'L0_gnn_b1': (0.0, 0.1), 'L0_gnn_b2': (0.0, 0.1)}
    factors = {'L0_gnn_a_dst2': 3.075,
     'L0_ffn_bg': 26.803,
     'L0_ffn_be': 37.574,
     'L0_ffn_b1': 63.386,
     'L0_ffn_b2': 8.0}
    for name, (base, spread) in spreads.items():
        noise = np.random.default_rng([zlib.crc32(name.encode()), seed]).standard_normal(out[name].shape)
        drawn = base * np.exp(spread * noise) if base else spread * noise
        out[name] = jnp.asarray(drawn.astype(out[name].dtype))
    for name, factor in factors.items():
        out[name] = (out[name] * factor).astype(out[name].dtype)
    return out
```

```python
import concourse.bass as bass
from concourse import mybir
from contextlib import ExitStack

F32 = mybir.dt.float32
F32R = mybir.dt.float32r
BF16 = mybir.dt.bfloat16
I32 = mybir.dt.int32
I16 = mybir.dt.int16
U16 = mybir.dt.uint16
ALU = mybir.AluOpType
ACT = mybir.ActivationFunctionType
AX = mybir.AxisListType

P = 128
N = 1250
NT = -(-N // P)
NP = NT * P
TAIL = N - (NT - 1) * P
D = 768
KD = D // P
HALF = D // 2
EDGES = 20000
ET = -(-EDGES // P)
H1 = 8
C1 = D // H1
G = 4
EG = 8
E = G * EG
RC = G + E
TW = D + 2 * E
KG = 2
KE = 4
PAIRS = N * KG * KE
NO_SLOT = 2 * PAIRS
GATE_MIN = 1e-6
MIN_TILES = 2
LIST = PAIRS // P + 1 + MIN_TILES * E + NT
HID = 384
KH = HID // P
RING = 4
SLOPE = 0.2
LN_EPS = 1e-5
NOT_A_NEIGHBOUR = -1e30
PARTS = ((0, 512), (512, 512), (1024, 256))


class Shared:
    pass


def semaphore(nc, s, name):
    s.early.append(nc.alloc_semaphore(name=name))
    return s.early[-1]


def node_features(nc, s, x, w1, edge_src, edge_dst, att1):
    with ExitStack() as ctx:
        def sb(name, shape, dt=F32):
            return ctx.enter_context(nc.sbuf_tensor(name, shape, dt))

        def sem(name):
            return semaphore(nc, s, name)

        xs = sb("xs", [P, NT, D])
        w1_raw = sb("w1_raw", [P, KD, D])
        w1_t = sb("w1_t", [P, KD, D])
        att_col = sb("att_col", [P, 2, KD])
        att_low = sb("att_low", [P, 2, KD, H1])
        att_diag = sb("att_diag", [P, KD, 2, H1])
        wa = sb("wa", [P, KD, 2 * H1])
        stats = sb("stats", [P, NT, 2, 6])
        mv = sb("mv", [P, NT, 2])
        veps = sb("veps", [P, NT])
        rstd = sb("rstd", [P, 4, NT])
        xn = sb("xn", [P, 2, D])
        al_rows = sb("al_rows", [2 * H1, NP])
        edge_i = sb("edge_i", [P, 2, ET], I32)
        dst_hi = sb("dst_hi", [P, ET])
        tile_ids_i = sb("tile_ids_i", [P, 2], I32)
        tile_ids = sb("tile_ids", [P, 2])
        tile_rev = sb("tile_rev", [P, 2])
        block_i = sb("block_i", [P, NT], I32)
        block_lo = s.block_col
        block_hi = sb("block_hi", [P, NT])
        tmax = sb("tmax", [P, 2])
        tmin = sb("tmin", [P, 2])
        hit = sb("hit", [P, 2, NT])
        ge = sb("ge", [P, 2, NT])
        span = sb("span", [P, 2, 2 * NT])
        span_col = sb("span_col", [2 * NT, 1])
        span_row = sb("span_row", [1, 2 * NT])
        span_fix = sb("span_fix", [1, 2 * NT])

        ps_x = ctx.enter_context(nc.psum_tensor("ps_x", [P, 2, 2, 512], F32))
        ps_al = ctx.enter_context(nc.psum_tensor("ps_al", [P, 3, 512], F32))
        ps_m = ctx.enter_context(nc.psum_tensor("ps_m", [P, 512], F32))

        x_in, w_in, e_in, a_in = sem("x_in"), sem("w_in"), sem("e_in"), sem("a_in")
        consts, dve_step, act_step = sem("consts"), sem("dve_step"), sem("act_step")
        edge_step, ranged = sem("edge_step"), sem("ranged")
        pe_edges, pe_w1t, w1t_kept = sem("pe_edges"), sem("pe_w1t"), sem("w1t_kept")
        diag_low = sem("diag_low")
        diag, pe_wa, wa_kept = sem("diag"), sem("pe_wa"), sem("wa_kept")
        sqrt_done, normed, pe_xt, xt_kept = sem("sqrt_done"), sem("normed"), sem("pe_xt"), sem("xt_kept")
        pe_al, al_kept, pe_alc, stored = sem("pe_al"), sem("al_kept"), sem("pe_alc"), sem("stored")
        split_hi = sem("split_hi")
        id_done, stat_done = sem("id_done"), sem("stat_done")

        with nc.Block() as block:
            @block.sync
            def _(sp):
                sp.dma_start(edge_i[:, 0], edge_src).then_inc(e_in, 16)
                sp.dma_start(edge_i[:, 1], edge_dst).then_inc(e_in, 16)
                sp.dma_start(xs[:, :, :], x.rearrange("(t p) d -> p t d", p=P)).then_inc(x_in, 16)
                sp.wait_ge(al_kept, 3)
                sp.dma_start(s.al_dram.ap(), al_rows[:, :]).then_inc(stored, 16)
                sp.wait_ge(stored, 16)

            @block.gpsimd
            def _(pool):
                pool.dma_start(att_col[:, :, :], att1).then_inc(a_in, 16)
                nc.gpsimd.memset(s.ident[:, :], 0.0).then_inc(id_done, 1)
                nc.gpsimd.iota(tile_ids_i[:, :], [[P, 2]], base=0, channel_multiplier=1).then_inc(consts, 1)
                nc.gpsimd.iota(block_i[:, :], [[P, NT]], base=0, channel_multiplier=0).then_inc(consts, 1)
                nc.gpsimd.iota(s.column[:, :], [[1, NP]], base=0, channel_multiplier=0).then_inc(consts, 1)
                pool.wait_ge(id_done, 1)
                nc.gpsimd.affine_select(out=s.ident[:, :], in_=s.ident[:, :], compare_op=ALU.not_equal,
                                        fill=1.0, base=0, pattern=[[-1, P]],
                                        channel_multiplier=1).then_inc(consts, 1)
                pool.wait_ge(a_in, 16)
                for a in range(2):
                    nc.gpsimd.affine_select(out=att_low[:, a], compare_op=ALU.is_ge, fill=0.0,
                                            in_=att_col[:, a].unsqueeze(2).broadcast_to([P, KD, H1]),
                                            base=0, pattern=[[P, KD], [-C1, H1]],
                                            channel_multiplier=1).then_inc(diag_low, 1)
                pool.wait_ge(diag_low, 2)
                for a in range(2):
                    nc.gpsimd.affine_select(out=att_diag[:, :, a, :], in_=att_low[:, a], compare_op=ALU.is_ge,
                                            fill=0.0, base=C1 - 1, pattern=[[-P, KD], [C1, H1]],
                                            channel_multiplier=-1).then_inc(diag, 1)

            @block.vector
            def _(dve):
                step = [0]

                def then(ins):
                    step[0] += 1
                    ins.then_inc(dve_step, 1)
                    dve.wait_ge(dve_step, step[0])

                nc.vector.memset(tmax[:, :], -1.0)
                then(nc.vector.memset(tmin[:, :], 2.0 * NP))
                dve.wait_ge(e_in, 32)
                nc.vector.tensor_copy(s.src_f[:, :], edge_i[:, 0])
                then(nc.vector.tensor_copy(s.dst_f[:, :], edge_i[:, 1]))
                nc.vector.tensor_scalar(dst_hi[:, :], s.dst_f[:, :], 0.0, 4.0 * NP, ALU.is_lt, ALU.mult)
                dve.wait_ge(consts, 4)
                nc.vector.tensor_copy(tile_ids[:, :], tile_ids_i[:, :])
                nc.vector.tensor_copy(block_lo[:, :], block_i[:, :])
                then(nc.vector.memset(span[:, :, :], 0.0))
                nc.vector.tensor_scalar(block_hi[:, :], block_lo[:, :], float(P - 1), None, ALU.add)
                nc.vector.tensor_scalar(tile_rev[:, :], tile_ids[:, :], -1.0, float(ET), ALU.mult, ALU.add)
                nc.vector.tensor_scalar(tile_ids[:, :], tile_ids[:, :], 1.0, None, ALU.add)
                nc.vector.tensor_tensor(dst_hi[:, :], dst_hi[:, :], s.dst_f[:, :],
                                        ALU.add).then_inc(edge_step, 1)
                dve.wait_ge(pe_edges, 1)
                rest = ET - P
                nc.vector.tensor_reduce(tmax[:, 0:1], ps_m[:, 0:P], AX.X, ALU.max)
                nc.vector.tensor_reduce(tmax[0:rest, 1:2], ps_m[0:rest, P:2 * P], AX.X, ALU.max)
                nc.vector.tensor_reduce(tmin[:, 0:1], ps_m[:, 2 * P:3 * P], AX.X, ALU.min)
                then(nc.vector.tensor_reduce(tmin[0:rest, 1:2], ps_m[0:rest, 3 * P:4 * P], AX.X, ALU.min))
                for c in range(2):
                    nc.vector.tensor_scalar(ge[:, c], block_lo[:, :], tmax[:, c:c + 1], None, ALU.is_le)
                then(nc.vector.memset(veps[:, :], 0.0))
                for c in range(2):
                    nc.vector.scalar_tensor_tensor(hit[:, c], block_hi[:, :], tmin[:, c:c + 1], ge[:, c],
                                                   ALU.is_ge, ALU.mult)
                then(nc.vector.memset(veps[:, :], 0.0))
                for c in range(2):
                    nc.vector.tensor_scalar(span[:, c, 0:NT], hit[:, c], tile_ids[:, c:c + 1], None, ALU.mult)
                    last = nc.vector.tensor_scalar(span[:, c, NT:2 * NT], hit[:, c], tile_rev[:, c:c + 1],
                                                   None, ALU.mult)
                last.then_inc(edge_step, 1)
                dve.wait_ge(pe_edges, 2)
                nc.vector.tensor_reduce(span_col[:, :], ps_m[0:2 * NT, 0:2 * P], AX.X,
                                        ALU.max).then_inc(edge_step, 1)
                dve.wait_ge(pe_edges, 3)
                then(nc.vector.tensor_scalar(span_row[:, :], ps_m[0:1, 0:2 * NT], 1.0, None, ALU.max))
                then(nc.vector.tensor_scalar(span_fix[:, 0:NT], ps_m[0:1, NT:2 * NT], -1.0, float(ET),
                                             ALU.mult, ALU.add))
                then(nc.vector.tensor_scalar(span_fix[:, NT:2 * NT], span_row[:, 0:NT], -1.0, None, ALU.add))
                then(nc.vector.tensor_tensor(span_fix[:, 0:NT], span_fix[:, 0:NT], span_fix[:, NT:2 * NT],
                                             ALU.min))
                nc.vector.tensor_copy(s.ranges[:, 0:NT], span_fix[:, 0:NT])
                nc.vector.tensor_copy(s.ranges[:, NT:2 * NT], span_row[:, 0:NT])
                for j in range(KD):
                    dve.wait_ge(pe_w1t, j + 1)
                    nc.vector.tensor_copy(w1_t[:, j, :].rearrange("p (b d) -> p b d", b=2),
                                          ps_x[:, j % 2, :, 0:HALF]).then_inc(w1t_kept, 1)
                dve.wait_ge(x_in, 16)
                with dve.Fori(0, NT) as t:
                    for half in range(2):
                        nc.vector.bn_stats(stats[:, bass.ds(t, 1), half, :],
                                           xs[:, bass.ds(t, 1), half * HALF:(half + 1) * HALF]).then_inc(stat_done, 1)
                dve.wait_ge(stat_done, 2 * NT)
                for t in range(NT):
                    last = nc.vector.bn_aggr(mv[:, t, :], stats[:, t, :, :].rearrange("p a b -> p (a b)"))
                then(last)
                nc.vector.tensor_scalar(veps[:, :], mv[:, :, 1], LN_EPS, None, ALU.add).then_inc(stat_done, 1)
                dve.wait_ge(sqrt_done, 1)
                then(nc.vector.reciprocal(rstd[:, 1], rstd[:, 0]))
                then(nc.vector.tensor_tensor(rstd[:, 2], rstd[:, 1], rstd[:, 1], ALU.mult))
                then(nc.vector.tensor_tensor(rstd[:, 2], rstd[:, 2], veps[:, :], ALU.mult))
                then(nc.vector.tensor_scalar(rstd[:, 2], rstd[:, 2], -0.5, 1.5, ALU.mult, ALU.add))
                then(nc.vector.tensor_tensor(rstd[:, 3], rstd[:, 1], rstd[:, 2], ALU.mult))
                with dve.Fori(0, NT // 2) as i:
                    for u in range(2):
                        t = 2 * i + u
                        dve.wait_ge(xt_kept, t + 1)
                        nc.vector.tensor_scalar(xn[:, u, :], xs[:, bass.ds(t, 1), :].rearrange("p o d -> p (o d)"),
                                                mv[:, bass.ds(t, 1), 0:1].rearrange("p o d -> p (o d)"),
                                                rstd[:, 3, bass.ds(t, 1)], ALU.subtract, ALU.mult).then_inc(normed, 1)
                dve.wait_ge(split_hi, KD)
                for k in range(KD):
                    nc.vector.tensor_tensor(s.w1_lo[:, k, :], w1_raw[:, k, :], s.w1_hi[:, k, :].bitcast(F32),
                                            ALU.subtract)
                dve.wait_ge(pe_alc, 1)
                nc.vector.tensor_copy(s.al_col[:, :, :], ps_m[:, 0:NT * 16].rearrange("p (t c) -> p t c", c=16))

            @block.scalar
            def _(act):
                act.dma_start(w1_raw[:, :, :], w1.rearrange("(k p) c -> p k c", p=P)).then_inc(w_in, 16)
                act.sem_inc(xt_kept, 2)
                act.wait_ge(w_in, 16)
                for k in range(KD):
                    nc.scalar.activation(s.w1_hi[:, k, :], w1_raw[:, k, :], ACT.Copy).then_inc(split_hi, 1)
                act.wait_ge(pe_wa, 1)
                nc.scalar.activation(wa[:, :, :], ps_m[:, 0:KD * 16].rearrange("p (k c) -> p k c", c=16),
                                     ACT.Copy).then_inc(wa_kept, 1)
                act.wait_ge(stat_done, 2 * NT + 1)
                nc.scalar.activation(rstd[:, 0], veps[:, :], ACT.Sqrt).then_inc(sqrt_done, 1)
                with act.Fori(0, NT // 2) as i:
                    for u in range(2):
                        t = 2 * i + u
                        act.wait_ge(pe_xt, t + 1)
                        nc.scalar.activation(
                            s.x_t[:, bass.ds(t, 1), :, :].rearrange("p o (b k) n -> p (o b) (k n)", b=2),
                            ps_x[:, u, :, 0:HALF], ACT.Copy).then_inc(xt_kept, 1)
                for c, (at, width) in enumerate(PARTS):
                    act.wait_ge(pe_al, c + 1)
                    nc.scalar.activation(al_rows[:, at:at + width], ps_al[0:16, c, 0:width],
                                         ACT.Copy).then_inc(al_kept, 1)

            @block.tensor
            def _(pe):
                pe.wait_ge(consts, 4)
                pe.wait_ge(edge_step, 1)
                for c, src in enumerate((s.dst_f, dst_hi)):
                    nc.tensor.transpose(ps_m[:, 2 * c * P:(2 * c + 1) * P], src[:, 0:P], s.ident[:, :])
                    last = nc.tensor.transpose(ps_m[0:ET - P, (2 * c + 1) * P:(2 * c + 2) * P], src[:, P:ET],
                                               s.ident[:, :])
                last.then_inc(pe_edges, 1)
                pe.wait_ge(edge_step, 2)
                for c in range(2):
                    last = nc.tensor.transpose(ps_m[0:2 * NT, c * P:(c + 1) * P], span[:, c, :], s.ident[:, :])
                last.then_inc(pe_edges, 1)
                pe.wait_ge(edge_step, 3)
                nc.tensor.transpose(ps_m[0:1, 0:2 * NT], span_col[:, :],
                                    s.ident[0:2 * NT, 0:2 * NT]).then_inc(pe_edges, 1)
                pe.wait_ge(w_in, 16)
                for j in range(KD):
                    if j >= 2:
                        pe.wait_ge(w1t_kept, j - 1)
                    for k in range(KD):
                        last = nc.tensor.transpose(ps_x[:, j % 2, k // 3, (k % 3) * P:(k % 3 + 1) * P],
                                                   w1_raw[:, k, j * P:(j + 1) * P], s.ident[:, :])
                    last.then_inc(pe_w1t, 1)
                pe.wait_ge(w1t_kept, KD)
                pe.wait_ge(diag, 2)
                for k in range(KD):
                    for j in range(KD):
                        last = nc.tensor.matmul(ps_m[:, k * 16:(k + 1) * 16], w1_t[:, j, k * P:(k + 1) * P],
                                                att_diag[:, j, :, :].rearrange("p s h -> p (s h)"),
                                                start=(j == 0), stop=(j == KD - 1))
                last.then_inc(pe_wa, 1)
                with pe.Fori(0, NT // 2) as i:
                    for u in range(2):
                        t = 2 * i + u
                        pe.wait_ge(normed, t + 1)
                        pe.wait_ge(xt_kept, t + 1)
                        for k in range(KD):
                            last = nc.tensor.transpose(ps_x[:, u, k // 3, (k % 3) * P:(k % 3 + 1) * P],
                                                       xn[:, u, k * P:(k + 1) * P], s.ident[:, :])
                        last.then_inc(pe_xt, 1)
                pe.wait_ge(wa_kept, 1)
                pe.wait_ge(xt_kept, NT + 2)
                for c, (at, width) in enumerate(PARTS):
                    for k in range(KD):
                        last = nc.tensor.matmul(ps_al[0:16, c, 0:width], wa[:, k, :],
                                                s.x_t[:, at // P:(at + width) // P, k, :],
                                                start=(k == 0), stop=(k == KD - 1))
                    last.then_inc(pe_al, 1)
                pe.wait_ge(al_kept, 3)
                for t in range(NT):
                    last = nc.tensor.transpose(ps_m[:, t * 16:(t + 1) * 16], al_rows[:, t * P:(t + 1) * P],
                                               s.ident[0:16, 0:16])
                last.then_inc(pe_alc, 1)


def transform_and_count(nc, s):
    with ExitStack() as ctx:
        def sb(name, shape, dt=F32):
            return ctx.enter_context(nc.sbuf_tensor(name, shape, dt))

        def sem(name):
            return ctx.enter_context(nc.semaphore(name))

        al_src = sb("al_src", [P, H1, NP])
        xt_hi = sb("xt_hi", [P, 2, D], F32R)
        xt_lo = sb("xt_lo", [P, 2, D], F32R)
        counts = sb("counts", [P, NP])
        mask = sb("mask", [P, 2, NP], BF16)
        junk = sb("junk", [P, 2, NP], BF16)
        one_src = sb("one_src", [P, 2, NP], BF16)
        one_dst = sb("one_dst", [P, 2, P], BF16)
        dst_rel = sb("dst_rel", [P, ET])
        zeros = sb("zeros", [P, 512], BF16)
        best = sb("best", [P, 2, H1])
        ps_h = ctx.enter_context(nc.psum_tensor("ps_h", [P, 2, 512], F32))
        ps_c = ctx.enter_context(nc.psum_tensor("ps_c", [P, 3, 512], F32))
        ps_t = ctx.enter_context(nc.psum_tensor("ps_t", [P, 3, 512], F32))

        al_in, zeroed, ones_set = sem("al_in"), sem("zeroed"), sem("ones_set")
        xhi_made, xlo_made, h_summed, h_kept = sem("xhi_made"), sem("xlo_made"), sem("h_summed"), sem("h_kept")
        onehot_made, onehot_used, rel_made = sem("onehot_made"), sem("onehot_used"), sem("rel_made")
        counted, counts_kept, turned, turned_kept = sem("counted"), sem("counts_kept"), sem("turned"), sem("turned_kept")
        mask_made, maxed, best_kept = sem("mask_made"), sem("maxed"), sem("best_kept")
        mask_out = [sem("mask_out0"), sem("mask_out1")]

        with nc.Block() as block:
            @block.sync
            def _(sp):
                sp.dma_start(al_src[:, :, :].rearrange("p h n -> p (h n)"),
                             s.al_dram.ap()[0:H1, :].rearrange("(o h) n -> o (h n)", o=1)
                             .broadcast_to([P, H1 * NP])).then_inc(al_in, 16)
                with sp.Fori(0, NT // 2) as i:
                    for u in range(2):
                        t = 2 * i + u
                        sp.wait_ge(mask_made, t + 1)
                        sp.dma_start(s.mask_dram.ap()[bass.ds(t, 1), :, :].rearrange("o p n -> (o p) n"),
                                     mask[:, u, :]).then_inc(mask_out[u], 16)
                for u in range(2):
                    sp.wait_ge(mask_out[u], 16 * (NT // 2))

            @block.gpsimd
            def _(pool):
                nc.gpsimd.memset(s.h_ext[:, :, :, C1:C1 + 1], 1.0).then_inc(ones_set, 1)
                with pool.Fori(0, NT // 2) as i:
                    for u in range(2):
                        t = 2 * i + u
                        pool.wait_ge(xhi_made, t + 1)
                        nc.gpsimd.tensor_tensor(
                            xt_lo[:, u, :], s.x_t[:, bass.ds(t, 1), :, :].rearrange("p o k n -> p (o k n)"),
                            xt_hi[:, u, :].bitcast(F32), ALU.subtract).then_inc(xlo_made, 1)

            @block.scalar
            def _(act):
                act.sem_inc(h_kept, 2)
                with act.Fori(0, NT // 2) as i:
                    for u in range(2):
                        t = 2 * i + u
                        act.wait_ge(h_summed, t)
                        nc.scalar.activation(
                            xt_hi[:, u, :], s.x_t[:, bass.ds(t, 1), :, :].rearrange("p o k n -> p (o k n)"),
                            ACT.Copy).then_inc(xhi_made, 1)
                        act.wait_ge(h_summed, t + 1)
                        for half in range(2):
                            last = nc.scalar.activation(
                                s.h_ext[:, bass.ds(t, 1), 4 * half:4 * half + 4, 0:C1]
                                .rearrange("p o h c -> p (o h) c"),
                                ps_h[:, half, 0:HALF].rearrange("p (h c) -> p h c", c=C1), ACT.Copy)
                        last.then_inc(h_kept, 1)
                        act.wait_ge(turned, t + 1)
                        last = nc.scalar.activation(
                            s.count[:, 0:8, bass.ds(t * P, P)],
                            ps_t[:, 0:2, :].rearrange("p a (b n) -> p (a b) n", n=P), ACT.Copy)
                        last = nc.scalar.activation(
                            s.count[:, 8:NT, bass.ds(t * P, P)],
                            ps_t[:, 2, 0:2 * P].rearrange("p (b n) -> p b n", n=P), ACT.Copy)
                        last.then_inc(turned_kept, 1)

            @block.vector
            def _(dve):
                nc.vector.memset(zeros[:, :], 0.0).then_inc(zeroed, 1)
                made = dve.alloc_register("made_dve")
                dve.reg_mov(made, 0)
                freed = dve.alloc_register("freed")
                dve.reg_mov(freed, 0)
                with dve.Fori(0, NT // 2) as i:
                    for u in range(2):
                        t = 2 * i + u
                        nc.vector.tensor_scalar(dst_rel[:, :], s.dst_f[:, :],
                                                s.block_col[:, bass.ds(t, 1)],
                                                None, ALU.subtract).then_inc(rel_made, 1)
                        dve.wait_ge(rel_made, t + 1)
                        first = dve.value_load(s.ranges[0:1, bass.ds(t, 1)], min_val=0, max_val=ET - 1)
                        end = dve.value_load(s.ranges[0:1, bass.ds(t + NT, 1)], min_val=1, max_val=ET)
                        with dve.Fori(first, end) as e:
                            m = dve.snap(made)
                            dve.wait_ge(onehot_used, m + 1)
                            nc.vector.tensor_scalar(one_src[:, m % 2, :], s.column[:, :],
                                                    s.src_f[:, bass.ds(e, 1)], None, ALU.is_equal)
                            nc.vector.tensor_scalar(one_dst[:, m % 2, :], s.column[:, 0:P],
                                                    dst_rel[:, bass.ds(e, 1)], None,
                                                    ALU.is_equal).then_inc(onehot_made, 1)
                            dve.reg_add(made, made, 1)
                        dve.wait_ge(counted, t + 1)
                        dve.wait_ge(turned, t)
                        nc.vector.tensor_copy(counts[:, 0:1024], ps_c[:, 0:2, :].rearrange("p a n -> p (a n)"))
                        nc.vector.tensor_copy(counts[:, 1024:NP], ps_c[:, 2, 0:256]).then_inc(counts_kept, 1)
                        dve.wait_ge(counts_kept, t + 1)
                        dve.wait_ge(mask_out[u], 16 * i)
                        nc.vector.tensor_scalar(mask[:, u, :], counts[:, :], 0.0, NOT_A_NEIGHBOUR,
                                                ALU.is_equal, ALU.mult).then_inc(mask_made, 1)
                        dve.wait_ge(al_in, 16)
                        dve.wait_ge(mask_made, t + 1)
                        for h in range(H1):
                            if h >= 2:
                                dve.reg_add(freed, freed, 1)
                                now = dve.snap(freed)
                                dve.wait_ge(al_in, 16)
                                dve.wait_ge(maxed, now)
                            nc.vector.tensor_tensor_reduce(
                                junk[:, h % 2, :], mask[:, u, :], al_src[:, h, :], 1.0,
                                2.0 * NOT_A_NEIGHBOUR, ALU.add, ALU.max, best[:, u, h:h + 1]).then_inc(maxed, 1)
                        dve.reg_add(freed, freed, 2)
                        dve.wait_ge(maxed, (t + 1) * H1)
                        nc.vector.tensor_copy(s.al_max[:, bass.ds(t, 1), :].rearrange("p o h -> p (o h)"),
                                              best[:, u, :]).then_inc(best_kept, 1)
                        dve.wait_ge(best_kept, t + 1)

            @block.tensor
            def _(pe):
                pe.sem_inc(onehot_used, 2)
                pe.wait_ge(zeroed, 1)
                made = pe.alloc_register("made_pe")
                pe.reg_mov(made, 0)
                with pe.Fori(0, NT // 2) as i:
                    for u in range(2):
                        t = 2 * i + u
                        first = pe.value_load(s.ranges[0:1, bass.ds(t, 1)], min_val=0, max_val=ET - 1)
                        end = pe.value_load(s.ranges[0:1, bass.ds(t + NT, 1)], min_val=1, max_val=ET)
                        pe.wait_ge(counts_kept, t)
                        for c, (at, width) in enumerate(PARTS):
                            nc.tensor.matmul(ps_c[:, c, 0:width], zeros[:, 0:P], zeros[:, 0:width],
                                             start=True, stop=False)
                        with pe.Fori(first, end) as e:
                            m = pe.snap(made)
                            pe.wait_ge(onehot_made, m + 1)
                            for c, (at, width) in enumerate(PARTS):
                                last = nc.tensor.matmul(ps_c[:, c, 0:width], one_dst[:, m % 2, :],
                                                        one_src[:, m % 2, at:at + width],
                                                        start=False, stop=False)
                            last.then_inc(onehot_used, 1)
                            pe.reg_add(made, made, 1)
                        for c, (at, width) in enumerate(PARTS):
                            last = nc.tensor.matmul(ps_c[:, c, 0:width], zeros[:, 0:P], zeros[:, 0:width],
                                                    start=False, stop=True)
                        last.then_inc(counted, 1)
                        pe.wait_ge(xlo_made, t + 1)
                        pe.wait_ge(h_kept, t + 2)
                        for half in range(2):
                            at = half * HALF
                            for k in range(KD):
                                hi, lo = (w[:, u, k * P:(k + 1) * P] for w in (xt_hi, xt_lo))
                                for n, (a, b) in enumerate(((hi, s.w1_hi), (hi, s.w1_lo), (lo, s.w1_hi))):
                                    last = nc.tensor.matmul(ps_h[:, half, 0:HALF], a, b[:, k, at:at + HALF],
                                                            start=(k == 0 and n == 0),
                                                            stop=(k == KD - 1 and n == 2))
                        last.then_inc(h_summed, 1)
                        pe.wait_ge(counts_kept, t + 1)
                        pe.wait_ge(turned_kept, t)
                        for b in range(NT):
                            last = nc.tensor.transpose(ps_t[:, b // 4, (b % 4) * P:(b % 4 + 1) * P],
                                                       counts[:, b * P:(b + 1) * P], s.ident[:, :])
                        last.then_inc(turned, 1)

def attend_by_head(nc, s, bias1):
    with ExitStack() as ctx:
        def sb(name, shape, dt=F32):
            return ctx.enter_context(nc.sbuf_tensor(name, shape, dt))

        def sem(name):
            return ctx.enter_context(nc.semaphore(name))

        rel = sb("rel", [P, NT, 2, H1])
        top = sb("top", [P, 2, NT, H1])
        src_small = sb("src_small", [P, NT, H1])
        rel_rows = sb("rel_rows", [2 * H1, NP])
        bias_col = sb("bias_col", [C1, H1])
        bias_now = sb("bias_now", [C1, 1])
        h_head = sb("h_head", [P, 2, NT, C1 + 1])
        steep = sb("steep", [P, 2, NP])
        flat = sb("flat", [P, 2, NP])
        ex = sb("ex", [P, 2, NP])
        ey = sb("ey", [P, 2, NP])
        prob = sb("prob", [P, 2, NP])
        out_t = sb("out_t", [C1 + 1, 2, NP])
        scale_t = sb("scale_t", [C1, 2, NP])
        neg_t = sb("neg_t", [C1, NP])
        z_rows = sb("z_rows", [NT, 2, N // NT])

        ps_o = [ctx.enter_context(nc.psum_tensor(f"ps_o{u}", [P, 3, 512], F32)) for u in range(2)]
        ps_r = ctx.enter_context(nc.psum_tensor("ps_r", [P, 512], F32))

        step, rel_made, rel_turned, rel_kept, rel_out = (sem("c_step"), sem("rel_made_2"), sem("rel_turned"),
                                                         sem("rel_kept"), sem("rel_out"))
        rows_in = [sem("rows_in0"), sem("rows_in1")]
        head_set, exped, joined, made, mixed = (sem("head_set"), sem("exped"), sem("joined"), sem("made"),
                                                sem("mixed"))
        out_kept, z_out, z_in, z_done, zi_out = (sem("out_kept"), sem("z_out"), sem("z_in"), sem("z_done"),
                                                 sem("zi_out"))
        scale_in = [sem("scale_in0"), sem("scale_in1")]
        neg_made, neg_exped, elued = sem("neg_made"), sem("neg_exped"), sem("elued")
        pool_step, bias_in, head_mixed = sem("pool_step"), sem("bias_in"), sem("head_mixed")
        count_out = sem("count_out")
        WID = [512, 512, N - 1024]

        with nc.Block() as block:
            @block.sync
            def _(sp):
                sp.dma_start(bias_col[:, :], bias1).then_inc(bias_in, 16)
                sp.dma_start(s.count_dram.ap(), s.count[:, :, :]).then_inc(count_out, 16)
                sp.wait_ge(rel_kept, 3)
                sp.dma_start(s.rel_dram.ap(), rel_rows[:, :]).then_inc(rel_out, 16)
                sp.wait_ge(rel_out, 16)

                def load_rows(h, u):
                    sp.dma_start(steep[:, u, :], s.rel_dram.ap()[bass.ds(h, 1), :].broadcast_to([P, NP])) \
                      .then_inc(rows_in[u], 16)
                    sp.dma_start(flat[:, u, :], s.rel_dram.ap()[bass.ds(h + H1, 1), :].broadcast_to([P, NP])) \
                      .then_inc(rows_in[u], 16)

                def reciprocal_sums(h, u):
                    sp.wait_ge(out_kept, h + 1)
                    sp.dma_start(s.z_dram.ap()[bass.ds(h, 1), :], out_t[C1:C1 + 1, u, 0:N]).then_inc(z_out, 16)
                    sp.wait_ge(z_out, 16 * h + 16)
                    sp.dma_start(z_rows[:, u, :], s.z_dram.ap()[bass.ds(h, 1), :]
                                 .rearrange("o (a b) -> (o a) b", a=NT)).then_inc(z_in, 16)
                    sp.wait_ge(z_done, 2 * h + 2)
                    sp.dma_start(s.zi_dram.ap()[bass.ds(h, 1), :].rearrange("o (a b) -> (o a) b", a=NT),
                                 z_rows[:, u, :]).then_inc(zi_out, 16)
                    sp.wait_ge(zi_out, 16 * h + 16)
                    sp.dma_start(scale_t[:, u, 0:N], s.zi_dram.ap()[bass.ds(h, 1), :].broadcast_to([C1, N])) \
                      .then_inc(scale_in[u], 16)

                load_rows(0, 0)
                load_rows(1, 1)
                reciprocal_sums(0, 0)
                with sp.Fori(0, H1 // 2 - 1) as i:
                    for u in range(2):
                        h = 2 * i + u
                        load_rows(h + 2, u)
                        sp.wait_ge(elued, h)
                        reciprocal_sums(h + 1, 1 - u)
                reciprocal_sums(H1 - 1, 1)
                for u in range(2):
                    sp.wait_ge(scale_in[u], 16 * (H1 // 2))
                sp.wait_ge(count_out, 16)

            @block.gpsimd
            def _(pool):
                def stage_head(h, u):
                    nc.gpsimd.tensor_copy(h_head[:, u], s.h_ext[:, :, bass.ds(h, 1), :]
                                          .rearrange("p t o c -> p (t o) c")).then_inc(head_set, 1)

                steps = pool.alloc_register("pool_steps")
                pool.reg_mov(steps, 0)

                def then(ins):
                    ins.then_inc(pool_step, 1)
                    pool.reg_add(steps, steps, 1)
                    done = pool.snap(steps)
                    pool.wait_ge(bias_in, 16)
                    pool.wait_ge(pool_step, done)

                def finish(h, i, u):
                    pool.wait_ge(scale_in[u], 16 * i + 16)
                    then(nc.gpsimd.tensor_copy(bias_now[:, :], bias_col[:, bass.ds(h, 1)]))
                    then(nc.gpsimd.tensor_tensor(out_t[0:C1, u, 0:N], out_t[0:C1, u, 0:N], scale_t[:, u, 0:N],
                                                 ALU.mult))
                    then(nc.gpsimd.tensor_scalar(out_t[0:C1, u, 0:N], out_t[0:C1, u, 0:N], bias_now[:, 0:1],
                                                 None, ALU.add))
                    nc.gpsimd.tensor_scalar(neg_t[:, 0:N], out_t[0:C1, u, 0:N], 0.0, None,
                                            ALU.min).then_inc(neg_made, 1)
                    then(nc.gpsimd.tensor_scalar(scale_t[:, u, 0:N], out_t[0:C1, u, 0:N], 0.0, -1.0,
                                                 ALU.max, ALU.add))
                    pool.wait_ge(neg_exped, h + 1)
                    nc.gpsimd.tensor_tensor(s.g_t[:, bass.ds(h, 1), 0:N].rearrange("p o n -> p (o n)"),
                                            scale_t[:, u, 0:N], neg_t[:, 0:N], ALU.add).then_inc(elued, 1)
                    pool.wait_ge(elued, h + 1)

                nc.gpsimd.memset(s.g_t[:, :, N:NP], 0.0)
                pool.wait_ge(bias_in, 16)
                stage_head(0, 0)
                stage_head(1, 1)
                with pool.Fori(0, H1 // 2 - 1) as i:
                    for u in range(2):
                        h = 2 * i + u
                        pool.wait_ge(mixed, (h + 1) * NT + 2)
                        stage_head(h + 2, u)
                        finish(h, i, u)
                for u in range(2):
                    finish(H1 - 2 + u, H1 // 2 - 1, u)

            @block.scalar
            def _(act):
                act.wait_ge(rel_turned, 1)
                for c, (at, width) in enumerate(PARTS):
                    act.wait_ge(rel_turned, c + 1)
                    nc.scalar.activation(rel_rows[:, at:at + width], ps_r[0:16, 0:width],
                                         ACT.Copy).then_inc(rel_kept, 1)
                act.wait_ge(step, 1)

                def keep_out(h, u):
                    act.wait_ge(mixed, (h + 1) * NT + 2)
                    if not (isinstance(h, int) and h == 0):
                        act.wait_ge(elued, h - 1)
                    nc.scalar.activation(out_t[:, u, 0:1024].rearrange("p (a n) -> p a n", a=2),
                                         ps_o[u][0:C1 + 1, 0:2, :], ACT.Copy)
                    nc.scalar.activation(out_t[:, u, 1024:N], ps_o[u][0:C1 + 1, 2, 0:WID[2]],
                                         ACT.Copy).then_inc(out_kept, 1)

                def exp_negative(h):
                    act.wait_ge(neg_made, h + 1)
                    nc.scalar.activation(neg_t[:, 0:N], neg_t[:, 0:N], ACT.Exp).then_inc(neg_exped, 1)

                def exps(h, i, u, first):
                    act.wait_ge(rows_in[u], 32 * i + 32)
                    for t in range(NT):
                        act.wait_ge(joined, h * NT + t + 1)
                        nc.scalar.activation(ex[:, t % 2, 0:N], steep[:, u, 0:N], ACT.Exp,
                                             bias=s.al_col[:, t, bass.ds(h, 1)])
                        nc.scalar.activation(ey[:, t % 2, 0:N], flat[:, u, 0:N], ACT.Exp,
                                             bias=src_small[:, t, bass.ds(h, 1)]).then_inc(exped, 1)
                        if t == 2 and not first:
                            keep_out(h - 1, 1 - u)

                def head(h, i, u, first=False, second=False):
                    exps(h, i, u, first)
                    if not first and not second:
                        exp_negative(h - 2)

                head(0, 0, 0, first=True)
                head(1, 0, 1, second=True)
                with act.Fori(1, H1 // 2) as i:
                    for u in range(2):
                        head(2 * i + u, i, u)
                keep_out(H1 - 1, 1)
                exp_negative(H1 - 2)
                exp_negative(H1 - 1)

            @block.vector
            def _(dve):
                n = [0]

                def then(ins):
                    n[0] += 1
                    ins.then_inc(rel_made, 1)
                    dve.wait_ge(rel_made, n[0])

                src, dst = s.al_col[:, :, 0:H1], s.al_col[:, :, H1:2 * H1]
                then(nc.vector.tensor_tensor(top[:, 0], s.al_max[:, :, :], dst, ALU.add))
                then(nc.vector.scalar_tensor_tensor(top[:, 1], top[:, 0], SLOPE, top[:, 0], ALU.mult, ALU.max))
                then(nc.vector.scalar_tensor_tensor(top[:, 1], s.al_max[:, :, :], 0.5 * NOT_A_NEIGHBOUR, top[:, 1],
                                                    ALU.is_gt, ALU.mult))
                nc.vector.tensor_tensor(rel[:, :, 0, :], dst, top[:, 1], ALU.subtract)
                nc.vector.scalar_tensor_tensor(rel[:, :, 1, :], dst, SLOPE, top[:, 1], ALU.mult, ALU.subtract)
                nc.vector.tensor_scalar(src_small[:, :, :], src, SLOPE, None, ALU.mult).then_inc(step, 1)
                dve.wait_ge(step, 1)
                dve.sem_inc(joined, 2)

                def invert_sums(h, u):
                    dve.wait_ge(z_in, 16 * h + 16)
                    nc.vector.tensor_scalar(z_rows[:, u, :], z_rows[:, u, :], 1e-16, None,
                                            ALU.add).then_inc(z_done, 1)
                    dve.wait_ge(z_done, 2 * h + 1)
                    nc.vector.reciprocal(z_rows[:, u, :], z_rows[:, u, :]).then_inc(z_done, 1)

                def head(h, u, first=False):
                    for t in range(NT):
                        dve.wait_ge(exped, h * NT + t + 1)
                        nc.vector.scalar_tensor_tensor(ex[:, t % 2, 0:N], ey[:, t % 2, 0:N], 1.0,
                                                       ex[:, t % 2, 0:N], ALU.min, ALU.max).then_inc(step, 1)
                        dve.wait_ge(step, h * NT + t + 2)
                        dve.wait_ge(mixed, h * NT + t + 1)
                        nc.vector.scalar_tensor_tensor(prob[:, t % 2, 0:N], ex[:, t % 2, 0:N], 1.0,
                                                       s.count[:, t, 0:N], ALU.min,
                                                       ALU.mult).then_inc(joined, 1)
                        if t == 6 and not first:
                            invert_sums(h - 1, 1 - u)

                head(0, 0, first=True)
                head(1, 1)
                with dve.Fori(1, H1 // 2) as i:
                    for u in range(2):
                        head(2 * i + u, u)
                invert_sums(H1 - 1, 1)

            @block.tensor
            def _(pe):
                pe.sem_inc(mixed, 2)
                pe.wait_ge(step, 1)
                for c, (at, width) in enumerate(PARTS):
                    if c:
                        pe.wait_ge(rel_kept, c)
                    for t in range(at // P, (at + width) // P):
                        last = nc.tensor.transpose(ps_r[0:16, t * P - at:(t + 1) * P - at],
                                                   rel[:, t, :, :].rearrange("p a h -> p (a h)"), s.ident[:, :])
                    last.then_inc(rel_turned, 1)

                def head(h, u, early=False):
                    pe.wait_ge(head_set, h + 1)
                    if not early:
                        pe.wait_ge(out_kept, h - 1)
                    for t in range(NT):
                        pe.wait_ge(joined, h * NT + t + 3)
                        for c in range(3):
                            last = nc.tensor.matmul(ps_o[u][0:C1 + 1, c, 0:WID[c]], h_head[:, u, t, :],
                                                    prob[:, t % 2, 512 * c:512 * c + WID[c]],
                                                    start=(t == 0), stop=(t == NT - 1))
                        last.then_inc(mixed, 1)

                head(0, 0, early=True)
                head(1, 1, early=True)
                with pe.Fori(1, H1 // 2) as i:
                    for u in range(2):
                        head(2 * i + u, u)

def transform_again(nc, s, w2, att2):
    with ExitStack() as ctx:
        def sb(name, shape, dt=F32):
            return ctx.enter_context(nc.sbuf_tensor(name, shape, dt))

        def sem(name):
            return ctx.enter_context(nc.semaphore(name))

        w2_raw = sb("w2_raw", [C1, 2, D])
        w2_hi = sb("w2_hi", [C1, H1, D], F32R)
        w2_lo = sb("w2_lo", [C1, H1, D], F32R)
        g_hi = sb("g_hi", [C1, 2, H1, P], F32R)
        g_lo = sb("g_lo", [C1, 2, H1, P], F32R)
        att = sb("att", [P, 2, D])
        junk = sb("junk2", [P, 2, 2, HALF], BF16)
        al_now = sb("al_now", [P, 2, 2])
        ps = [ctx.enter_context(nc.psum_tensor(f"ps_h2{u}", [P, 2, 512], F32)) for u in range(2)]

        w_in = [sem("w2_in0"), sem("w2_in1")]
        a_in, w_hi, w_lo, ones_set = sem("a2_in"), sem("w2_hi_made"), sem("w2_lo_made"), sem("ones2_set")
        ghi_made, glo_made, summed, h_hi, h_lo, al_made, al_kept = (
            sem("ghi_made"), sem("glo_made"), sem("h2_summed"), sem("h2_hi_made"), sem("h2_lo_made"),
            sem("al2_made"), sem("al2_kept"))

        with nc.Block() as block:
            @block.sync
            def _(sp):
                for k in range(H1):
                    if k >= 2:
                        sp.wait_ge(w_lo, k - 1)
                    sp.dma_start(w2_raw[:, k % 2, :], w2[k * C1:(k + 1) * C1, :]).then_inc(w_in[k % 2], 16)
                sp.dma_start(att[:, :, :].rearrange("p a d -> p (a d)"), att2.broadcast_to([P, 2 * D])) \
                  .then_inc(a_in, 16)

            @block.gpsimd
            def _(pool):
                nc.gpsimd.memset(s.h2_hi[:, :, D:D + 4].bitcast(F32), 0.0).then_inc(ones_set, 1)
                nc.gpsimd.memset(s.h2_lo[:, :, D:D + 4].bitcast(F32), 0.0)
                pool.wait_ge(ones_set, 1)
                nc.gpsimd.memset(s.h2_hi[:, :, D:D + 1].bitcast(F32), 1.0).then_inc(ones_set, 1)
                with pool.Fori(0, NT // 2) as i:
                    for u in range(2):
                        t = 2 * i + u
                        pool.wait_ge(ghi_made, t + 1)
                        nc.gpsimd.tensor_tensor(g_lo[:, u], s.g_t[:, :, bass.ds(t * P, P)],
                                                g_hi[:, u].bitcast(F32), ALU.subtract).then_inc(glo_made, 1)
                pool.wait_ge(ones_set, 2)

            @block.scalar
            def _(act):
                for k in range(H1):
                    act.wait_ge(w_in[k % 2], 16 * (k // 2 + 1))
                    nc.scalar.activation(w2_hi[:, k, :], w2_raw[:, k % 2, :], ACT.Copy).then_inc(w_hi, 1)
                act.sem_inc(h_hi, 2)

                def split_g(t, u):
                    nc.scalar.activation(g_hi[:, u], s.g_t[:, :, bass.ds(t * P, P)], ACT.Copy).then_inc(ghi_made, 1)

                split_g(0, 0)
                split_g(1, 1)
                with act.Fori(0, NT // 2) as i:
                    for u in range(2):
                        t = 2 * i + u
                        act.wait_ge(summed, t + 1)
                        nc.scalar.activation(
                            s.h2_hi[:, bass.ds(t, 1), 0:D].rearrange("p o (b d) -> p (o b) d", b=2),
                            ps[u][:, :, 0:HALF], ACT.Copy).then_inc(h_hi, 1)
                        nc.scalar.activation(g_hi[:, u], s.g_t[:, :, bass.ds((t + 2) % NT * P, P)],
                                             ACT.Copy).then_inc(ghi_made, 1)

            @block.vector
            def _(dve):
                for k in range(H1):
                    dve.wait_ge(w_hi, k + 1)
                    nc.vector.tensor_tensor(w2_lo[:, k, :], w2_raw[:, k % 2, :], w2_hi[:, k, :].bitcast(F32),
                                            ALU.subtract).then_inc(w_lo, 1)
                dve.wait_ge(a_in, 16)
                with dve.Fori(0, NT // 2) as i:
                    for u in range(2):
                        t = 2 * i + u
                        dve.wait_ge(h_hi, t + 3)
                        out = s.h2_lo[:, bass.ds(t, 1), 0:D].rearrange("p o (b d) -> p (o b) d", b=2)
                        hi = s.h2_hi[:, bass.ds(t, 1), 0:D].bitcast(F32).rearrange("p o (b d) -> p (o b) d", b=2)
                        nc.vector.tensor_tensor(out, ps[u][:, :, 0:HALF], hi, ALU.subtract)
                        for a in range(2):
                            last = nc.vector.scalar_tensor_tensor(
                                junk[:, a], ps[u][:, :, 0:HALF], 1.0,
                                att[:, a, :].rearrange("p (b d) -> p b d", b=2),
                                ALU.mult, ALU.mult, accum_out=al_now[:, u, a:a + 1])
                        last.then_inc(al_made, 1)
                        dve.wait_ge(al_made, t + 1)
                        nc.vector.tensor_copy(s.al2_col[:, bass.ds(t, 1), :].rearrange("p o a -> p (o a)"),
                                              al_now[:, u, :]).then_inc(al_kept, 1)
                        dve.wait_ge(al_kept, t + 1)

            @block.tensor
            def _(pe):
                pe.wait_ge(w_lo, H1)
                with pe.Fori(0, NT // 2) as i:
                    for u in range(2):
                        t = 2 * i + u
                        pe.wait_ge(glo_made, t + 1)
                        pe.wait_ge(al_made, 2 * i)
                        for half in range(2):
                            at = half * HALF
                            for k in range(H1):
                                hi, lo = g_hi[:, u, k, :], g_lo[:, u, k, :]
                                for n, (a, b) in enumerate(((hi, w2_hi), (hi, w2_lo), (lo, w2_hi))):
                                    last = nc.tensor.matmul(ps[u][:, half, 0:HALF], a, b[:, k, at:at + HALF],
                                                            start=(k == 0 and n == 0),
                                                            stop=(k == H1 - 1 and n == 2))
                        last.then_inc(summed, 1)


def attention_again(nc, s):
    with ExitStack() as ctx:
        def sb(name, shape, dt=F32):
            return ctx.enter_context(nc.sbuf_tensor(name, shape, dt))

        def sem(name):
            return ctx.enter_context(nc.semaphore(name))

        MS = NT // 2
        count = sb("count2", [P, NT, NP], U16)
        mask = sb("mask2", [P, MS, NP], BF16)
        al_src = sb("al2_src", [P, NP])
        al_rows = sb("al2_rows", [2, NP])
        junk = sb("junk3", [P, 2, NP], BF16)
        best = sb("best2", [P, NT])
        top = sb("top2", [P, 2, NT])
        rel = sb("rel2", [P, NT, 2])
        rel_rows = sb("rel2_rows", [2, NP])
        small = sb("small2", [P, NT])
        rows = sb("rows2", [P, 2, NP])
        ex = sb("ex2", [P, 2, NP])
        ey = sb("ey2", [P, 2, NP])
        ps = ctx.enter_context(nc.psum_tensor("ps_rows", [P, 3, 512], F32))
        count_in, al_in, al_turned, al_kept, al_out = (sem("count_in"), sem("al2s_in"), sem("al2_turned"),
                                                       sem("al2_rows_kept"), sem("al2_out"))
        mask_in = [sem("mask2_in0"), sem("mask2_in1")]
        maxed, step, rel_turned, rel_kept, rel_out, rows_in = (sem("max2"), sem("e_step"), sem("rel2_turned"),
                                                               sem("rel2_kept"), sem("rel2_out"), sem("rows2_in"))
        exped, joined, made = sem("exped2"), sem("joined2"), sem("made2")

        with nc.Block() as block:
            @block.sync
            def _(sp):
                sp.dma_start(mask[:, :, :], s.mask_dram.ap()[0:MS].rearrange("t p n -> p t n")).then_inc(mask_in[0], 16)
                sp.wait_ge(al_kept, 3)
                sp.dma_start(s.al2_dram.ap(), al_rows[:, :]).then_inc(al_out, 16)
                sp.wait_ge(al_out, 16)
                sp.dma_start(al_src[:, :], s.al2_dram.ap()[0:1, :].broadcast_to([P, NP])).then_inc(al_in, 16)
                sp.dma_start(count[:, :, :], s.count_dram.ap()).then_inc(count_in, 16)
                sp.wait_ge(maxed, MS)
                sp.dma_start(mask[:, :, :], s.mask_dram.ap()[MS:NT].rearrange("t p n -> p t n")).then_inc(mask_in[1], 16)
                sp.wait_ge(rel_kept, 3)
                sp.dma_start(s.rel2_dram.ap(), rel_rows[:, :]).then_inc(rel_out, 16)
                sp.wait_ge(rel_out, 16)
                for a in range(2):
                    sp.dma_start(rows[:, a, :], s.rel2_dram.ap()[a:a + 1, :].broadcast_to([P, NP])).then_inc(rows_in, 16)

            @block.tensor
            def _(pe):
                for src, waits, turned, kept in ((s.al2_col, None, al_turned, al_kept), (rel, 5, rel_turned, rel_kept)):
                    if waits:
                        pe.wait_ge(step, waits)
                    for c, (at, width) in enumerate(PARTS):
                        for t in range(at // P, (at + width) // P):
                            last = nc.tensor.transpose(ps[0:2, c, t * P - at:(t + 1) * P - at], src[:, t, :],
                                                       s.ident[:, :])
                        last.then_inc(turned, 1)
                    pe.wait_ge(kept, 3)

            @block.scalar
            def _(act):
                for rows_to, turned, kept in ((al_rows, al_turned, al_kept), (rel_rows, rel_turned, rel_kept)):
                    for c, (at, width) in enumerate(PARTS):
                        act.wait_ge(turned, c + 1)
                        nc.scalar.activation(rows_to[:, at:at + width], ps[0:2, c, 0:width],
                                             ACT.Copy).then_inc(kept, 1)
                act.wait_ge(rows_in, 32)
                act.wait_ge(step, 5)
                for t in range(NT):
                    if t >= 2:
                        act.wait_ge(made, t - 1)
                    nc.scalar.activation(ex[:, t % 2, :], rows[:, 0, :], ACT.Exp, bias=s.al2_col[:, t, 0:1])
                    nc.scalar.activation(ey[:, t % 2, :], rows[:, 1, :], ACT.Exp,
                                         bias=small[:, t:t + 1]).then_inc(exped, 1)

            @block.vector
            def _(dve):
                n = [0]

                def then(ins):
                    n[0] += 1
                    ins.then_inc(step, 1)
                    dve.wait_ge(step, n[0])

                dve.wait_ge(al_in, 16)
                for t in range(NT):
                    dve.wait_ge(mask_in[t // MS], 16)
                    if t >= 2:
                        dve.wait_ge(maxed, t - 1)
                    nc.vector.tensor_tensor_reduce(junk[:, t % 2, :], mask[:, t % MS, :], al_src[:, :], 1.0,
                                                   2.0 * NOT_A_NEIGHBOUR, ALU.add, ALU.max,
                                                   best[:, t:t + 1]).then_inc(maxed, 1)
                dve.wait_ge(maxed, NT)
                src, dst = s.al2_col[:, :, 0], s.al2_col[:, :, 1]
                then(nc.vector.tensor_tensor(top[:, 0], best[:, :], dst, ALU.add))
                then(nc.vector.scalar_tensor_tensor(top[:, 1], top[:, 0], SLOPE, top[:, 0], ALU.mult, ALU.max))
                then(nc.vector.scalar_tensor_tensor(top[:, 1], best[:, :], 0.5 * NOT_A_NEIGHBOUR, top[:, 1],
                                                    ALU.is_gt, ALU.mult))
                nc.vector.tensor_scalar(small[:, :], src, SLOPE, None, ALU.mult)
                then(nc.vector.tensor_tensor(rel[:, :, 0], dst, top[:, 1], ALU.subtract))
                then(nc.vector.scalar_tensor_tensor(rel[:, :, 1], dst, SLOPE, top[:, 1], ALU.mult, ALU.subtract))
                dve.wait_ge(count_in, 16)
                for t in range(NT):
                    dve.wait_ge(exped, t + 1)
                    nc.vector.scalar_tensor_tensor(ex[:, t % 2, :], ey[:, t % 2, :], 1.0, ex[:, t % 2, :],
                                                   ALU.min, ALU.max).then_inc(joined, 1)
                    dve.wait_ge(joined, t + 1)
                    nc.vector.scalar_tensor_tensor(s.prob2[:, t, :], ex[:, t % 2, :], 1.0, count[:, t, :],
                                                   ALU.min, ALU.mult).then_inc(made, 1)


def mix_and_route(nc, s, x, bias2, wg, we, bg, be):
    with ExitStack() as ctx:
        def sb(name, shape, dt=F32):
            return ctx.enter_context(nc.sbuf_tensor(name, shape, dt))

        def sem(name):
            return ctx.enter_context(nc.semaphore(name))

        p_hi = sb("p_hi", [P, 2, NT, P], F32R)
        p_lo = sb("p_lo", [P, 2, NT, P], F32R)
        x_in_t = sb("x_in_t", [P, 2, D])
        x2 = sb("x2", [P, 2, D])
        xf = sb("xf", [P, 2, D])
        xf_t = sb("xf_t", [P, 2, KD, P])
        b_row = sb("b_row", [P, D])
        wr = sb("wr", [P, KD, RC])
        br = sb("br", [P, RC])
        zi = sb("zi", [P, 2, 2])
        stats = sb("stats2", [P, 2, 2, 6])
        mv = sb("mv2", [P, 2, 2])
        veps = sb("veps2", [P, 2, 1])
        half_neg = sb("half_neg", [P, 1])
        rstd = sb("rstd2", [P, 2, 1])
        ps_o = [ctx.enter_context(nc.psum_tensor(f"ps_mix{u}", [P, 2, 512], F32)) for u in range(2)]
        ps_x = ctx.enter_context(nc.psum_tensor("ps_xf", [P, 2, 512], F32))
        ps_l = ctx.enter_context(nc.psum_tensor("ps_logit", [P, 512], F32))
        W2H = (D + 4) // 2

        wr_in, br_in = sem("wr_in"), sem("br_in")
        x_in = [sem("xt_in0"), sem("xt_in1")]
        phi_made, plo_made, mixed, x_biased, z_step = (sem("phi_made"), sem("plo_made"), sem("mixed2"),
                                                       sem("x_biased"), sem("z_step"))
        x2_made, stat, var_made, rooted, xf_made = (sem("x2_made"), sem("stat2"), sem("var_made"),
                                                    sem("rooted"), sem("xf_made"))
        turned, xft_kept, logged, logits_kept = sem("xf_turned"), sem("xft_kept"), sem("logged"), sem("logits_kept")
        x2_out = [sem("x2_out0"), sem("x2_out1")]
        xf_out = [sem("xf_out0"), sem("xf_out1")]
        consts = sem("f_consts")

        with nc.Block() as block:
            @block.sync
            def _(sp):
                sp.dma_start(b_row[:, :], bias2.broadcast_to([P, D])).then_inc(br_in, 16)
                sp.dma_start(br[:, 0:G], bg.broadcast_to([P, G])).then_inc(br_in, 16)
                sp.dma_start(br[:, G:RC], be.broadcast_to([P, E])).then_inc(br_in, 16)
                sp.dma_start(wr[:, :, 0:G], wg.rearrange("(k p) g -> p k g", p=P)).then_inc(wr_in, 16)
                for g in range(G):
                    sp.dma_start(wr[:, :, G + g * EG:G + (g + 1) * EG],
                                 we[g].rearrange("(k p) e -> p k e", p=P)).then_inc(wr_in, 16)
                for u in range(2):
                    sp.dma_start(x_in_t[:, u, :], x[u * P:(u + 1) * P, :]).then_inc(x_in[u], 16)

                def out(t, i, u):
                    sp.wait_ge(x2_made, t + 1)
                    sp.dma_start(s.x2_dram.ap()[bass.ds(t * P, P), :], x2[:, u, :]).then_inc(x2_out[u], 16)
                    sp.wait_ge(xf_made, t + 1)
                    sp.dma_start(s.table.ap()[bass.ds(t * P + 1, P), 0:D], xf[:, u, :]).then_inc(xf_out[u], 16)

                with sp.Fori(0, NT // 2 - 1) as i:
                    for u in range(2):
                        t = 2 * i + u
                        sp.wait_ge(x2_made, t + 1)
                        sp.dma_start(x_in_t[:, u, :], x[bass.ds((t + 2) * P, P), :]).then_inc(x_in[u], 16)
                        out(t, i, u)
                for u in range(2):
                    out(NT - 2 + u, NT // 2 - 1, u)
                for u in range(2):
                    sp.wait_ge(x2_out[u], 16 * (NT // 2))
                    sp.wait_ge(xf_out[u], 16 * (NT // 2))

            @block.gpsimd
            def _(pool):
                nc.gpsimd.memset(half_neg[:, :], -0.5).then_inc(consts, 1)
                pool.wait_ge(consts, 1)
                pool.wait_ge(br_in, 48)
                with pool.Fori(0, NT // 2) as i:
                    for u in range(2):
                        t = 2 * i + u
                        pool.wait_ge(x_in[u], 16 * i + 16)
                        nc.gpsimd.tensor_tensor(x_in_t[:, u, :], x_in_t[:, u, :], b_row[:, :],
                                                ALU.add).then_inc(x_biased, 1)
                        pool.wait_ge(var_made, t + 1)
                        nc.gpsimd.tensor_tensor(rstd[:, u, :], veps[:, u, :], half_neg[:, :],
                                                ALU.pow).then_inc(rooted, 1)

            @block.scalar
            def _(act):
                def split(t, u):
                    nc.scalar.activation(p_hi[:, u], s.prob2[:, :, bass.ds(t * P, P)], ACT.Copy).then_inc(phi_made, 1)

                split(0, 0)
                split(1, 1)
                with act.Fori(0, NT // 2) as i:
                    for u in range(2):
                        t = 2 * i + u
                        act.wait_ge(mixed, t + 1)
                        nc.scalar.activation(p_hi[:, u], s.prob2[:, :, bass.ds((t + 2) % NT * P, P)],
                                             ACT.Copy).then_inc(phi_made, 1)
                        act.wait_ge(turned, t + 1)
                        nc.scalar.activation(xf_t[:, u].rearrange("p (b k) n -> p b (k n)", b=2),
                                             ps_x[:, :, 0:HALF], ACT.Copy).then_inc(xft_kept, 1)

            @block.vector
            def _(dve):
                def split(u):
                    nc.vector.tensor_tensor(p_lo[:, u], s.prob2[:, :, bass.ds(low_at[0], P)],
                                            p_hi[:, u].bitcast(F32), ALU.subtract).then_inc(plo_made, 1)

                low_at = [0]
                for t in range(2):
                    dve.wait_ge(phi_made, t + 1)
                    low_at[0] = t * P
                    split(t)
                steps = dve.alloc_register("f_steps")
                dve.reg_mov(steps, 0)

                def then(ins):
                    ins.then_inc(stat, 1)
                    dve.reg_add(steps, steps, 1)
                    done = dve.snap(steps)
                    dve.wait_ge(br_in, 48)
                    dve.wait_ge(stat, done)

                with dve.Fori(0, NT // 2) as i:
                    for u in range(2):
                        t = 2 * i + u
                        dve.wait_ge(mixed, t + 1)
                        then(nc.vector.tensor_scalar(zi[:, u, 0:1], ps_o[u][:, 1, D - W2H:D - W2H + 1], 1e-16,
                                                     None, ALU.add))
                        then(nc.vector.reciprocal(zi[:, u, 1:2], zi[:, u, 0:1]))
                        dve.wait_ge(x_biased, t + 1)
                        dve.wait_ge(x2_out[u], 16 * i)
                        nc.vector.scalar_tensor_tensor(x2[:, u, 0:W2H], ps_o[u][:, 0, 0:W2H], zi[:, u, 1:2],
                                                       x_in_t[:, u, 0:W2H], ALU.mult, ALU.add)
                        nc.vector.scalar_tensor_tensor(x2[:, u, W2H:D], ps_o[u][:, 1, 0:D - W2H], zi[:, u, 1:2],
                                                       x_in_t[:, u, W2H:D], ALU.mult,
                                                       ALU.add).then_inc(x2_made, 1)
                        dve.wait_ge(x2_made, t + 1)
                        nc.vector.bn_stats(stats[:, u, 0, :], x2[:, u, 0:HALF])
                        then(nc.vector.bn_stats(stats[:, u, 1, :], x2[:, u, HALF:D]))
                        then(nc.vector.bn_aggr(mv[:, u, :], stats[:, u, :, :].rearrange("p a b -> p (a b)")))
                        nc.vector.tensor_scalar(veps[:, u, :], mv[:, u, 1:2], LN_EPS, None,
                                                ALU.add).then_inc(var_made, 1)
                        dve.wait_ge(rooted, t + 1)
                        dve.wait_ge(xf_out[u], 16 * i)
                        nc.vector.tensor_scalar(xf[:, u, :], x2[:, u, :], mv[:, u, 0:1], rstd[:, u, :],
                                                ALU.subtract, ALU.mult).then_inc(xf_made, 1)
                        dve.wait_ge(phi_made, t + 3)
                        low_at[0] = (t + 2) % NT * P
                        split(u)
                        dve.wait_ge(logged, t + 1)
                        nc.vector.tensor_tensor(s.gl[:, bass.ds(t, 1), :].rearrange("p o g -> p (o g)"),
                                                ps_l[:, 0:G], br[:, 0:G], ALU.add)
                        nc.vector.tensor_tensor(s.el[:, bass.ds(t, 1), :].rearrange("p o g -> p (o g)"),
                                                ps_l[:, G:RC], br[:, G:RC], ALU.add).then_inc(logits_kept, 1)

            @block.tensor
            def _(pe):
                pe.wait_ge(wr_in, 16 * (1 + G))

                def mix(t, i, u):
                    pe.wait_ge(plo_made, t + 1)
                    pe.wait_ge(x2_made, 2 * i)
                    for half in range(2):
                        at = half * W2H
                        for k in range(NT):
                            hi, lo = p_hi[:, u, k, :], p_lo[:, u, k, :]
                            for n, (a, b) in enumerate(((hi, s.h2_hi), (hi, s.h2_lo), (lo, s.h2_hi))):
                                last = nc.tensor.matmul(ps_o[u][:, half, 0:W2H], a, b[:, k, at:at + W2H],
                                                        start=(k == 0 and n == 0),
                                                        stop=(k == NT - 1 and n == 2))
                    last.then_inc(mixed, 1)

                def route(t, u):
                    pe.wait_ge(xf_made, t + 1)
                    pe.wait_ge(xft_kept, t)
                    for k in range(KD):
                        last = nc.tensor.transpose(ps_x[:, k // 3, (k % 3) * P:(k % 3 + 1) * P],
                                                   xf[:, u, k * P:(k + 1) * P], s.ident[:, :])
                    last.then_inc(turned, 1)
                    pe.wait_ge(xft_kept, t + 1)
                    pe.wait_ge(logits_kept, t)
                    for k in range(KD):
                        last = nc.tensor.matmul(ps_l[:, 0:RC], xf_t[:, u, k, :], wr[:, k, :],
                                                start=(k == 0), stop=(k == KD - 1))
                    last.then_inc(logged, 1)

                mix(0, 0, 0)
                with pe.Fori(0, NT // 2 - 1) as i:
                    mix(2 * i + 1, i, 1)
                    route(2 * i, 0)
                    mix(2 * i + 2, i + 1, 0)
                    route(2 * i + 1, 1)
                mix(NT - 1, NT // 2 - 1, 1)
                route(NT - 2, 0)
                route(NT - 1, 1)


def plan_experts(nc, s):
    with ExitStack() as ctx:
        def sb(name, shape, dt=F32):
            return ctx.enter_context(nc.sbuf_tensor(name, shape, dt))

        def sem(name):
            return ctx.enter_context(nc.semaphore(name))

        ahead = sb("ahead", [P, NT * G, EG, EG])
        tied = sb("tied", [P, NT * G, EG, EG])
        before = sb("before", [P, EG, EG])
        g_ahead = sb("g_ahead", [P, NT, G, G])
        g_tied = sb("g_tied", [P, NT, G, G])
        rank = sb("rank", [P, NT * G, EG])
        sel = sb("sel", [P, NT * G, EG])
        g_rank = sb("g_rank", [P, NT, G])
        g_sel = sb("g_sel", [P, NT, G])
        peak = sb("peak", [P, NT * G])
        g_peak = sb("g_peak", [P, NT])
        weight = sb("weight", [P, NT * G, EG])
        g_weight = sb("g_weight", [P, NT, G])
        total = sb("total", [P, NT * G])
        g_total = sb("g_total", [P, NT])
        earlier = sb("earlier", [P, NT * G, EG])
        g_earlier = sb("g_earlier", [P, NT, G])
        chosen = sb("chosen", [P, NT, E])
        chosen_b = sb("chosen_b", [P, NT, E], BF16)
        passed = sb("passed", [P, NT + 1, E])
        passed_b = sb("passed_b", [P, NT + 1, E], BF16)
        tail = sb("tail", [P, TW - D])
        tab = sb("tab", [P, NT, 2, E])
        pad_row = sb("pad_row", [1, TW])
        node8_i = sb("node8_i", [P, NT], I32)
        node8 = sb("node8", [P, NT])
        upper = sb("upper", [P, P])
        upper_b = sb("upper_b", [P, P], BF16)
        ones_b = sb("ones_b", [P, P], BF16)
        place_i = sb("place_i", [P, 3, NT, E], I32)
        row_at = sb("row_at", [P, NT, E])
        tile_at = sb("tile_at", [P, NT, E], BF16)
        tile_no = sb("tile_no", [P, NT], I16)
        tile_bf = sb("tile_bf", [P, NT], BF16)
        in_tile = sb("in_tile", [P, NT, E, NT], BF16)
        token = sb("token", [P, NT, E, 2, NT], BF16)
        lane_i = sb("lane_i", [P, 1 + NT], I32)
        lane = sb("lane", [P, 1 + NT])
        is_node = sb("is_node", [P, 1])
        one_row = sb("one_row", [P, 2, NT, P], BF16)
        found = sb("found", [P, NT])
        level = sb("level", [1, NT])
        level_i = sb("level_i", [1, NT], I32)
        over = sb("over", [1, E, NT])
        tiles_f = sb("tiles_f", [1, 2, E])
        sums = sb("sums", [1, 2, E])

        ps_p = ctx.enter_context(nc.psum_tensor("ps_place", [P, 512], F32))
        ps_n = ctx.enter_context(nc.psum_tensor("ps_counts", [P, 512], F32))
        ps_t = ctx.enter_context(nc.psum_tensor("ps_gates_t", [P, 3, 512], F32))
        ps_l = [ctx.enter_context(nc.psum_tensor(f"ps_list{u}", [P, 512], F32)) for u in range(2)]

        consts, step, shifted, exped = sem("g_consts"), sem("g_step"), sem("g_shifted"), sem("g_exped")
        routed, chosen_set, placed = sem("routed"), sem("chosen_set"), sem("placed")
        turned, kept, out_done = sem("gates_turned"), sem("gates_kept"), sem("tab_out")
        rows_made, listed, list_read, values_made = sem("rows_made"), sem("listed"), sem("list_read"), sem("values")
        act_step = sem("g_act_step")

        with nc.Block() as block:
            @block.gpsimd
            def _(pool):
                nc.gpsimd.memset(before[:, :, :], 1.0).then_inc(consts, 1)
                nc.gpsimd.memset(upper[:, :], 1.0).then_inc(consts, 1)
                nc.gpsimd.memset(pad_row[:, :], 0.0).then_inc(consts, 1)
                nc.gpsimd.iota(node8_i[:, :], [[8 * P, NT]], base=0, channel_multiplier=8).then_inc(consts, 1)
                nc.gpsimd.iota(tile_no[:, :], [[1, NT]], base=0, channel_multiplier=0).then_inc(consts, 1)
                nc.gpsimd.iota(lane_i[:, 0:1], [[1, 1]], base=1, channel_multiplier=1).then_inc(consts, 1)
                nc.gpsimd.iota(lane_i[:, 1:1 + NT], [[P, NT]], base=0, channel_multiplier=0).then_inc(consts, 1)
                nc.gpsimd.iota(level_i[:, :], [[P, NT]], base=0, channel_multiplier=0).then_inc(consts, 1)
                nc.gpsimd.memset(ones_b[:, :], 1.0).then_inc(consts, 1)
                nc.gpsimd.memset(s.list_i[:, :], 0).then_inc(consts, 1)
                pool.wait_ge(consts, 10)
                nc.gpsimd.affine_select(out=before[:, :, :], in_=before[:, :, :], compare_op=ALU.is_gt, fill=0.0,
                                        base=0, pattern=[[1, EG], [-1, EG]], channel_multiplier=0).then_inc(consts, 1)
                nc.gpsimd.affine_select(out=upper[:, :], in_=upper[:, :], compare_op=ALU.is_gt, fill=0.0,
                                        base=0, pattern=[[1, P]], channel_multiplier=-1).then_inc(consts, 1)
                nc.gpsimd.memset(pad_row[:, D + E:TW], float(NO_SLOT)).then_inc(consts, 1)

            @block.sync
            def _(sp):
                sp.wait_ge(consts, 13)
                sp.dma_start(s.table.ap()[0:1, :], pad_row[:, :]).then_inc(out_done, 16)
                sp.wait_ge(routed, 1)
                sp.dma_start(s.table.ap()[1:1 + NP, D:TW].rearrange("(t p) c -> p t c", p=P),
                             tab[:, :, :, :].rearrange("p t a e -> p t (a e)")).then_inc(out_done, 16)
                sp.wait_ge(out_done, 32)

            @block.scalar
            def _(act):
                act.wait_ge(shifted, 1)
                nc.scalar.activation(weight[:, :, :], weight[:, :, :], ACT.Exp)
                nc.scalar.activation(g_weight[:, :, :], g_weight[:, :, :], ACT.Exp).then_inc(exped, 1)
                for c, (at, width) in enumerate(PARTS):
                    act.wait_ge(turned, c + 1)
                    nc.scalar.activation(s.gates_t[:, at:at + width], ps_t[0:E, c, 0:width],
                                         ACT.Copy).then_inc(kept, 1)

            @block.vector
            def _(dve):
                n = [0]

                def then(ins):
                    n[0] += 1
                    ins.then_inc(step, 1)
                    dve.wait_ge(step, n[0])

                el = s.el[:, :, :].rearrange("p t (g e) -> p (t g) e", g=G)
                gl = s.gl[:, :, :]
                dve.wait_ge(consts, 13)
                then(nc.vector.tensor_copy(lane[:, :], lane_i[:, :]))
                nc.vector.tensor_scalar(is_node[:, :], lane[:, 0:1], float(TAIL), None, ALU.is_le)
                nc.vector.tensor_reduce(peak[:, :], el, AX.X, ALU.max)
                then(nc.vector.tensor_reduce(g_peak[:, :], gl, AX.X, ALU.max))
                nc.vector.tensor_tensor(weight[:, :, :], el, peak[:, :].unsqueeze(2).broadcast_to([P, NT * G, EG]),
                                        ALU.subtract)
                nc.vector.tensor_tensor(g_weight[:, :, :], gl, g_peak[:, :].unsqueeze(2).broadcast_to([P, NT, G]),
                                        ALU.subtract).then_inc(shifted, 1)
                wide = [P, NT * G, EG, EG]
                nc.vector.tensor_tensor(ahead[:, :, :, :], el.unsqueeze(2).broadcast_to(wide),
                                        el.unsqueeze(3).broadcast_to(wide), ALU.is_gt)
                nc.vector.tensor_tensor(tied[:, :, :, :], el.unsqueeze(2).broadcast_to(wide),
                                        el.unsqueeze(3).broadcast_to(wide), ALU.is_equal)
                g_wide = [P, NT, G, G]
                nc.vector.tensor_tensor(g_ahead[:, :, :, :], gl.unsqueeze(2).broadcast_to(g_wide),
                                        gl.unsqueeze(3).broadcast_to(g_wide), ALU.is_gt)
                then(nc.vector.tensor_tensor(g_tied[:, :, :, :], gl.unsqueeze(2).broadcast_to(g_wide),
                                             gl.unsqueeze(3).broadcast_to(g_wide), ALU.is_equal))
                nc.vector.tensor_tensor(tied[:, :, :, :], tied[:, :, :, :],
                                        before[:, :, :].unsqueeze(1).broadcast_to(wide), ALU.mult)
                then(nc.vector.tensor_tensor(g_tied[:, :, :, :], g_tied[:, :, :, :],
                                             before[:, 0:G, 0:G].unsqueeze(1).broadcast_to(g_wide), ALU.mult))
                nc.vector.tensor_tensor(ahead[:, :, :, :], ahead[:, :, :, :], tied[:, :, :, :], ALU.add)
                then(nc.vector.tensor_tensor(g_ahead[:, :, :, :], g_ahead[:, :, :, :], g_tied[:, :, :, :], ALU.add))
                nc.vector.tensor_reduce(rank[:, :, :], ahead[:, :, :, :], AX.X, ALU.add)
                then(nc.vector.tensor_reduce(g_rank[:, :, :], g_ahead[:, :, :, :], AX.X, ALU.add))
                nc.vector.tensor_scalar(sel[:, :, :], rank[:, :, :], float(KE), None, ALU.is_lt)
                then(nc.vector.tensor_scalar(g_sel[:, :, :], g_rank[:, :, :], float(KG), None, ALU.is_lt))
                all_g = g_sel[:, :, :].rearrange("p t g -> p (t g)").unsqueeze(2).broadcast_to([P, NT * G, EG])
                then(nc.vector.tensor_tensor(chosen[:, :, :].rearrange("p t (g e) -> p (t g) e", g=G),
                                             sel[:, :, :], all_g, ALU.mult))
                then(nc.vector.tensor_scalar(chosen[:, NT - 1, :], chosen[:, NT - 1, :], is_node[:, 0:1], None,
                                             ALU.mult))
                nc.vector.tensor_copy(chosen_b[:, :, :], chosen[:, :, :])
                nc.vector.tensor_copy(upper_b[:, :], upper[:, :])
                then(nc.vector.memset(passed[:, 0, :], 0.0))
                for t in range(NT):
                    then(nc.vector.tensor_tensor(passed[:, t + 1, :], passed[:, t, :], chosen[:, t, :], ALU.add))
                nc.vector.tensor_copy(passed_b[:, :, :], passed[:, :, :]).then_inc(chosen_set, 1)
                nc.vector.memset(earlier[:, :, 0:1], 0.0)
                then(nc.vector.memset(g_earlier[:, :, 0:1], 0.0))
                for j in range(1, EG):
                    last = nc.vector.tensor_tensor(earlier[:, :, j:j + 1], earlier[:, :, j - 1:j],
                                                   sel[:, :, j - 1:j], ALU.add)
                    if j < G:
                        last = nc.vector.tensor_tensor(g_earlier[:, :, j:j + 1], g_earlier[:, :, j - 1:j],
                                                       g_sel[:, :, j - 1:j], ALU.add)
                    then(last)
                nc.vector.tensor_copy(node8[:, :], node8_i[:, :])
                nc.vector.tensor_copy(tile_bf[:, :], tile_no[:, :])
                then(nc.vector.tensor_copy(level[:, :], level_i[:, :]))
                then(nc.vector.scalar_tensor_tensor(g_earlier[:, :, :], g_earlier[:, :, :], float(KE),
                                                    node8[:, :].unsqueeze(2).broadcast_to([P, NT, G]),
                                                    ALU.mult, ALU.add))
                all_g = g_earlier[:, :, :].rearrange("p t g -> p (t g)").unsqueeze(2) \
                    .broadcast_to([P, NT * G, EG])
                then(nc.vector.tensor_tensor(earlier[:, :, :], earlier[:, :, :], all_g, ALU.add))
                nc.vector.tensor_copy(tab[:, :, 1, :], earlier[:, :, :].rearrange("p (t g) e -> p t (g e)", g=G))
                dve.wait_ge(exped, 1)
                nc.vector.tensor_tensor(weight[:, :, :], weight[:, :, :], sel[:, :, :], ALU.mult)
                then(nc.vector.tensor_tensor(g_weight[:, :, :], g_weight[:, :, :], g_sel[:, :, :], ALU.mult))
                nc.vector.tensor_reduce(total[:, :], weight[:, :, :], AX.X, ALU.add)
                then(nc.vector.tensor_reduce(g_total[:, :], g_weight[:, :, :], AX.X, ALU.add))
                nc.vector.reciprocal(total[:, :], total[:, :])
                then(nc.vector.reciprocal(g_total[:, :], g_total[:, :]))
                nc.vector.tensor_tensor(weight[:, :, :], weight[:, :, :],
                                        total[:, :].unsqueeze(2).broadcast_to([P, NT * G, EG]), ALU.mult)
                then(nc.vector.tensor_tensor(g_weight[:, :, :], g_weight[:, :, :],
                                             g_total[:, :].unsqueeze(2).broadcast_to([P, NT, G]), ALU.mult))
                nc.vector.scalar_tensor_tensor(weight[:, :, :], weight[:, :, :], GATE_MIN, weight[:, :, :],
                                               ALU.is_ge, ALU.mult)
                then(nc.vector.scalar_tensor_tensor(g_weight[:, :, :], g_weight[:, :, :], GATE_MIN,
                                                    g_weight[:, :, :], ALU.is_ge, ALU.mult))
                all_g = g_weight[:, :, :].rearrange("p t g -> p (t g)").unsqueeze(2).broadcast_to([P, NT * G, EG])
                then(nc.vector.tensor_tensor(weight[:, :, :], weight[:, :, :], all_g, ALU.mult))
                nc.vector.tensor_copy(tab[:, :, 0, :],
                                      weight[:, :, :].rearrange("p (t g) e -> p t (g e)", g=G)).then_inc(routed, 1)
                dve.wait_ge(placed, 1)
                then(nc.vector.tensor_copy(place_i[:, 0], ps_p[:, 0:NT * E].rearrange("p (t e) -> p t e", e=E)))
                nc.vector.tensor_scalar(place_i[:, 1], place_i[:, 0], 7, None, ALU.arith_shift_right)
                then(nc.vector.tensor_scalar(place_i[:, 2], place_i[:, 0], P - 1, None, ALU.bitwise_and))
                nc.vector.tensor_copy(tile_at[:, :, :], place_i[:, 1])
                then(nc.vector.tensor_copy(row_at[:, :, :], place_i[:, 2]))
                then(nc.vector.scalar_tensor_tensor(row_at[:, :, :], row_at[:, :, :], 1.0, chosen[:, :, :],
                                                    ALU.add, ALU.mult))
                nc.vector.tensor_scalar(row_at[:, :, :], row_at[:, :, :], -1.0, None, ALU.add)
                then(nc.vector.tensor_tensor(
                    in_tile[:, :, :, :].rearrange("p t e a -> p (t e) a"),
                    tile_at[:, :, :].rearrange("p t e -> p (t e)").unsqueeze(2).broadcast_to([P, NT * E, NT]),
                    tile_bf[:, :].unsqueeze(1).broadcast_to([P, NT * E, NT]), ALU.is_equal))
                nc.vector.tensor_scalar(token[:, :, :, 0, :], in_tile[:, :, :, :], lane[:, 0:1], None, ALU.mult)
                for t in range(NT):
                    last = nc.vector.tensor_scalar(token[:, t, :, 1, :], in_tile[:, t, :, :], float(P * t), None,
                                                   ALU.mult)
                last.then_inc(values_made, 1)
                nc.vector.tensor_tensor(over[:, :, :], ps_n[0:1, 0:E].unsqueeze(2).broadcast_to([1, E, NT]),
                                        level[:, :].unsqueeze(1).broadcast_to([1, E, NT]), ALU.is_gt)
                then(nc.vector.memset(sums[:, :, :], 0.0))
                then(nc.vector.tensor_reduce(tiles_f[:, 0, :], over[:, :, :], AX.X, ALU.add))
                then(nc.vector.tensor_scalar(tiles_f[:, 1, :], tiles_f[:, 0, :], float(MIN_TILES), None, ALU.max))
                nc.vector.tensor_copy(s.tiles[:, :], tiles_f[:, 1, :])
                then(nc.vector.tensor_copy(sums[:, 0, 1:E], tiles_f[:, 1, 0:E - 1]))
                reach, u = 1, 0
                while reach < E:
                    nc.vector.tensor_copy(sums[:, 1 - u, 0:reach], sums[:, u, 0:reach])
                    then(nc.vector.tensor_tensor(sums[:, 1 - u, reach:E], sums[:, u, reach:E],
                                                 sums[:, u, 0:E - reach], ALU.add))
                    reach, u = 2 * reach, 1 - u
                then(nc.vector.tensor_copy(s.starts[:, :], sums[:, u, :]))
                with dve.Fori(0, E // 2) as i:
                    for u in range(2):
                        e = 2 * i + u
                        dve.wait_ge(listed, e)
                        for t in range(NT):
                            last = nc.vector.tensor_scalar(one_row[:, u, t, :], s.column[:, 0:P],
                                                           row_at[:, t, bass.ds(e, 1)], None, ALU.is_equal)
                        last.then_inc(rows_made, 1)
                        dve.wait_ge(listed, e + 1)
                        start = dve.value_load(s.starts[0:1, bass.ds(e, 1)], min_val=0,
                                               max_val=LIST - NT)
                        nc.vector.tensor_copy(s.list_i[:, bass.ds(start, NT)],
                                              ps_l[u][:, 0:NT]).then_inc(list_read, 1)
                        dve.wait_ge(list_read, e + 1)

            @block.tensor
            def _(pe):
                pe.wait_ge(chosen_set, 1)
                nc.tensor.matmul(ps_n[:, 0:E], ones_b[:, :], passed_b[:, NT, :], start=True, stop=True)
                nc.tensor.matmul(ps_p[:, 0:NT * E], upper_b[:, :], chosen_b[:, :, :].rearrange("p t e -> p (t e)"),
                                 start=True, stop=False)
                nc.tensor.matmul(ps_p[:, 0:NT * E], ones_b[:, :],
                                 passed_b[:, 0:NT, :].rearrange("p t e -> p (t e)"),
                                 start=False, stop=True).then_inc(placed, 1)
                pe.wait_ge(routed, 1)
                for c, (at, width) in enumerate(PARTS):
                    for t in range(at // P, (at + width) // P):
                        last = nc.tensor.transpose(ps_t[0:E, c, t * P - at:(t + 1) * P - at], tab[:, t, 0, :],
                                                   s.ident[:, :])
                    last.then_inc(turned, 1)
                pe.wait_ge(values_made, 1)
                with pe.Fori(0, E // 2) as i:
                    for u in range(2):
                        e = 2 * i + u
                        pe.wait_ge(rows_made, e + 1)
                        pe.wait_ge(list_read, 2 * i)
                        for t in range(NT):
                            for part in range(2):
                                last = nc.tensor.matmul(ps_l[u][:, 0:NT], one_row[:, u, t, :],
                                                        token[:, t, bass.ds(e, 1), part, :]
                                                        .rearrange("p o a -> p (o a)"),
                                                        start=(t == 0 and part == 0),
                                                        stop=(t == NT - 1 and part == 1))
                        last.then_inc(listed, 1)


def run_experts(nc, s, w1, b1, w2):
    with ExitStack() as ctx:
        def sb(name, shape, dt=F32):
            return ctx.enter_context(nc.sbuf_tensor(name, shape, dt))

        def sem(name):
            return ctx.enter_context(nc.semaphore(name))

        ROW = KD * HID
        PIECE = ROW // 3
        raw1 = sb("raw1", [P, 2, ROW])
        raw2 = sb("raw2", [P, 2, ROW])
        w1_hi, w1_lo = sb("e1_hi", [P, 2, ROW], F32R), sb("e1_lo", [P, 2, ROW], F32R)
        w2_hi, w2_lo = sb("e2_hi", [P, 2, ROW], F32R), sb("e2_lo", [P, 2, ROW], F32R)
        b1_all = sb("b1_all", [P, RING, HID])
        rows = sb("rows", [P, TW])
        index = sb("index", [P, 1], I32)
        slot = sb("slot", [P, 1], I32)
        meta = sb("meta", [P, RING, 2])
        xt_hi, xt_lo = sb("e_xt_hi", [P, KD, P], F32R), sb("e_xt_lo", [P, KD, P], F32R)
        h_in = sb("h_in", [P, HID])
        h_act = sb("h_act", [P, HID])
        ht_hi, ht_lo = sb("e_ht_hi", [P, KH, P], F32R), sb("e_ht_lo", [P, KH, P], F32R)
        y = sb("y", [P, D])

        ps_h = ctx.enter_context(nc.psum_tensor("ps_h_2", [P, 512], F32))
        ps_x = ctx.enter_context(nc.psum_tensor("ps_xt", [P, 2, 512], F32))
        ps_y = ctx.enter_context(nc.psum_tensor("ps_y", [P, 2, 512], F32))
        ps_t = ctx.enter_context(nc.psum_tensor("ps_ht", [P, 512], F32))

        w1_in, w2_in, b1_in = sem("e_w1_in"), sem("e_w2_in"), sem("e_b1_in")
        w1_hi_made, w1_lo_made, w2_hi_made, w2_lo_made = (sem("e_w1_hi"), sem("e_w1_lo"), sem("e_w2_hi"),
                                                          sem("e_w2_lo"))
        gathered, turned, x_hi_made, x_lo_made = sem("gathered"), sem("x_turned"), sem("x_hi"), sem("x_lo")
        h_summed, biased, gelued, h_turned = sem("h_summed_2"), sem("biased"), sem("gelued"), sem("h_turned")
        h_hi_made, h_lo_made, y_summed, y_made = sem("h_hi"), sem("h_lo"), sem("y_summed"), sem("y_made")
        meta_made, index_set, slot_set, scattered, ready = (sem("meta_made"), sem("index_set"), sem("slot_set"),
                                                            sem("scattered"), sem("h_ready"))

        def tiles_of(eng, e):
            return eng.value_load(s.tiles[0:1, bass.ds(e, 1)], min_val=MIN_TILES, max_val=NT)

        def over_tiles(eng, name, tile, around=None):
            count = eng.alloc_register(name)
            eng.reg_mov(count, 0)

            def one(e, head, start=False, last=False):
                k = eng.snap(count)
                tile(k, e, head, start, last)
                eng.reg_add(count, count, 1)

            def expert(e, start=False, last=False):
                one(e, True, start, last)
                with eng.Fori(1, tiles_of(eng, e)):
                    one(e, False)

            expert(0, start=True)
            with eng.Fori(1, E - 1) as e:
                expert(e)
            expert(E - 1, last=True)
            return eng.snap(count)

        with nc.Block() as block:
            @block.sync
            def _(sp):
                def load(e, u):
                    sp.dma_start(raw1[:, u, :].rearrange("p (k m) -> p k m", k=KD),
                                 w1[bass.ds(e * D, D), :].rearrange("(k p) m -> p k m", p=P)).then_inc(w1_in, 16)
                    sp.dma_start(raw2[:, u, :].rearrange("p (k d) -> p k d", k=KH),
                                 w2[bass.ds(e * HID, HID), :].rearrange("(k p) d -> p k d", p=P)) \
                      .then_inc(w2_in, 16)
                    sp.dma_start(b1_all[:, bass.ds(e % RING, 1), :].rearrange("p o m -> p (o m)"),
                                 b1[bass.ds(e, 1), :].broadcast_to([P, HID])).then_inc(b1_in, 16)

                def loaded(e):
                    sp.wait_ge(w1_in, 16 * e + 16)
                    sp.wait_ge(w2_in, 16 * e + 16)
                    sp.wait_ge(b1_in, 16 * e + 16)

                load(0, 0)
                loaded(0)
                load(1, 1)
                with sp.Fori(1, E // 2) as i:
                    for u in range(2):
                        e = 2 * i + u
                        loaded(e - 1)
                        sp.wait_ge(w1_lo_made, 3 * e - 3)
                        sp.wait_ge(w2_lo_made, 3 * e - 3)
                        load(e, u)
                loaded(E - 1)

            @block.gpsimd
            def _(pool):
                def gather(column):
                    nc.gpsimd.tensor_copy(index[:, :], s.list_i[:, bass.ds(column, 1)]).then_inc(index_set, 1)
                    pool.wait_ge(ready, 1)
                    pool.wait_ge(index_set, column + 1)
                    nc.gpsimd.indirect_dma_start(rows[:, :], None, s.table.ap(),
                                                 bass.IndirectOffsetOnAxis(index[:, 0:1], 0),
                                                 bounds_check=NP, oob_is_err=False).then_inc(gathered, 16)

                def scatter(k, ring):
                    pool.wait_ge(y_made, k + 1)
                    pool.wait_ge(ready, 1)
                    pool.wait_ge(scattered, 16 * k)
                    nc.gpsimd.tensor_copy(slot[:, :], meta[:, bass.ds(ring, 1), 1:2]
                                          .rearrange("p o c -> p (o c)")).then_inc(slot_set, 1)
                    pool.wait_ge(ready, 1)
                    pool.wait_ge(slot_set, k + 1)
                    nc.gpsimd.indirect_dma_start(s.slots_dram.ap(), bass.IndirectOffsetOnAxis(slot[:, 0:1], 0),
                                                 y[:, :], None, bounds_check=PAIRS - 1,
                                                 oob_is_err=False).then_inc(scattered, 16)

                def tile(k, e, head, start, last):
                    pool.wait_ge(ready, 1)
                    pool.wait_ge(turned, k + 1)
                    nc.gpsimd.tensor_copy(meta[:, bass.ds((k + 2) % RING, 1), 0:1].rearrange("p o c -> p (o c)"),
                                          rows[:, bass.ds(e + D, 1)])
                    nc.gpsimd.tensor_copy(meta[:, bass.ds((k + 2) % RING, 1), 1:2].rearrange("p o c -> p (o c)"),
                                          rows[:, bass.ds(e + (D + E), 1)]).then_inc(meta_made, 1)
                    pool.wait_ge(ready, 1)
                    pool.wait_ge(meta_made, k + 1)
                    gather(k + 1)
                    scatter(k, k % RING)

                nc.gpsimd.memset(meta[:, :, :], float(NO_SLOT)).then_inc(ready, 1)
                pool.wait_ge(ready, 1)
                gather(0)
                n = over_tiles(pool, "pool_tiles", tile)
                for after in range(2):
                    scatter(n + after, (n + after) % RING)
                pool.wait_ge(gathered, 16 * n + 16)
                pool.wait_ge(scattered, 16 * n + 32)

            @block.scalar
            def _(act):
                def split(raw, hi, piece, u, made):
                    at = piece * PIECE
                    nc.scalar.activation(hi[:, u, at:at + PIECE], raw[:, u, at:at + PIECE],
                                         ACT.Copy).then_inc(made, 1)

                def split_x(k):
                    act.wait_ge(turned, k + 1)
                    nc.scalar.activation(xt_hi[:, :, :].rearrange("p (b k) n -> p b (k n)", b=2),
                                         ps_x[:, :, 0:HALF], ACT.Copy).then_inc(x_hi_made, 1)

                def weights(e, which):
                    raw, hi, arrived, made = ((raw1, w1_hi, w1_in, w1_hi_made), (raw2, w2_hi, w2_in, w2_hi_made))[which]
                    act.wait_ge(arrived, 16 * e + 16)
                    for piece in range(3):
                        at = piece * PIECE
                        u = bass.ds(e % 2, 1)
                        nc.scalar.activation(hi[:, u, at:at + PIECE], raw[:, u, at:at + PIECE],
                                             ACT.Copy).then_inc(made, 1)

                def tile(k, e, head, start, last):
                    act.wait_ge(biased, k + 1)
                    if not start:
                        act.wait_ge(h_turned, k)
                    nc.scalar.activation(h_act[:, :], h_in[:, :], ACT.Gelu).then_inc(gelued, 1)
                    split_x(k + 1)
                    if head and not last:
                        weights(e + 1, 0)
                    act.wait_ge(h_turned, k + 1)
                    nc.scalar.activation(ht_hi[:, :, :].rearrange("p k n -> p (k n)"), ps_t[:, 0:HID],
                                         ACT.Copy).then_inc(h_hi_made, 1)
                    if head and not last:
                        weights(e + 1, 1)

                weights(0, 0)
                split_x(0)
                weights(0, 1)
                over_tiles(act, "act_tiles", tile)

            @block.vector
            def _(dve):
                def split_x(k):
                    dve.wait_ge(x_hi_made, k + 1)
                    nc.vector.tensor_tensor(xt_lo[:, :, :].rearrange("p (b k) n -> p b (k n)", b=2),
                                            ps_x[:, :, 0:HALF],
                                            xt_hi[:, :, :].bitcast(F32).rearrange("p (b k) n -> p b (k n)", b=2),
                                            ALU.subtract).then_inc(x_lo_made, 1)

                def weights(e, which):
                    raw, hi, lo, halved, made = ((raw1, w1_hi, w1_lo, w1_hi_made, w1_lo_made),
                                                 (raw2, w2_hi, w2_lo, w2_hi_made, w2_lo_made))[which]
                    for piece in range(3):
                        at = piece * PIECE
                        u = bass.ds(e % 2, 1)
                        dve.wait_ge(halved, 3 * e + piece + 1)
                        nc.vector.tensor_tensor(lo[:, u, at:at + PIECE], raw[:, u, at:at + PIECE],
                                                hi[:, u, at:at + PIECE].bitcast(F32),
                                                ALU.subtract).then_inc(made, 1)

                def keep_y(k):
                    dve.wait_ge(y_summed, k)
                    dve.wait_ge(meta_made, k)
                    dve.wait_ge(scattered, 16 * k + 16)
                    nc.vector.tensor_scalar(y[:, :].rearrange("p (b d) -> p b d", b=2), ps_y[:, :, 0:HALF],
                                            meta[:, bass.ds((k + 1) % RING, 1), 0:1].rearrange("p o c -> p (o c)"),
                                            None, ALU.mult).then_inc(y_made, 1)

                def tile(k, e, head, start, last):
                    dve.wait_ge(h_summed, k + 1)
                    if head:
                        dve.wait_ge(b1_in, 16 * e + 16)
                    if not start:
                        dve.wait_ge(gelued, k)
                    nc.vector.tensor_tensor(h_in[:, :], ps_h[:, 0:HID],
                                            b1_all[:, bass.ds(e % RING, 1), :].rearrange("p o m -> p (o m)"),
                                            ALU.add).then_inc(biased, 1)
                    split_x(k + 1)
                    if head and not last:
                        weights(e + 1, 0)
                    if not start:
                        keep_y(k)
                    dve.wait_ge(h_hi_made, k + 1)
                    nc.vector.tensor_tensor(ht_lo[:, :, :].rearrange("p k n -> p (k n)"), ps_t[:, 0:HID],
                                            ht_hi[:, :, :].bitcast(F32).rearrange("p k n -> p (k n)"),
                                            ALU.subtract).then_inc(h_lo_made, 1)
                    if head and not last:
                        weights(e + 1, 1)

                nc.vector.memset(y[:, :], 0.0).then_inc(y_made, 1)
                dve.wait_ge(y_made, 1)
                dve.sem_inc(y_made, 1)
                weights(0, 0)
                split_x(0)
                weights(0, 1)
                n = over_tiles(dve, "dve_tiles", tile)
                keep_y(n)

            @block.tensor
            def _(pe):
                def turn_x(k):
                    pe.wait_ge(gathered, 16 * k + 16)
                    for c in range(KD):
                        last = nc.tensor.transpose(ps_x[:, c // 3, (c % 3) * P:(c % 3 + 1) * P],
                                                   rows[:, c * P:(c + 1) * P], s.ident[:, :])
                    last.then_inc(turned, 1)

                def down(k, u):
                    pe.wait_ge(h_lo_made, k)
                    pe.wait_ge(y_made, k + 1)
                    for half in range(2):
                        for c in range(KH):
                            at = c * D + half * HALF
                            hi, lo = ht_hi[:, c, :], ht_lo[:, c, :]
                            for n, (a, b) in enumerate(((hi, w2_hi), (hi, w2_lo), (lo, w2_hi))):
                                last = nc.tensor.matmul(ps_y[:, half, 0:HALF], a,
                                                        b[:, bass.ds(u, 1), at:at + HALF]
                                                        .rearrange("p o d -> p (o d)"),
                                                        start=(c == 0 and n == 0),
                                                        stop=(c == KH - 1 and n == 2))
                    last.then_inc(y_summed, 1)

                def tile(k, e, head, start, last):
                    if head:
                        pe.wait_ge(w1_lo_made, 3 * e + 3)
                    pe.wait_ge(x_lo_made, k + 1)
                    if not start:
                        pe.wait_ge(biased, k)
                    for c in range(KD):
                        hi, lo = xt_hi[:, c, :], xt_lo[:, c, :]
                        for n, (a, b) in enumerate(((hi, w1_hi), (hi, w1_lo), (lo, w1_hi))):
                            summed = nc.tensor.matmul(ps_h[:, 0:HID], a,
                                                      b[:, bass.ds(e % 2, 1), c * HID:(c + 1) * HID]
                                                      .rearrange("p o m -> p (o m)"),
                                                      start=(c == 0 and n == 0), stop=(c == KD - 1 and n == 2))
                    summed.then_inc(h_summed, 1)
                    turn_x(k + 1)
                    if not head:
                        pe.wait_ge(w2_lo_made, 3 * e + 3)
                        down(k, e % 2)
                    elif not start:
                        down(k, (e + 1) % 2)
                    pe.wait_ge(gelued, k + 1)
                    if not start:
                        pe.wait_ge(h_lo_made, k)
                    for c in range(KH):
                        last_t = nc.tensor.transpose(ps_t[:, c * P:(c + 1) * P], h_act[:, c * P:(c + 1) * P],
                                                     s.ident[:, :])
                    last_t.then_inc(h_turned, 1)

                turn_x(0)
                n = over_tiles(pe, "pe_tiles", tile)
                down(n, (E - 1) % 2)


def add_up(nc, s, b2, out):
    with ExitStack() as ctx:
        def sb(name, shape, dt=F32):
            return ctx.enter_context(nc.sbuf_tensor(name, shape, dt))

        def sem(name):
            return ctx.enter_context(nc.semaphore(name))

        PAIR = KG * KE
        b2_all = sb("b2_all", [E, D])
        got = sb("got", [P, 2, PAIR, D])
        base = sb("base", [P, 2, D])
        total = sb("node_total", [P, 2, D])
        ps = [ctx.enter_context(nc.psum_tensor(f"ps_bias{u}", [P, 2, 512], F32)) for u in range(2)]
        b2_in, biased, step = sem("b2_in"), sem("bias_summed"), sem("i_step")
        slots_in = [sem("slots_in0"), sem("slots_in1")]
        base_in = [sem("base_in0"), sem("base_in1")]
        out_done = [sem("node_out0"), sem("node_out1")]
        added, halved = sem("added"), sem("halved")

        def size(t):
            return P if t < NT - 1 else TAIL

        with nc.Block() as block:
            @block.sync
            def _(sp):
                for t in range(NT):
                    u, m = t % 2, size(t)
                    if t >= 2:
                        sp.wait_ge(added, t - 1)
                    sp.dma_start(got[0:m, u], s.slots_dram.ap()[t * P * PAIR:(t * P + m) * PAIR, :]
                                 .rearrange("(p j) d -> p j d", j=PAIR)).then_inc(slots_in[u], 16)

            @block.scalar
            def _(act):
                act.dma_start(b2_all[:, :], b2).then_inc(b2_in, 16)
                for t in range(2):
                    act.dma_start(base[:, t, :], s.x2_dram.ap()[t * P:(t + 1) * P, :]).then_inc(base_in[t], 16)
                for t in range(NT):
                    u, m = t % 2, size(t)
                    act.wait_ge(added, t + 1)
                    act.dma_start(out[t * P:t * P + m, :], total[0:m, u, :]).then_inc(out_done[u], 16)
                    if t + 2 < NT:
                        act.dma_start(base[:, u, :], s.x2_dram.ap()[(t + 2) * P:(t + 3) * P, :]) \
                           .then_inc(base_in[u], 16)
                for u in range(2):
                    act.wait_ge(out_done[u], 16 * (NT // 2))

            @block.tensor
            def _(pe):
                pe.wait_ge(b2_in, 16)
                for t in range(NT):
                    u = t % 2
                    if t >= 2:
                        pe.wait_ge(halved, t - 1)
                    for half in range(2):
                        last = nc.tensor.matmul(ps[u][:, half, 0:HALF], s.gates_t[:, t * P:(t + 1) * P],
                                                b2_all[:, half * HALF:(half + 1) * HALF], start=True, stop=True)
                    last.then_inc(biased, 1)

            @block.vector
            def _(dve):
                n = [0]

                def then(ins):
                    n[0] += 1
                    ins.then_inc(step, 1)
                    dve.wait_ge(step, n[0])

                for t in range(NT):
                    u, i, m = t % 2, t // 2, size(t)
                    dve.wait_ge(biased, t + 1)
                    dve.wait_ge(base_in[u], 16 * (i + 1))
                    nc.vector.tensor_tensor(base[0:m, u, :].rearrange("p (b d) -> p b d", b=2),
                                            ps[u][0:m, :, 0:HALF],
                                            base[0:m, u, :].rearrange("p (b d) -> p b d", b=2),
                                            ALU.add).then_inc(halved, 1)
                    dve.wait_ge(halved, t + 1)
                    dve.wait_ge(slots_in[u], 16 * (i + 1))
                    then(nc.vector.tensor_tensor(got[0:m, u, 0:4], got[0:m, u, 0:4], got[0:m, u, 4:8], ALU.add))
                    then(nc.vector.tensor_tensor(got[0:m, u, 0:2], got[0:m, u, 0:2], got[0:m, u, 2:4], ALU.add))
                    then(nc.vector.tensor_tensor(got[0:m, u, 0], got[0:m, u, 0], got[0:m, u, 1], ALU.add))
                    if t >= 2:
                        dve.wait_ge(out_done[u], 16 * i)
                    nc.vector.tensor_tensor(total[0:m, u, :], got[0:m, u, 0], base[0:m, u, :],
                                            ALU.add).then_inc(added, 1)


def program(nc, x, edge_src, edge_dst, w1, att1, bias1, w2, att2, bias2, wg, we, bg, be, ew1, eb1, ew2, eb2, out):
    s = Shared()
    s.early = []
    with ExitStack() as ctx:
        def sb(name, shape, dt=F32, where=ctx, side="left"):
            return where.enter_context(nc.sbuf_tensor(name, shape, dt, side=side))

        s.al_dram = nc.dram_tensor("al_dram", [2 * H1, NP], F32)
        s.mask_dram = nc.dram_tensor("mask_dram", [NT, P, NP], BF16)
        s.rel_dram = nc.dram_tensor("rel_dram", [2 * H1, NP], F32)
        s.z_dram = nc.dram_tensor("z_dram", [H1, N], F32)
        s.zi_dram = nc.dram_tensor("zi_dram", [H1, N], F32)
        s.count_dram = nc.dram_tensor("count_dram", [P, NT, NP], U16)
        s.al2_dram = nc.dram_tensor("al2_dram", [2, NP], F32)
        s.rel2_dram = nc.dram_tensor("rel2_dram", [2, NP], F32)
        s.x2_dram = nc.dram_tensor("x2_dram", [NP, D], F32)
        s.table = nc.dram_tensor("table", [NP + 1, TW], F32)
        s.slots_dram = nc.dram_tensor("slots_dram", [PAIRS, D], F32)
        s.ident = sb("ident", [P, P])
        s.column = sb("column", [P, NP], I16)
        s.al_col = sb("al_col", [P, NT, 2 * H1])
        s.al2_col = sb("al2_col", [P, NT, 2])
        s.gl = sb("gl", [P, NT, G])
        s.el = sb("el", [P, NT, E])
        s.al_max = sb("al_max", [P, NT, H1])
        with ExitStack() as layer1:
            with ExitStack() as inputs1:
                s.ranges = sb("ranges", [1, 2 * NT], I32, where=inputs1)
                s.block_col = sb("block_col", [P, NT], where=inputs1)
                s.src_f = sb("src_f", [P, ET], where=inputs1)
                s.dst_f = sb("dst_f", [P, ET], where=inputs1)
                s.x_t = sb("x_t", [P, NT, KD, P], where=inputs1)
                s.w1_hi = sb("w1_hi", [P, KD, D], F32R, where=inputs1)
                s.w1_lo = sb("w1_lo", [P, KD, D], F32R, where=inputs1)
                node_features(nc, s, x, w1, edge_src, edge_dst, att1)
                nc.clear_and_free_semaphores(s.early)
                nc.all_engine_barrier()
                s.count = sb("count", [P, NT, NP], U16, where=layer1, side="right")
                s.h_ext = sb("h_ext", [P, NT, H1, C1 + 1], where=layer1, side="right")
                transform_and_count(nc, s)
            g_held = ExitStack()
            s.g_t = sb("g_t", [C1, H1, NP], where=g_held)
            attend_by_head(nc, s, bias1)
        with ExitStack() as layer2:
            s.h2_hi = sb("h2_hi", [P, NT, D + 4], F32R, where=layer2, side="right")
            s.h2_lo = sb("h2_lo", [P, NT, D + 4], F32R, where=layer2, side="right")
            transform_again(nc, s, w2, att2)
            g_held.close()
            s.prob2 = sb("prob2", [P, NT, NP], where=layer2, side="right")
            attention_again(nc, s)
            mix_and_route(nc, s, x, bias2, wg, we, bg, be)
        with ExitStack() as routing:
            s.tiles = sb("tiles", [1, E], I32, where=routing)
            s.starts = sb("starts", [1, E], I32, where=routing)
            s.list_i = sb("list_i", [P, LIST], I32, where=routing)
            s.gates_t = sb("gates_t", [E, NP], where=routing)
            plan_experts(nc, s)
            run_experts(nc, s, ew1, eb1, ew2)
            add_up(nc, s, eb2, out)


def kernel(**inputs):
    import numpy as np
    import concourse.bacc as bacc
    from concourse.bass_utils import run_bass_kernel_spmd

    def edges(ends):
        padded = np.full(ET * P, -1, np.int32)
        padded[:EDGES] = ends
        return padded.reshape(ET, P).T

    def columns(a):
        return a.reshape(KD, P).T

    a = {name: np.asarray(value) for name, value in inputs.items()}
    gnn = {name[7:]: value for name, value in a.items() if name.startswith("L0_gnn_")}
    ffn = {name[7:]: value for name, value in a.items() if name.startswith("L0_ffn_")}
    x = np.zeros((NP, D), np.float32)
    x[:N] = a["x"]
    laid = {
        "x": x,
        "edge_src": edges(a["src"]),
        "edge_dst": edges(a["dst"]),
        "w1": gnn["W1"],
        "att1": np.stack([columns(gnn["a_src1"]), columns(gnn["a_dst1"])], 1),
        "bias1": gnn["b1"].reshape(H1, C1).T,
        "w2": gnn["W2"],
        "att2": np.concatenate([gnn["a_src2"], gnn["a_dst2"]], 1),
        "bias2": gnn["b2"].reshape(1, D),
        "wg": ffn["Wg"],
        "we": ffn["We"],
        "bg": ffn["bg"].reshape(1, G),
        "be": ffn["be"].reshape(1, E),
        "ew1": ffn["W1"].reshape(E * D, HID),
        "eb1": ffn["b1"].reshape(E, HID),
        "ew2": ffn["W2"].reshape(E * HID, D),
        "eb2": ffn["b2"].reshape(E, D),
    }
    laid = {f"in_{name}": np.ascontiguousarray(value) for name, value in laid.items()}
    nc = bacc.Bacc("TRN2", target_bir_lowering=False, num_devices=1)
    args = [nc.dram_tensor(name, value.shape, mybir.dt.from_np(value.dtype), kind="ExternalInput").ap()
            for name, value in laid.items()]
    out = nc.dram_tensor("out_nodes", (N, D), F32, kind="ExternalOutput")
    program(nc, *args, out.ap())
    ran = run_bass_kernel_spmd(nc, [laid], core_ids=[0])
    return ran.results[0]["out_nodes"]
```

```python
import concourse.bass as bass
from concourse import mybir
from contextlib import ExitStack

F32 = mybir.dt.float32
F32R = mybir.dt.float32r
BF16 = mybir.dt.bfloat16
I32 = mybir.dt.int32
I16 = mybir.dt.int16
U16 = mybir.dt.uint16
ALU = mybir.AluOpType
ACT = mybir.ActivationFunctionType
AX = mybir.AxisListType

P = 128
N = 1250
NT = -(-N // P)
NP = NT * P
TAIL = N - (NT - 1) * P
D = 768
KD = D // P
HALF = D // 2
EDGES = 20000
EP = -(-EDGES // (2 * P))
ET = 2 * EP
H1 = 8
C1 = D // H1
G = 4
EG = 8
E = G * EG
RC = G + E
TW = D + E
ROWS = NP + P
KG = 2
KE = 4
PAIRS = N * KG * KE
GATE_MIN = 1e-6
MIN_TILES = 1
LEAD = 2
LIST = LEAD + PAIRS // P + 1 + MIN_TILES * E + NT
HID = 384
KH = HID // P
RING = 4
SLOPE = 0.2
LN_EPS = 1e-5
NOT_A_NEIGHBOUR = -1e30
PARTS = ((0, 512), (512, 512), (1024, 256))


class Shared:
    pass


def semaphore(nc, s, name):
    s.early.append(nc.alloc_semaphore(name=name))
    return s.early[-1]


def node_features(nc, s, x, w1, edge_src, edge_dst, att1):
    with ExitStack() as ctx:
        def sb(name, shape, dt=F32):
            return ctx.enter_context(nc.sbuf_tensor(name, shape, dt))

        def sem(name):
            return semaphore(nc, s, name)

        xs = sb("xs", [P, NT, D])
        w1_raw = sb("w1_raw", [P, KD, D])
        w1_t = sb("w1_t", [P, KD, D])
        att_col = sb("att_col", [P, 2, KD])
        att_low = sb("att_low", [P, 2, KD, H1])
        att_diag = sb("att_diag", [P, KD, 2, H1])
        wa = sb("wa", [P, KD, 2 * H1])
        stats = sb("stats", [P, NT, 2, 6])
        mv = sb("mv", [P, NT, 2])
        veps = sb("veps", [P, NT])
        rstd = sb("rstd", [P, 4, NT])
        xn = sb("xn", [P, 2, D])
        al_rows = sb("al_rows", [2 * H1, NP])
        edge_i = sb("edge_i", [P, 2, ET], I32)
        dst_hi = sb("dst_hi", [P, ET])
        tile_ids_i = sb("tile_ids_i", [P, 2], I32)
        tile_ids = sb("tile_ids", [P, 2])
        tile_rev = sb("tile_rev", [P, 2])
        block_i = sb("block_i", [P, NT], I32)
        block_lo = s.block_col
        block_hi = sb("block_hi", [P, NT])
        tmax = sb("tmax", [P, 2])
        tmin = sb("tmin", [P, 2])
        hit = sb("hit", [P, 2, NT])
        ge = sb("ge", [P, 2, NT])
        span = sb("span", [P, 2, 2 * NT])
        span_col = sb("span_col", [2 * NT, 1])
        span_row = sb("span_row", [1, 2 * NT])
        span_fix = sb("span_fix", [1, 2 * NT])
        span_i = sb("span_i", [1, 2 * NT], I32)

        ps_x = ctx.enter_context(nc.psum_tensor("ps_x", [P, 2, 2, 512], F32))
        ps_al = ctx.enter_context(nc.psum_tensor("ps_al", [P, 3, 512], F32))
        ps_m = ctx.enter_context(nc.psum_tensor("ps_m", [P, 512], F32))

        x_in, w_in, e_in, a_in = sem("x_in"), sem("w_in"), sem("e_in"), sem("a_in")
        consts, dve_step, act_step = sem("consts"), sem("dve_step"), sem("act_step")
        edge_step, ranged = sem("edge_step"), sem("ranged")
        pe_edges, pe_w1t, w1t_kept = sem("pe_edges"), sem("pe_w1t"), sem("w1t_kept")
        diag_low = sem("diag_low")
        diag, pe_wa, wa_kept = sem("diag"), sem("pe_wa"), sem("wa_kept")
        sqrt_done, normed, pe_xt, xt_kept = sem("sqrt_done"), sem("normed"), sem("pe_xt"), sem("xt_kept")
        pe_al, al_kept, pe_alc, stored = sem("pe_al"), sem("al_kept"), sem("pe_alc"), sem("stored")
        split_hi = sem("split_hi")
        id_done, stat_done = sem("id_done"), sem("stat_done")

        with nc.Block() as block:
            @block.sync
            def _(sp):
                sp.dma_start(edge_i[:, 0], edge_src).then_inc(e_in, 16)
                sp.dma_start(edge_i[:, 1], edge_dst).then_inc(e_in, 16)
                sp.dma_start(xs[:, :, :], x.rearrange("(t p) d -> p t d", p=P)).then_inc(x_in, 16)
                sp.wait_ge(al_kept, 3)
                sp.dma_start(s.al_dram.ap(), al_rows[:, :]).then_inc(stored, 16)
                sp.wait_ge(stored, 16)

            @block.gpsimd
            def _(pool):
                pool.dma_start(att_col[:, :, :], att1).then_inc(a_in, 16)
                nc.gpsimd.memset(s.ident[:, :], 0.0).then_inc(id_done, 1)
                nc.gpsimd.iota(tile_ids_i[:, :], [[P, 2]], base=0, channel_multiplier=1).then_inc(consts, 1)
                nc.gpsimd.iota(block_i[:, :], [[P, NT]], base=0, channel_multiplier=0).then_inc(consts, 1)
                nc.gpsimd.iota(s.column[:, :], [[1, NP]], base=0, channel_multiplier=0).then_inc(consts, 1)
                pool.wait_ge(id_done, 1)
                nc.gpsimd.affine_select(out=s.ident[:, :], in_=s.ident[:, :], compare_op=ALU.not_equal,
                                        fill=1.0, base=0, pattern=[[-1, P]],
                                        channel_multiplier=1).then_inc(consts, 1)
                pool.wait_ge(a_in, 16)
                for a in range(2):
                    nc.gpsimd.affine_select(out=att_low[:, a], compare_op=ALU.is_ge, fill=0.0,
                                            in_=att_col[:, a].unsqueeze(2).broadcast_to([P, KD, H1]),
                                            base=0, pattern=[[P, KD], [-C1, H1]],
                                            channel_multiplier=1).then_inc(diag_low, 1)
                pool.wait_ge(diag_low, 2)
                for a in range(2):
                    nc.gpsimd.affine_select(out=att_diag[:, :, a, :], in_=att_low[:, a], compare_op=ALU.is_ge,
                                            fill=0.0, base=C1 - 1, pattern=[[-P, KD], [C1, H1]],
                                            channel_multiplier=-1).then_inc(diag, 1)

            @block.vector
            def _(dve):
                step = [0]

                def then(ins):
                    step[0] += 1
                    ins.then_inc(dve_step, 1)
                    dve.wait_ge(dve_step, step[0])

                nc.vector.memset(tmax[:, :], -1.0)
                then(nc.vector.memset(tmin[:, :], 2.0 * NP))
                dve.wait_ge(e_in, 32)
                nc.vector.tensor_copy(s.src_f[:, :], edge_i[:, 0])
                then(nc.vector.tensor_copy(s.dst_f[:, :], edge_i[:, 1]))
                nc.vector.tensor_scalar(dst_hi[:, :], s.dst_f[:, :], 0.0, 4.0 * NP, ALU.is_lt, ALU.mult)
                dve.wait_ge(consts, 4)
                nc.vector.tensor_copy(tile_ids[:, :], tile_ids_i[:, :])
                nc.vector.tensor_copy(block_lo[:, :], block_i[:, :])
                then(nc.vector.memset(span[:, :, :], 0.0))
                nc.vector.tensor_scalar(block_hi[:, :], block_lo[:, :], float(P - 1), None, ALU.add)
                nc.vector.tensor_scalar(tile_rev[:, :], tile_ids[:, :], -1.0, float(ET), ALU.mult, ALU.add)
                nc.vector.tensor_scalar(tile_ids[:, :], tile_ids[:, :], 1.0, None, ALU.add)
                nc.vector.tensor_tensor(dst_hi[:, :], dst_hi[:, :], s.dst_f[:, :],
                                        ALU.add).then_inc(edge_step, 1)
                dve.wait_ge(pe_edges, 1)
                rest = ET - P
                nc.vector.tensor_reduce(tmax[:, 0:1], ps_m[:, 0:P], AX.X, ALU.max)
                nc.vector.tensor_reduce(tmax[0:rest, 1:2], ps_m[0:rest, P:2 * P], AX.X, ALU.max)
                nc.vector.tensor_reduce(tmin[:, 0:1], ps_m[:, 2 * P:3 * P], AX.X, ALU.min)
                then(nc.vector.tensor_reduce(tmin[0:rest, 1:2], ps_m[0:rest, 3 * P:4 * P], AX.X, ALU.min))
                for c in range(2):
                    nc.vector.tensor_scalar(ge[:, c], block_lo[:, :], tmax[:, c:c + 1], None, ALU.is_le)
                then(nc.vector.memset(veps[:, :], 0.0))
                for c in range(2):
                    nc.vector.scalar_tensor_tensor(hit[:, c], block_hi[:, :], tmin[:, c:c + 1], ge[:, c],
                                                   ALU.is_ge, ALU.mult)
                then(nc.vector.memset(veps[:, :], 0.0))
                for c in range(2):
                    nc.vector.tensor_scalar(span[:, c, 0:NT], hit[:, c], tile_ids[:, c:c + 1], None, ALU.mult)
                    last = nc.vector.tensor_scalar(span[:, c, NT:2 * NT], hit[:, c], tile_rev[:, c:c + 1],
                                                   None, ALU.mult)
                last.then_inc(edge_step, 1)
                dve.wait_ge(pe_edges, 2)
                nc.vector.tensor_reduce(span_col[:, :], ps_m[0:2 * NT, 0:2 * P], AX.X,
                                        ALU.max).then_inc(edge_step, 1)
                dve.wait_ge(pe_edges, 3)
                then(nc.vector.tensor_scalar(span_row[:, :], ps_m[0:1, 0:2 * NT], 1.0, None, ALU.max))
                then(nc.vector.tensor_scalar(span_fix[:, 0:NT], ps_m[0:1, NT:2 * NT], -1.0, float(ET),
                                             ALU.mult, ALU.add))
                then(nc.vector.tensor_scalar(span_fix[:, NT:2 * NT], span_row[:, 0:NT], -1.0, None, ALU.add))
                then(nc.vector.tensor_tensor(span_fix[:, 0:NT], span_fix[:, 0:NT], span_fix[:, NT:2 * NT],
                                             ALU.min))
                nc.vector.tensor_copy(span_i[:, 0:NT], span_fix[:, 0:NT])
                then(nc.vector.tensor_scalar(span_i[:, NT:2 * NT], span_row[:, 0:NT], 1.0, None, ALU.add))
                nc.vector.tensor_scalar(s.ranges[:, :], span_i[:, :], 1, None, ALU.arith_shift_right)
                for j in range(KD):
                    dve.wait_ge(pe_w1t, j + 1)
                    nc.vector.tensor_copy(w1_t[:, j, :].rearrange("p (b d) -> p b d", b=2),
                                          ps_x[:, j % 2, :, 0:HALF]).then_inc(w1t_kept, 1)
                dve.wait_ge(x_in, 16)
                with dve.Fori(0, NT) as t:
                    for half in range(2):
                        nc.vector.bn_stats(stats[:, bass.ds(t, 1), half, :],
                                           xs[:, bass.ds(t, 1), half * HALF:(half + 1) * HALF]).then_inc(stat_done, 1)
                dve.wait_ge(stat_done, 2 * NT)
                for t in range(NT):
                    last = nc.vector.bn_aggr(mv[:, t, :], stats[:, t, :, :].rearrange("p a b -> p (a b)"))
                then(last)
                nc.vector.tensor_scalar(veps[:, :], mv[:, :, 1], LN_EPS, None, ALU.add).then_inc(stat_done, 1)
                dve.wait_ge(sqrt_done, 1)
                then(nc.vector.reciprocal(rstd[:, 1], rstd[:, 0]))
                then(nc.vector.tensor_tensor(rstd[:, 2], rstd[:, 1], rstd[:, 1], ALU.mult))
                then(nc.vector.tensor_tensor(rstd[:, 2], rstd[:, 2], veps[:, :], ALU.mult))
                then(nc.vector.tensor_scalar(rstd[:, 2], rstd[:, 2], -0.5, 1.5, ALU.mult, ALU.add))
                then(nc.vector.tensor_tensor(rstd[:, 3], rstd[:, 1], rstd[:, 2], ALU.mult))
                with dve.Fori(0, NT // 2) as i:
                    for u in range(2):
                        t = 2 * i + u
                        dve.wait_ge(xt_kept, t + 1)
                        nc.vector.tensor_scalar(xn[:, u, :], xs[:, bass.ds(t, 1), :].rearrange("p o d -> p (o d)"),
                                                mv[:, bass.ds(t, 1), 0:1].rearrange("p o d -> p (o d)"),
                                                rstd[:, 3, bass.ds(t, 1)], ALU.subtract, ALU.mult).then_inc(normed, 1)
                dve.wait_ge(split_hi, KD)
                for k in range(KD):
                    nc.vector.tensor_tensor(s.w1_lo[:, k, :], w1_raw[:, k, :], s.w1_hi[:, k, :].bitcast(F32),
                                            ALU.subtract)
                dve.wait_ge(pe_alc, 1)
                nc.vector.tensor_copy(s.al_col[:, :, :], ps_m[:, 0:NT * 16].rearrange("p (t c) -> p t c", c=16))

            @block.scalar
            def _(act):
                act.dma_start(w1_raw[:, :, :], w1.rearrange("(k p) c -> p k c", p=P)).then_inc(w_in, 16)
                act.sem_inc(xt_kept, 2)
                act.wait_ge(w_in, 16)
                for k in range(KD):
                    nc.scalar.activation(s.w1_hi[:, k, :], w1_raw[:, k, :], ACT.Copy).then_inc(split_hi, 1)
                act.wait_ge(pe_wa, 1)
                nc.scalar.activation(wa[:, :, :], ps_m[:, 0:KD * 16].rearrange("p (k c) -> p k c", c=16),
                                     ACT.Copy).then_inc(wa_kept, 1)
                act.wait_ge(stat_done, 2 * NT + 1)
                nc.scalar.activation(rstd[:, 0], veps[:, :], ACT.Sqrt).then_inc(sqrt_done, 1)
                with act.Fori(0, NT // 2) as i:
                    for u in range(2):
                        t = 2 * i + u
                        act.wait_ge(pe_xt, t + 1)
                        nc.scalar.activation(
                            s.x_t[:, bass.ds(t, 1), :, :].rearrange("p o (b k) n -> p (o b) (k n)", b=2),
                            ps_x[:, u, :, 0:HALF], ACT.Copy).then_inc(xt_kept, 1)
                for c, (at, width) in enumerate(PARTS):
                    act.wait_ge(pe_al, c + 1)
                    nc.scalar.activation(al_rows[:, at:at + width], ps_al[0:16, c, 0:width],
                                         ACT.Copy).then_inc(al_kept, 1)

            @block.tensor
            def _(pe):
                pe.wait_ge(consts, 4)
                pe.wait_ge(edge_step, 1)
                for c, src in enumerate((s.dst_f, dst_hi)):
                    nc.tensor.transpose(ps_m[:, 2 * c * P:(2 * c + 1) * P], src[:, 0:P], s.ident[:, :])
                    last = nc.tensor.transpose(ps_m[0:ET - P, (2 * c + 1) * P:(2 * c + 2) * P], src[:, P:ET],
                                               s.ident[:, :])
                last.then_inc(pe_edges, 1)
                pe.wait_ge(edge_step, 2)
                for c in range(2):
                    last = nc.tensor.transpose(ps_m[0:2 * NT, c * P:(c + 1) * P], span[:, c, :], s.ident[:, :])
                last.then_inc(pe_edges, 1)
                pe.wait_ge(edge_step, 3)
                nc.tensor.transpose(ps_m[0:1, 0:2 * NT], span_col[:, :],
                                    s.ident[0:2 * NT, 0:2 * NT]).then_inc(pe_edges, 1)
                pe.wait_ge(w_in, 16)
                for j in range(KD):
                    if j >= 2:
                        pe.wait_ge(w1t_kept, j - 1)
                    for k in range(KD):
                        last = nc.tensor.transpose(ps_x[:, j % 2, k // 3, (k % 3) * P:(k % 3 + 1) * P],
                                                   w1_raw[:, k, j * P:(j + 1) * P], s.ident[:, :])
                    last.then_inc(pe_w1t, 1)
                pe.wait_ge(w1t_kept, KD)
                pe.wait_ge(diag, 2)
                for k in range(KD):
                    for j in range(KD):
                        last = nc.tensor.matmul(ps_m[:, k * 16:(k + 1) * 16], w1_t[:, j, k * P:(k + 1) * P],
                                                att_diag[:, j, :, :].rearrange("p s h -> p (s h)"),
                                                start=(j == 0), stop=(j == KD - 1))
                last.then_inc(pe_wa, 1)
                with pe.Fori(0, NT // 2) as i:
                    for u in range(2):
                        t = 2 * i + u
                        pe.wait_ge(normed, t + 1)
                        pe.wait_ge(xt_kept, t + 1)
                        for k in range(KD):
                            last = nc.tensor.transpose(ps_x[:, u, k // 3, (k % 3) * P:(k % 3 + 1) * P],
                                                       xn[:, u, k * P:(k + 1) * P], s.ident[:, :])
                        last.then_inc(pe_xt, 1)
                pe.wait_ge(wa_kept, 1)
                pe.wait_ge(xt_kept, NT + 2)
                for c, (at, width) in enumerate(PARTS):
                    for k in range(KD):
                        last = nc.tensor.matmul(ps_al[0:16, c, 0:width], wa[:, k, :],
                                                s.x_t[:, at // P:(at + width) // P, k, :],
                                                start=(k == 0), stop=(k == KD - 1))
                    last.then_inc(pe_al, 1)
                pe.wait_ge(al_kept, 3)
                for t in range(NT):
                    last = nc.tensor.transpose(ps_m[:, t * 16:(t + 1) * 16], al_rows[:, t * P:(t + 1) * P],
                                               s.ident[0:16, 0:16])
                last.then_inc(pe_alc, 1)


def transform_and_count(nc, s):
    with ExitStack() as ctx:
        def sb(name, shape, dt=F32):
            return ctx.enter_context(nc.sbuf_tensor(name, shape, dt))

        def sem(name):
            return ctx.enter_context(nc.semaphore(name))

        HOTS = 2

        al_src = sb("al_src", [P, H1, NP])
        xt_hi = sb("xt_hi", [P, 2, D], F32R)
        xt_lo = sb("xt_lo", [P, 2, D], F32R)
        counts = sb("counts", [P, NP])
        mask = sb("mask", [P, 2, NP], BF16)
        junk = sb("junk", [P, 2, NP], BF16)
        one_src = sb("one_src", [P, HOTS, 2, NP], BF16)
        one_dst = sb("one_dst", [P, HOTS, 2, P], BF16)
        dst_rel = sb("dst_rel", [P, 2, ET])
        zeros = sb("zeros", [P, P], BF16)
        best = sb("best", [P, 2, H1])
        ps_h = ctx.enter_context(nc.psum_tensor("ps_h", [P, 2, 512], F32))
        ps_c = ctx.enter_context(nc.psum_tensor("ps_c", [P, 3, 512], F32))
        ps_t = ctx.enter_context(nc.psum_tensor("ps_t", [P, 3, 512], F32))

        al_in, zeroed, ones_set = sem("al_in"), sem("zeroed"), sem("ones_set")
        xhi_made, xlo_made, h_summed, h_kept = sem("xhi_made"), sem("xlo_made"), sem("h_summed"), sem("h_kept")
        onehot_made, onehot_used, rel_made = sem("onehot_made"), sem("onehot_used"), sem("rel_made")
        counted, counts_kept, turned, turned_kept = sem("counted"), sem("counts_kept"), sem("turned"), sem("turned_kept")
        mask_made, maxed, best_kept = sem("mask_made"), sem("maxed"), sem("best_kept")
        mask_out = [sem("mask_out0"), sem("mask_out1")]

        with nc.Block() as block:
            @block.sync
            def _(sp):
                sp.dma_start(al_src[:, :, :].rearrange("p h n -> p (h n)"),
                             s.al_dram.ap()[0:H1, :].rearrange("(o h) n -> o (h n)", o=1)
                             .broadcast_to([P, H1 * NP])).then_inc(al_in, 16)
                with sp.Fori(0, NT // 2) as i:
                    for u in range(2):
                        t = 2 * i + u
                        sp.wait_ge(mask_made, t + 2)
                        sp.dma_start(s.mask_dram.ap()[bass.ds(t, 1), :, :].rearrange("o p n -> (o p) n"),
                                     mask[:, u, :]).then_inc(mask_out[u], 16)
                for u in range(2):
                    sp.wait_ge(mask_out[u], 16 * (NT // 2))

            @block.gpsimd
            def _(pool):
                nc.gpsimd.memset(s.h_ext[:, :, :, C1:C1 + 1], 1.0).then_inc(ones_set, 1)
                with pool.Fori(0, NT // 2) as i:
                    for u in range(2):
                        t = 2 * i + u
                        pool.wait_ge(xhi_made, t + 1)
                        nc.gpsimd.tensor_tensor(
                            xt_lo[:, u, :], s.x_t[:, bass.ds(t, 1), :, :].rearrange("p o k n -> p (o k n)"),
                            xt_hi[:, u, :].bitcast(F32), ALU.subtract).then_inc(xlo_made, 1)

            @block.scalar
            def _(act):
                act.sem_inc(h_kept, 2)
                act.sem_inc(turned_kept, 1)
                act.sem_inc(counts_kept, 1)
                with act.Fori(0, NT // 2) as i:
                    for u in range(2):
                        t = 2 * i + u
                        act.wait_ge(h_kept, t + 2)
                        nc.scalar.activation(
                            xt_hi[:, u, :], s.x_t[:, bass.ds(t, 1), :, :].rearrange("p o k n -> p (o k n)"),
                            ACT.Copy).then_inc(xhi_made, 1)
                        act.wait_ge(counted, t + 1)
                        act.wait_ge(mask_made, t + 1)
                        act.wait_ge(turned_kept, t + 1)
                        nc.scalar.activation(counts[:, 0:1024], ps_c[:, 0:2, :].rearrange("p a n -> p (a n)"),
                                             ACT.Copy)
                        nc.scalar.activation(counts[:, 1024:NP], ps_c[:, 2, 0:256], ACT.Copy).then_inc(counts_kept, 1)
                        act.wait_ge(h_summed, t + 1)
                        for half in range(2):
                            last = nc.scalar.activation(
                                s.h_ext[:, bass.ds(t, 1), 4 * half:4 * half + 4, 0:C1]
                                .rearrange("p o h c -> p (o h) c"),
                                ps_h[:, half, 0:HALF].rearrange("p (h c) -> p h c", c=C1), ACT.Copy)
                        last.then_inc(h_kept, 1)
                        act.wait_ge(turned, t + 1)
                        nc.scalar.activation(
                            s.count[:, 0:8, bass.ds(t * P, P)],
                            ps_t[:, 0:2, :].rearrange("p a (b n) -> p (a b) n", n=P), ACT.Copy)
                        nc.scalar.activation(
                            s.count[:, 8:NT, bass.ds(t * P, P)],
                            ps_t[:, 2, 0:2 * P].rearrange("p (b n) -> p b n", n=P),
                            ACT.Copy).then_inc(turned_kept, 1)

            @block.vector
            def _(dve):
                nc.vector.memset(zeros[:, :], 0.0).then_inc(zeroed, 1)
                dve.sem_inc(mask_made, 1)
                made = dve.alloc_register("made_dve")
                dve.reg_mov(made, 0)
                freed = dve.alloc_register("freed")
                dve.reg_mov(freed, 0)

                def one_hots(t, u):
                    nc.vector.tensor_scalar(dst_rel[:, u, :], s.dst_f[:, :], s.block_col[:, bass.ds(t, 1)],
                                            None, ALU.subtract).then_inc(rel_made, 1)
                    dve.wait_ge(rel_made, t + 1)
                    first = dve.value_load(s.ranges[0:1, bass.ds(t, 1)], min_val=0, max_val=EP - 1)
                    end = dve.value_load(s.ranges[0:1, bass.ds(t + NT, 1)], min_val=1, max_val=EP)
                    with dve.Fori(first, end) as e:
                        m = dve.snap(made)
                        dve.wait_ge(onehot_used, m + 1)
                        for q in range(2):
                            nc.vector.tensor_scalar(one_src[:, m % HOTS, q, :], s.column[:, :],
                                                    s.src_f[:, bass.ds(2 * e + q, 1)], None, ALU.is_equal)
                            last = nc.vector.tensor_scalar(one_dst[:, m % HOTS, q, :], s.column[:, 0:P],
                                                           dst_rel[:, u, bass.ds(2 * e + q, 1)], None,
                                                           ALU.is_equal)
                        last.then_inc(onehot_made, 1)
                        dve.reg_add(made, made, 1)

                def largest(t, i, u, first=False):
                    dve.wait_ge(counts_kept, t + 2)
                    if not first:
                        dve.wait_ge(mask_out[u], 16 * i)
                    nc.vector.tensor_scalar(mask[:, u, :], counts[:, :], 0.0, NOT_A_NEIGHBOUR,
                                            ALU.is_equal, ALU.mult).then_inc(mask_made, 1)
                    dve.wait_ge(al_in, 16)
                    dve.wait_ge(mask_made, t + 2)
                    for h in range(H1):
                        if h >= 2:
                            dve.reg_add(freed, freed, 1)
                            now = dve.snap(freed)
                            dve.wait_ge(al_in, 16)
                            dve.wait_ge(maxed, now)
                        nc.vector.tensor_tensor_reduce(
                            junk[:, h % 2, :], mask[:, u, :], al_src[:, h, :], 1.0,
                            2.0 * NOT_A_NEIGHBOUR, ALU.add, ALU.max, best[:, u, h:h + 1]).then_inc(maxed, 1)
                    dve.reg_add(freed, freed, 2)
                    dve.wait_ge(maxed, (t + 1) * H1)
                    nc.vector.tensor_copy(s.al_max[:, bass.ds(t, 1), :].rearrange("p o h -> p (o h)"),
                                          best[:, u, :]).then_inc(best_kept, 1)
                    dve.wait_ge(best_kept, t + 1)

                one_hots(0, 0)
                one_hots(1, 1)
                largest(0, 0, 0, first=True)
                one_hots(2, 0)
                largest(1, 0, 1, first=True)
                with dve.Fori(1, NT // 2 - 1) as i:
                    one_hots(2 * i + 1, 1)
                    largest(2 * i, i, 0)
                    one_hots(2 * i + 2, 0)
                    largest(2 * i + 1, i, 1)
                one_hots(NT - 1, 1)
                largest(NT - 2, NT // 2 - 1, 0)
                largest(NT - 1, NT // 2 - 1, 1)

            @block.tensor
            def _(pe):
                pe.sem_inc(onehot_used, HOTS)
                pe.wait_ge(zeroed, 1)
                made = pe.alloc_register("made_pe")
                pe.reg_mov(made, 0)
                with pe.Fori(0, NT // 2) as i:
                    for u in range(2):
                        t = 2 * i + u
                        first = pe.value_load(s.ranges[0:1, bass.ds(t, 1)], min_val=0, max_val=EP - 1)
                        end = pe.value_load(s.ranges[0:1, bass.ds(t + NT, 1)], min_val=1, max_val=EP)
                        pe.wait_ge(counts_kept, t + 1)
                        for c, (at, width) in enumerate(PARTS):
                            nc.tensor.matmul(ps_c[:, c, 0:width], zeros[:, :], zeros[:, 0:1].broadcast_to([P, width]),
                                             start=True, stop=False)
                        with pe.Fori(first, end) as e:
                            m = pe.snap(made)
                            pe.wait_ge(onehot_made, m + 1)
                            for q in range(2):
                                for c, (at, width) in enumerate(PARTS):
                                    last = nc.tensor.matmul(ps_c[:, c, 0:width], one_dst[:, m % HOTS, q, :],
                                                            one_src[:, m % HOTS, q, at:at + width],
                                                            start=False, stop=False)
                            last.then_inc(onehot_used, 1)
                            pe.reg_add(made, made, 1)
                        for c, (at, width) in enumerate(PARTS):
                            last = nc.tensor.matmul(ps_c[:, c, 0:width], zeros[:, :], zeros[:, 0:1].broadcast_to([P, width]),
                                                    start=False, stop=True)
                        last.then_inc(counted, 1)
                        pe.wait_ge(xlo_made, t + 1)
                        pe.wait_ge(h_kept, t + 2)
                        for half in range(2):
                            at = half * HALF
                            for k in range(KD):
                                hi, lo = (w[:, u, k * P:(k + 1) * P] for w in (xt_hi, xt_lo))
                                for n, (a, b) in enumerate(((hi, s.w1_hi), (hi, s.w1_lo), (lo, s.w1_hi))):
                                    last = nc.tensor.matmul(ps_h[:, half, 0:HALF], a, b[:, k, at:at + HALF],
                                                            start=(k == 0 and n == 0),
                                                            stop=(k == KD - 1 and n == 2))
                        last.then_inc(h_summed, 1)
                        pe.wait_ge(counts_kept, t + 2)
                        pe.wait_ge(turned_kept, t + 1)
                        for b in range(NT):
                            last = nc.tensor.transpose(ps_t[:, b // 4, (b % 4) * P:(b % 4 + 1) * P],
                                                       counts[:, b * P:(b + 1) * P], s.ident[:, :])
                        last.then_inc(turned, 1)

def attend_by_head(nc, s, bias1):
    with ExitStack() as ctx:
        def sb(name, shape, dt=F32):
            return ctx.enter_context(nc.sbuf_tensor(name, shape, dt))

        def sem(name):
            return ctx.enter_context(nc.semaphore(name))

        rel = sb("rel", [P, NT, 2, H1])
        top = sb("top", [P, 2, NT, H1])
        src_small = sb("src_small", [P, NT, H1])
        rel_rows = sb("rel_rows", [2 * H1, NP])
        bias_col = sb("bias_col", [C1, H1])
        bias_now = sb("bias_now", [C1, 1])
        h_head = sb("h_head", [P, 2, NT, C1 + 1])
        steep = sb("steep", [P, 2, NP])
        flat = sb("flat", [P, 2, NP])
        ex = sb("ex", [P, 2, NP])
        ey = sb("ey", [P, 2, NP])
        prob = sb("prob", [P, 2, NP])
        out_t = sb("out_t", [C1 + 1, 2, NP])
        scale_t = sb("scale_t", [C1, 2, NP])
        neg_t = sb("neg_t", [C1, NP])
        z_rows = sb("z_rows", [NT, 2, N // NT])

        ps_o = [ctx.enter_context(nc.psum_tensor(f"ps_o{u}", [P, 3, 512], F32)) for u in range(2)]
        ps_r = ctx.enter_context(nc.psum_tensor("ps_r", [P, 512], F32))

        step, rel_made, rel_turned, rel_kept, rel_out = (sem("c_step"), sem("rel_made_2"), sem("rel_turned"),
                                                         sem("rel_kept"), sem("rel_out"))
        rows_in = [sem("rows_in0"), sem("rows_in1")]
        head_set, exped, joined, made, mixed = (sem("head_set"), sem("exped"), sem("joined"), sem("made"),
                                                sem("mixed"))
        out_kept, z_out, z_in, z_done, zi_out = (sem("out_kept"), sem("z_out"), sem("z_in"), sem("z_done"),
                                                 sem("zi_out"))
        scale_in = [sem("scale_in0"), sem("scale_in1")]
        neg_made, neg_exped, elued = sem("neg_made"), sem("neg_exped"), sem("elued")
        pool_step, bias_in, head_mixed = sem("pool_step"), sem("bias_in"), sem("head_mixed")
        count_out = sem("count_out")
        WID = [512, 512, N - 1024]

        with nc.Block() as block:
            @block.sync
            def _(sp):
                sp.dma_start(bias_col[:, :], bias1).then_inc(bias_in, 16)
                sp.dma_start(s.count_dram.ap(), s.count[:, :, :]).then_inc(count_out, 16)
                sp.wait_ge(rel_kept, 3)
                sp.dma_start(s.rel_dram.ap(), rel_rows[:, :]).then_inc(rel_out, 16)
                sp.wait_ge(rel_out, 16)

                def load_rows(h, u):
                    sp.dma_start(steep[:, u, :], s.rel_dram.ap()[bass.ds(h, 1), :].broadcast_to([P, NP])) \
                      .then_inc(rows_in[u], 16)
                    sp.dma_start(flat[:, u, :], s.rel_dram.ap()[bass.ds(h + H1, 1), :].broadcast_to([P, NP])) \
                      .then_inc(rows_in[u], 16)

                def reciprocal_sums(h, u):
                    sp.wait_ge(out_kept, h + 1)
                    sp.dma_start(s.z_dram.ap()[bass.ds(h, 1), :], out_t[C1:C1 + 1, u, 0:N]).then_inc(z_out, 16)
                    sp.wait_ge(z_out, 16 * h + 16)
                    sp.dma_start(z_rows[:, u, :], s.z_dram.ap()[bass.ds(h, 1), :]
                                 .rearrange("o (a b) -> (o a) b", a=NT)).then_inc(z_in, 16)
                    sp.wait_ge(z_done, 2 * h + 2)
                    sp.dma_start(s.zi_dram.ap()[bass.ds(h, 1), :].rearrange("o (a b) -> (o a) b", a=NT),
                                 z_rows[:, u, :]).then_inc(zi_out, 16)
                    sp.wait_ge(zi_out, 16 * h + 16)
                    sp.dma_start(scale_t[:, u, 0:N], s.zi_dram.ap()[bass.ds(h, 1), :].broadcast_to([C1, N])) \
                      .then_inc(scale_in[u], 16)

                load_rows(0, 0)
                load_rows(1, 1)
                reciprocal_sums(0, 0)
                with sp.Fori(0, H1 // 2 - 1) as i:
                    for u in range(2):
                        h = 2 * i + u
                        load_rows(h + 2, u)
                        sp.wait_ge(elued, h + 1)
                        reciprocal_sums(h + 1, 1 - u)
                reciprocal_sums(H1 - 1, 1)
                for u in range(2):
                    sp.wait_ge(scale_in[u], 16 * (H1 // 2))
                sp.wait_ge(count_out, 16)

            @block.gpsimd
            def _(pool):
                def stage_head(h, u):
                    nc.gpsimd.tensor_copy(h_head[:, u], s.h_ext[:, :, bass.ds(h, 1), :]
                                          .rearrange("p t o c -> p (t o) c")).then_inc(head_set, 1)

                steps = pool.alloc_register("pool_steps")
                pool.reg_mov(steps, 0)

                def then(ins):
                    ins.then_inc(pool_step, 1)
                    pool.reg_add(steps, steps, 1)
                    done = pool.snap(steps)
                    pool.wait_ge(bias_in, 16)
                    pool.wait_ge(pool_step, done)

                def finish(h, i, u):
                    pool.wait_ge(scale_in[u], 16 * i + 16)
                    then(nc.gpsimd.tensor_copy(bias_now[:, :], bias_col[:, bass.ds(h, 1)]))
                    then(nc.gpsimd.tensor_tensor(out_t[0:C1, u, 0:N], out_t[0:C1, u, 0:N], scale_t[:, u, 0:N],
                                                 ALU.mult))
                    then(nc.gpsimd.tensor_scalar(out_t[0:C1, u, 0:N], out_t[0:C1, u, 0:N], bias_now[:, 0:1],
                                                 None, ALU.add))
                    nc.gpsimd.tensor_scalar(neg_t[:, 0:N], out_t[0:C1, u, 0:N], 0.0, None,
                                            ALU.min).then_inc(neg_made, 1)
                    then(nc.gpsimd.tensor_scalar(scale_t[:, u, 0:N], out_t[0:C1, u, 0:N], 0.0, -1.0,
                                                 ALU.max, ALU.add))
                    pool.wait_ge(neg_exped, h + 1)
                    nc.gpsimd.tensor_tensor(s.g_t[:, bass.ds(h, 1), 0:N].rearrange("p o n -> p (o n)"),
                                            scale_t[:, u, 0:N], neg_t[:, 0:N], ALU.add).then_inc(elued, 1)
                    pool.wait_ge(elued, h + 2)

                nc.gpsimd.memset(s.g_t[:, :, N:NP], 0.0)
                pool.sem_inc(elued, 1)
                pool.wait_ge(bias_in, 16)
                stage_head(0, 0)
                stage_head(1, 1)
                with pool.Fori(0, H1 // 2 - 1) as i:
                    for u in range(2):
                        h = 2 * i + u
                        pool.wait_ge(mixed, (h + 1) * NT + 2)
                        stage_head(h + 2, u)
                        finish(h, i, u)

            @block.scalar
            def _(act):
                act.wait_ge(rel_turned, 1)
                for c, (at, width) in enumerate(PARTS):
                    act.wait_ge(rel_turned, c + 1)
                    nc.scalar.activation(rel_rows[:, at:at + width], ps_r[0:16, 0:width],
                                         ACT.Copy).then_inc(rel_kept, 1)
                act.wait_ge(step, 1)

                def keep_out(h, u):
                    act.wait_ge(mixed, (h + 1) * NT + 2)
                    if not (isinstance(h, int) and h == 0):
                        act.wait_ge(elued, h)
                    nc.scalar.activation(out_t[:, u, 0:1024].rearrange("p (a n) -> p a n", a=2),
                                         ps_o[u][0:C1 + 1, 0:2, :], ACT.Copy)
                    nc.scalar.activation(out_t[:, u, 1024:N], ps_o[u][0:C1 + 1, 2, 0:WID[2]],
                                         ACT.Copy).then_inc(out_kept, 1)

                def exp_negative(h):
                    act.wait_ge(neg_made, h + 1)
                    nc.scalar.activation(neg_t[:, 0:N], neg_t[:, 0:N], ACT.Exp).then_inc(neg_exped, 1)

                def exps(h, i, u, first):
                    act.wait_ge(rows_in[u], 32 * i + 32)
                    for t in range(NT):
                        act.wait_ge(joined, h * NT + t + 1)
                        nc.scalar.activation(ex[:, t % 2, 0:N], steep[:, u, 0:N], ACT.Exp,
                                             bias=s.al_col[:, t, bass.ds(h, 1)])
                        nc.scalar.activation(ey[:, t % 2, 0:N], flat[:, u, 0:N], ACT.Exp,
                                             bias=src_small[:, t, bass.ds(h, 1)]).then_inc(exped, 1)
                        if t == 2 and not first:
                            keep_out(h - 1, 1 - u)

                def head(h, i, u, first=False, second=False):
                    exps(h, i, u, first)
                    if not first and not second:
                        exp_negative(h - 2)

                head(0, 0, 0, first=True)
                head(1, 0, 1, second=True)
                with act.Fori(1, H1 // 2) as i:
                    for u in range(2):
                        head(2 * i + u, i, u)
                keep_out(H1 - 1, 1)
                exp_negative(H1 - 2)
                exp_negative(H1 - 1)

            @block.vector
            def _(dve):
                n = [0]

                def then(ins):
                    n[0] += 1
                    ins.then_inc(rel_made, 1)
                    dve.wait_ge(rel_made, n[0])

                src, dst = s.al_col[:, :, 0:H1], s.al_col[:, :, H1:2 * H1]
                then(nc.vector.tensor_tensor(top[:, 0], s.al_max[:, :, :], dst, ALU.add))
                then(nc.vector.scalar_tensor_tensor(top[:, 1], top[:, 0], SLOPE, top[:, 0], ALU.mult, ALU.max))
                then(nc.vector.scalar_tensor_tensor(top[:, 1], s.al_max[:, :, :], 0.5 * NOT_A_NEIGHBOUR, top[:, 1],
                                                    ALU.is_gt, ALU.mult))
                nc.vector.tensor_tensor(rel[:, :, 0, :], dst, top[:, 1], ALU.subtract)
                nc.vector.scalar_tensor_tensor(rel[:, :, 1, :], dst, SLOPE, top[:, 1], ALU.mult, ALU.subtract)
                nc.vector.tensor_scalar(src_small[:, :, :], src, SLOPE, None, ALU.mult).then_inc(step, 1)
                dve.wait_ge(step, 1)
                dve.sem_inc(joined, 2)

                def invert_sums(h, u):
                    dve.wait_ge(z_in, 16 * h + 16)
                    nc.vector.tensor_scalar(z_rows[:, u, :], z_rows[:, u, :], 1e-16, None,
                                            ALU.add).then_inc(z_done, 1)
                    dve.wait_ge(z_done, 2 * h + 1)
                    nc.vector.reciprocal(z_rows[:, u, :], z_rows[:, u, :]).then_inc(z_done, 1)

                def head(h, u, first=False):
                    for t in range(NT):
                        dve.wait_ge(exped, h * NT + t + 1)
                        nc.vector.scalar_tensor_tensor(ex[:, t % 2, 0:N], ey[:, t % 2, 0:N], 1.0,
                                                       ex[:, t % 2, 0:N], ALU.min, ALU.max).then_inc(step, 1)
                        dve.wait_ge(step, h * NT + t + 2)
                        dve.wait_ge(mixed, h * NT + t + 1)
                        nc.vector.scalar_tensor_tensor(prob[:, t % 2, 0:N], ex[:, t % 2, 0:N], 1.0,
                                                       s.count[:, t, 0:N], ALU.min,
                                                       ALU.mult).then_inc(joined, 1)
                        if t == 6 and not first:
                            invert_sums(h - 1, 1 - u)

                head(0, 0, first=True)
                head(1, 1)
                with dve.Fori(1, H1 // 2) as i:
                    for u in range(2):
                        head(2 * i + u, u)

                def finish(h, u):
                    v, e = out_t[0:C1, u, 0:N], neg_t[:, 0:N]
                    dve.wait_ge(scale_in[u], 16 * (H1 // 2))
                    then(nc.vector.tensor_tensor(v, v, scale_t[:, u, 0:N], ALU.mult))
                    then(nc.vector.tensor_scalar(v, v, bias_col[:, h:h + 1], None, ALU.add))
                    dve.wait_ge(elued, h + 1)
                    nc.vector.tensor_scalar(e, v, 0.0, None, ALU.min).then_inc(neg_made, 1)
                    dve.wait_ge(neg_exped, h + 1)
                    nc.vector.scalar_tensor_tensor(s.g_t[:, h, 0:N], e, -1.0, v, ALU.add,
                                                   ALU.max).then_inc(elued, 1)

                dve.wait_ge(bias_in, 16)
                finish(H1 - 2, 0)
                invert_sums(H1 - 1, 1)
                finish(H1 - 1, 1)

            @block.tensor
            def _(pe):
                pe.sem_inc(mixed, 2)
                pe.wait_ge(step, 1)
                for c, (at, width) in enumerate(PARTS):
                    if c:
                        pe.wait_ge(rel_kept, c)
                    for t in range(at // P, (at + width) // P):
                        last = nc.tensor.transpose(ps_r[0:16, t * P - at:(t + 1) * P - at],
                                                   rel[:, t, :, :].rearrange("p a h -> p (a h)"), s.ident[:, :])
                    last.then_inc(rel_turned, 1)

                def head(h, u, early=False):
                    pe.wait_ge(head_set, h + 1)
                    if not early:
                        pe.wait_ge(out_kept, h - 1)
                    for t in range(NT):
                        pe.wait_ge(joined, h * NT + t + 3)
                        for c in range(3):
                            last = nc.tensor.matmul(ps_o[u][0:C1 + 1, c, 0:WID[c]], h_head[:, u, t, :],
                                                    prob[:, t % 2, 512 * c:512 * c + WID[c]],
                                                    start=(t == 0), stop=(t == NT - 1))
                        last.then_inc(mixed, 1)

                head(0, 0, early=True)
                head(1, 1, early=True)
                with pe.Fori(1, H1 // 2) as i:
                    for u in range(2):
                        head(2 * i + u, u)

def transform_again(nc, s, w2, att2):
    with ExitStack() as ctx:
        def sb(name, shape, dt=F32):
            return ctx.enter_context(nc.sbuf_tensor(name, shape, dt))

        def sem(name):
            return ctx.enter_context(nc.semaphore(name))

        RAW = 4
        w2_raw = sb("w2_raw", [C1, RAW, D])
        w2_hi = sb("w2_hi", [C1, H1, D], F32R)
        w2_lo = sb("w2_lo", [C1, H1, D], F32R)
        g_hi = sb("g_hi", [C1, 2, H1, P], F32R)
        g_lo = sb("g_lo", [C1, 2, H1, P], F32R)
        att = sb("att", [P, 2, D])
        junk = sb("junk2", [P, 2, 2, HALF], BF16)
        al_now = sb("al_now", [P, 2, 2])
        ps = [ctx.enter_context(nc.psum_tensor(f"ps_h2{u}", [P, 2, 512], F32)) for u in range(2)]

        w_in = [sem(f"w2_in{q}") for q in range(RAW)]
        a_in, w_hi, w_lo, ones_set = sem("a2_in"), sem("w2_hi_made"), sem("w2_lo_made"), sem("ones2_set")
        ghi_made, glo_made, summed, h_hi, h_lo, al_made, al_kept = (
            sem("ghi_made"), sem("glo_made"), sem("h2_summed"), sem("h2_hi_made"), sem("h2_lo_made"),
            sem("al2_made"), sem("al2_kept"))

        with nc.Block() as block:
            @block.sync
            def _(sp):
                for k in range(H1):
                    if k >= RAW:
                        sp.wait_ge(w_lo, k - RAW + 1)
                    sp.dma_start(w2_raw[:, k % RAW, :], w2[k * C1:(k + 1) * C1, :]).then_inc(w_in[k % RAW], 16)
                sp.dma_start(att[:, :, :].rearrange("p a d -> p (a d)"), att2.broadcast_to([P, 2 * D])) \
                  .then_inc(a_in, 16)

            @block.gpsimd
            def _(pool):
                nc.gpsimd.memset(s.h2_hi[:, :, D:D + 4].bitcast(F32), 0.0).then_inc(ones_set, 1)
                nc.gpsimd.memset(s.h2_lo[:, :, D:D + 4].bitcast(F32), 0.0)
                pool.wait_ge(ones_set, 1)
                nc.gpsimd.memset(s.h2_hi[:, :, D:D + 1].bitcast(F32), 1.0).then_inc(ones_set, 1)
                with pool.Fori(0, NT // 2) as i:
                    for u in range(2):
                        t = 2 * i + u
                        pool.wait_ge(ghi_made, t + 1)
                        nc.gpsimd.tensor_tensor(g_lo[:, u], s.g_t[:, :, bass.ds(t * P, P)],
                                                g_hi[:, u].bitcast(F32), ALU.subtract).then_inc(glo_made, 1)
                pool.wait_ge(ones_set, 2)

            @block.scalar
            def _(act):
                def split_g(t, u):
                    nc.scalar.activation(g_hi[:, u], s.g_t[:, :, bass.ds(t * P, P)], ACT.Copy).then_inc(ghi_made, 1)

                split_g(0, 0)
                for k in range(H1):
                    act.wait_ge(w_in[k % RAW], 16 * (k // RAW + 1))
                    nc.scalar.activation(w2_hi[:, k, :], w2_raw[:, k % RAW, :], ACT.Copy).then_inc(w_hi, 1)
                act.sem_inc(h_hi, 2)
                split_g(1, 1)
                with act.Fori(0, NT // 2) as i:
                    for u in range(2):
                        t = 2 * i + u
                        act.wait_ge(summed, t + 1)
                        nc.scalar.activation(
                            s.h2_hi[:, bass.ds(t, 1), 0:D].rearrange("p o (b d) -> p (o b) d", b=2),
                            ps[u][:, :, 0:HALF], ACT.Copy).then_inc(h_hi, 1)
                        nc.scalar.activation(g_hi[:, u], s.g_t[:, :, bass.ds((t + 2) % NT * P, P)],
                                             ACT.Copy).then_inc(ghi_made, 1)

            @block.vector
            def _(dve):
                for k in range(H1):
                    dve.wait_ge(w_hi, k + 1)
                    nc.vector.tensor_tensor(w2_lo[:, k, :], w2_raw[:, k % RAW, :], w2_hi[:, k, :].bitcast(F32),
                                            ALU.subtract).then_inc(w_lo, 1)
                dve.wait_ge(a_in, 16)
                dve.sem_inc(al_made, 2)
                with dve.Fori(0, NT // 2) as i:
                    for u in range(2):
                        t = 2 * i + u
                        dve.wait_ge(h_hi, t + 3)
                        out = s.h2_lo[:, bass.ds(t, 1), 0:D].rearrange("p o (b d) -> p (o b) d", b=2)
                        hi = s.h2_hi[:, bass.ds(t, 1), 0:D].bitcast(F32).rearrange("p o (b d) -> p (o b) d", b=2)
                        nc.vector.tensor_tensor(out, ps[u][:, :, 0:HALF], hi, ALU.subtract)
                        for a in range(2):
                            last = nc.vector.scalar_tensor_tensor(
                                junk[:, a], ps[u][:, :, 0:HALF], 1.0,
                                att[:, a, :].rearrange("p (b d) -> p b d", b=2),
                                ALU.mult, ALU.mult, accum_out=al_now[:, u, a:a + 1])
                        last.then_inc(al_made, 1)
                        dve.wait_ge(al_made, t + 3)
                        nc.vector.tensor_copy(s.al2_col[:, bass.ds(t, 1), :].rearrange("p o a -> p (o a)"),
                                              al_now[:, u, :]).then_inc(al_kept, 1)
                        dve.wait_ge(al_kept, t + 1)

            @block.tensor
            def _(pe):
                with pe.Fori(0, NT // 2) as i:
                    for u in range(2):
                        t = 2 * i + u
                        pe.wait_ge(glo_made, t + 1)
                        pe.wait_ge(al_made, 2 * i + 2)
                        for half in range(2):
                            at = half * HALF
                            for k in range(H1):
                                hi, lo = g_hi[:, u, k, :], g_lo[:, u, k, :]
                                if half == 0 and u == 0:
                                    pe.wait_ge(w_lo, k + 1)
                                for n, (a, b) in enumerate(((hi, w2_hi), (hi, w2_lo), (lo, w2_hi))):
                                    last = nc.tensor.matmul(ps[u][:, half, 0:HALF], a, b[:, k, at:at + HALF],
                                                            start=(k == 0 and n == 0),
                                                            stop=(k == H1 - 1 and n == 2))
                        last.then_inc(summed, 1)


def attention_again(nc, s):
    with ExitStack() as ctx:
        def sb(name, shape, dt=F32):
            return ctx.enter_context(nc.sbuf_tensor(name, shape, dt))

        def sem(name):
            return ctx.enter_context(nc.semaphore(name))

        MS = NT // 2
        count = sb("count2", [P, NT, NP], U16)
        mask = sb("mask2", [P, MS, NP], BF16)
        al_rows = sb("al2_rows", [2, NP])
        junk = sb("junk3", [P, 2, NP], BF16)
        best = sb("best2", [P, NT])
        top = sb("top2", [P, 2, NT])
        rel = sb("rel2", [P, NT, 2])
        rel_rows = sb("rel2_rows", [2, NP])
        small = sb("small2", [P, NT])
        ex = sb("ex2", [P, 2, NP])
        ey = sb("ey2", [P, 2, NP])
        ps = ctx.enter_context(nc.psum_tensor("ps_rows", [P, 3, 512], F32))
        ps_all = ctx.enter_context(nc.psum_tensor("ps_all", [P, 3, 512], F32))
        count_in, al_turned, al_kept, al_spread = (sem("count_in"), sem("al2_turned"), sem("al2_rows_kept"),
                                                   sem("al2_spread"))
        mask_in = [sem(f"mask2_in{q}") for q in range(MS)]
        maxed, step, rel_turned, rel_kept, rel_spread = (sem("max2"), sem("e_step"), sem("rel2_turned"),
                                                         sem("rel2_kept"), sem("rel2_spread"))
        everywhere = [rows[:, :, :].rearrange("p a n -> p (a n)")[:, 0:NP] for rows in (ps_all, ps)]
        exped, joined, made = sem("exped2"), sem("joined2"), sem("made2")

        with nc.Block() as block:
            @block.sync
            def _(sp):
                for t in range(MS):
                    sp.dma_start(mask[:, t, :], s.mask_dram.ap()[t]).then_inc(mask_in[t], 16)
                sp.dma_start(count[:, :, :], s.count_dram.ap()).then_inc(count_in, 16)
                for t in range(MS, NT):
                    sp.wait_ge(maxed, t - MS + 1)
                    sp.dma_start(mask[:, t - MS, :], s.mask_dram.ap()[t]).then_inc(mask_in[t - MS], 16)

            @block.tensor
            def _(pe):
                def turn(src, turned):
                    for c, (at, width) in enumerate(PARTS):
                        for t in range(at // P, (at + width) // P):
                            last = nc.tensor.transpose(ps[0:2, c, t * P - at:(t + 1) * P - at], src[:, t, :],
                                                       s.ident[:, :])
                        last.then_inc(turned, 1)

                def spread(rows, a, to):
                    for c, (at, width) in enumerate(PARTS):
                        last = nc.tensor.matmul(to[:, c, 0:width], s.ident[0:2, a:a + 1].broadcast_to([2, P]),
                                                rows[:, at:at + width], start=True, stop=True)
                    return last

                turn(s.al2_col, al_turned)
                pe.wait_ge(al_kept, 3)
                spread(al_rows, 0, ps_all).then_inc(al_spread, 1)
                pe.wait_ge(step, 5)
                turn(rel, rel_turned)
                pe.wait_ge(rel_kept, 3)
                spread(rel_rows, 0, ps_all)
                spread(rel_rows, 1, ps).then_inc(rel_spread, 1)

            @block.scalar
            def _(act):
                for rows_to, turned, kept in ((al_rows, al_turned, al_kept), (rel_rows, rel_turned, rel_kept)):
                    for c, (at, width) in enumerate(PARTS):
                        act.wait_ge(turned, c + 1)
                        nc.scalar.activation(rows_to[:, at:at + width], ps[0:2, c, 0:width],
                                             ACT.Copy).then_inc(kept, 1)
                act.wait_ge(rel_spread, 1)
                for t in range(NT):
                    if t >= 2:
                        act.wait_ge(made, t - 1)
                    nc.scalar.activation(ex[:, t % 2, :], everywhere[0], ACT.Exp, bias=s.al2_col[:, t, 0:1])
                    nc.scalar.activation(ey[:, t % 2, :], everywhere[1], ACT.Exp,
                                         bias=small[:, t:t + 1]).then_inc(exped, 1)

            @block.vector
            def _(dve):
                n = [0]

                def then(ins):
                    n[0] += 1
                    ins.then_inc(step, 1)
                    dve.wait_ge(step, n[0])

                dve.wait_ge(al_spread, 1)
                for t in range(NT):
                    dve.wait_ge(mask_in[t % MS], 16 * (t // MS + 1))
                    if t >= 2:
                        dve.wait_ge(maxed, t - 1)
                    nc.vector.tensor_tensor_reduce(junk[:, t % 2, :], mask[:, t % MS, :], everywhere[0], 1.0,
                                                   2.0 * NOT_A_NEIGHBOUR, ALU.add, ALU.max,
                                                   best[:, t:t + 1]).then_inc(maxed, 1)
                dve.wait_ge(maxed, NT)
                src, dst = s.al2_col[:, :, 0], s.al2_col[:, :, 1]
                then(nc.vector.tensor_tensor(top[:, 0], best[:, :], dst, ALU.add))
                then(nc.vector.scalar_tensor_tensor(top[:, 1], top[:, 0], SLOPE, top[:, 0], ALU.mult, ALU.max))
                then(nc.vector.scalar_tensor_tensor(top[:, 1], best[:, :], 0.5 * NOT_A_NEIGHBOUR, top[:, 1],
                                                    ALU.is_gt, ALU.mult))
                nc.vector.tensor_scalar(small[:, :], src, SLOPE, None, ALU.mult)
                then(nc.vector.tensor_tensor(rel[:, :, 0], dst, top[:, 1], ALU.subtract))
                then(nc.vector.scalar_tensor_tensor(rel[:, :, 1], dst, SLOPE, top[:, 1], ALU.mult, ALU.subtract))
                dve.wait_ge(count_in, 16)
                for t in range(NT):
                    dve.wait_ge(exped, t + 1)
                    nc.vector.scalar_tensor_tensor(ex[:, t % 2, :], ey[:, t % 2, :], 1.0, ex[:, t % 2, :],
                                                   ALU.min, ALU.max).then_inc(joined, 1)
                    dve.wait_ge(joined, t + 1)
                    nc.vector.scalar_tensor_tensor(s.prob2[:, t, :], ex[:, t % 2, :], 1.0, count[:, t, :],
                                                   ALU.min, ALU.mult).then_inc(made, 1)


def mix_and_route(nc, s, x, bias2, wg, we, bg, be):
    with ExitStack() as ctx:
        def sb(name, shape, dt=F32):
            return ctx.enter_context(nc.sbuf_tensor(name, shape, dt))

        def sem(name):
            return ctx.enter_context(nc.semaphore(name))

        p_hi = sb("p_hi", [P, 2, NT, P], F32R)
        p_lo = sb("p_lo", [P, 2, NT, P], F32R)
        x_in_t = sb("x_in_t", [P, 2, D])
        x2 = sb("x2", [P, 2, D])
        xf = sb("xf", [P, 2, D])
        xf_t = sb("xf_t", [P, 2, KD, P])
        b_row = sb("b_row", [P, D])
        wr = sb("wr", [P, KD, RC])
        br = sb("br", [P, RC])
        zi = sb("zi", [P, 2, 2])
        stats = sb("stats2", [P, 2, 2, 6])
        mv = sb("mv2", [P, 2, 2])
        veps = sb("veps2", [P, 2, 1])
        half_neg = sb("half_neg", [P, 1])
        rstd = sb("rstd2", [P, 2, 1])
        ps_o = [ctx.enter_context(nc.psum_tensor(f"ps_mix{u}", [P, 2, 512], F32)) for u in range(2)]
        ps_x = ctx.enter_context(nc.psum_tensor("ps_xf", [P, 2, 512], F32))
        ps_l = ctx.enter_context(nc.psum_tensor("ps_logit", [P, 512], F32))
        W2H = (D + 4) // 2

        wr_in, br_in = sem("wr_in"), sem("br_in")
        x_in = [sem("xt_in0"), sem("xt_in1")]
        phi_made, plo_made, mixed, x_biased, z_step = (sem("phi_made"), sem("plo_made"), sem("mixed2"),
                                                       sem("x_biased"), sem("z_step"))
        x2_made, stat, var_made, rooted, xf_made = (sem("x2_made"), sem("stat2"), sem("var_made"),
                                                    sem("rooted"), sem("xf_made"))
        turned, xft_kept, logged, logits_kept = sem("xf_turned"), sem("xft_kept"), sem("logged"), sem("logits_kept")
        x2_out = [sem("x2_out0"), sem("x2_out1")]
        xf_out = [sem("xf_out0"), sem("xf_out1")]
        consts = sem("f_consts")

        with nc.Block() as block:
            @block.sync
            def _(sp):
                sp.dma_start(b_row[:, :], bias2.broadcast_to([P, D])).then_inc(br_in, 16)
                sp.dma_start(br[:, 0:G], bg.broadcast_to([P, G])).then_inc(br_in, 16)
                sp.dma_start(br[:, G:RC], be.broadcast_to([P, E])).then_inc(br_in, 16)
                sp.dma_start(wr[:, :, 0:G], wg.rearrange("(k p) g -> p k g", p=P)).then_inc(wr_in, 16)
                for g in range(G):
                    sp.dma_start(wr[:, :, G + g * EG:G + (g + 1) * EG],
                                 we[g].rearrange("(k p) e -> p k e", p=P)).then_inc(wr_in, 16)
                for u in range(2):
                    sp.dma_start(x_in_t[:, u, :], x[u * P:(u + 1) * P, :]).then_inc(x_in[u], 16)

                def out(t, i, u):
                    sp.wait_ge(x2_made, t + 1)
                    sp.dma_start(s.sum_dram.ap()[bass.ds(t * P, P), :], x2[:, u, :]).then_inc(x2_out[u], 16)
                    sp.wait_ge(xf_made, t + 1)
                    sp.dma_start(s.table.ap()[bass.ds(t * P, P), 0:D], xf[:, u, :]).then_inc(xf_out[u], 16)

                with sp.Fori(0, NT // 2 - 1) as i:
                    for u in range(2):
                        t = 2 * i + u
                        sp.wait_ge(x2_made, t + 1)
                        sp.dma_start(x_in_t[:, u, :], x[bass.ds((t + 2) * P, P), :]).then_inc(x_in[u], 16)
                        out(t, i, u)
                for u in range(2):
                    out(NT - 2 + u, NT // 2 - 1, u)
                for u in range(2):
                    sp.wait_ge(x2_out[u], 16 * (NT // 2))
                    sp.wait_ge(xf_out[u], 16 * (NT // 2))

            @block.gpsimd
            def _(pool):
                nc.gpsimd.memset(half_neg[:, :], -0.5).then_inc(consts, 1)
                pool.wait_ge(consts, 1)
                pool.wait_ge(br_in, 48)
                with pool.Fori(0, NT // 2) as i:
                    for u in range(2):
                        t = 2 * i + u
                        pool.wait_ge(x_in[u], 16 * i + 16)
                        nc.gpsimd.tensor_tensor(x_in_t[:, u, :], x_in_t[:, u, :], b_row[:, :],
                                                ALU.add).then_inc(x_biased, 1)
                        pool.wait_ge(var_made, t + 1)
                        nc.gpsimd.tensor_tensor(rstd[:, u, :], veps[:, u, :], half_neg[:, :],
                                                ALU.pow).then_inc(rooted, 1)

            @block.scalar
            def _(act):
                def split(t, u):
                    nc.scalar.activation(p_hi[:, u], s.prob2[:, :, bass.ds(t * P, P)], ACT.Copy).then_inc(phi_made, 1)

                split(0, 0)
                split(1, 1)
                with act.Fori(0, NT // 2) as i:
                    for u in range(2):
                        t = 2 * i + u
                        act.wait_ge(mixed, t + 1)
                        nc.scalar.activation(p_hi[:, u], s.prob2[:, :, bass.ds((t + 2) % NT * P, P)],
                                             ACT.Copy).then_inc(phi_made, 1)
                        act.wait_ge(turned, t + 1)
                        nc.scalar.activation(xf_t[:, u].rearrange("p (b k) n -> p b (k n)", b=2),
                                             ps_x[:, :, 0:HALF], ACT.Copy).then_inc(xft_kept, 1)

            @block.vector
            def _(dve):
                def split(u):
                    nc.vector.tensor_tensor(p_lo[:, u], s.prob2[:, :, bass.ds(low_at[0], P)],
                                            p_hi[:, u].bitcast(F32), ALU.subtract).then_inc(plo_made, 1)

                low_at = [0]
                for t in range(2):
                    dve.wait_ge(phi_made, t + 1)
                    low_at[0] = t * P
                    split(t)
                steps = dve.alloc_register("f_steps")
                dve.reg_mov(steps, 0)

                def then(ins):
                    ins.then_inc(stat, 1)
                    dve.reg_add(steps, steps, 1)
                    done = dve.snap(steps)
                    dve.wait_ge(br_in, 48)
                    dve.wait_ge(stat, done)

                def normalize(t, i, u, first=False):
                    dve.wait_ge(mixed, t + 1)
                    then(nc.vector.tensor_scalar(zi[:, u, 0:1], ps_o[u][:, 1, D - W2H:D - W2H + 1], 1e-16,
                                                 None, ALU.add))
                    then(nc.vector.reciprocal(zi[:, u, 1:2], zi[:, u, 0:1]))
                    dve.wait_ge(x_biased, t + 1)
                    if not first:
                        dve.wait_ge(x2_out[u], 16 * i)
                    nc.vector.scalar_tensor_tensor(x2[:, u, 0:W2H], ps_o[u][:, 0, 0:W2H], zi[:, u, 1:2],
                                                   x_in_t[:, u, 0:W2H], ALU.mult, ALU.add)
                    nc.vector.scalar_tensor_tensor(x2[:, u, W2H:D], ps_o[u][:, 1, 0:D - W2H], zi[:, u, 1:2],
                                                   x_in_t[:, u, W2H:D], ALU.mult,
                                                   ALU.add).then_inc(x2_made, 1)
                    dve.wait_ge(x2_made, t + 1)
                    nc.vector.bn_stats(stats[:, u, 0, :], x2[:, u, 0:HALF])
                    then(nc.vector.bn_stats(stats[:, u, 1, :], x2[:, u, HALF:D]))
                    then(nc.vector.bn_aggr(mv[:, u, :], stats[:, u, :, :].rearrange("p a b -> p (a b)")))
                    nc.vector.tensor_scalar(veps[:, u, :], mv[:, u, 1:2], LN_EPS, None,
                                            ALU.add).then_inc(var_made, 1)
                    dve.wait_ge(rooted, t + 1)
                    if not first:
                        dve.wait_ge(xf_out[u], 16 * i)
                    nc.vector.tensor_scalar(xf[:, u, :], x2[:, u, :], mv[:, u, 0:1], rstd[:, u, :],
                                            ALU.subtract, ALU.mult).then_inc(xf_made, 1)
                    dve.wait_ge(phi_made, t + 3)
                    low_at[0] = (t + 2) % NT * P
                    split(u)
                    dve.wait_ge(logged, t + 1)
                    nc.vector.tensor_tensor(s.gl[:, bass.ds(t, 1), :].rearrange("p o g -> p (o g)"),
                                            ps_l[:, 0:G], br[:, 0:G], ALU.add)
                    nc.vector.tensor_tensor(s.el[:, bass.ds(t, 1), :].rearrange("p o g -> p (o g)"),
                                            ps_l[:, G:RC], br[:, G:RC], ALU.add).then_inc(logits_kept, 1)

                for t in range(2):
                    normalize(t, 0, t, first=True)
                with dve.Fori(1, NT // 2) as i:
                    for u in range(2):
                        normalize(2 * i + u, i, u)

            @block.tensor
            def _(pe):
                pe.wait_ge(wr_in, 16 * (1 + G))

                def mix(i, u, half, first=False):
                    if not first:
                        pe.wait_ge(x2_made, 2 * i)
                    at = half * W2H
                    for k in range(NT):
                        hi, lo = p_hi[:, u, k, :], p_lo[:, u, k, :]
                        for n, (a, b) in enumerate(((hi, s.h2_hi), (hi, s.h2_lo), (lo, s.h2_hi))):
                            last = nc.tensor.matmul(ps_o[u][:, half, 0:W2H], a, b[:, k, at:at + W2H],
                                                    start=(k == 0 and n == 0),
                                                    stop=(k == NT - 1 and n == 2))
                    if half == 1:
                        last.then_inc(mixed, 1)

                def turn(t, u, first=False):
                    pe.wait_ge(xf_made, t + 1)
                    if not first:
                        pe.wait_ge(xft_kept, t)
                    for k in range(KD):
                        last = nc.tensor.transpose(ps_x[:, k // 3, (k % 3) * P:(k % 3 + 1) * P],
                                                   xf[:, u, k * P:(k + 1) * P], s.ident[:, :])
                    last.then_inc(turned, 1)

                def route(t, u, first=False):
                    pe.wait_ge(xft_kept, t + 1)
                    if not first:
                        pe.wait_ge(logits_kept, t)
                    for k in range(KD):
                        last = nc.tensor.matmul(ps_l[:, 0:RC], xf_t[:, u, k, :], wr[:, k, :],
                                                start=(k == 0), stop=(k == KD - 1))
                    last.then_inc(logged, 1)

                def step(t, i, u, first=False, second=False):
                    pe.wait_ge(plo_made, t + 1)
                    mix(i, u, 0, first or second)
                    if not first:
                        turn(t - 1, 1 - u, second)
                    mix(i, u, 1, first or second)
                    if not first:
                        route(t - 1, 1 - u, second)

                step(0, 0, 0, first=True)
                step(1, 0, 1, second=True)
                with pe.Fori(1, NT // 2) as i:
                    for u in range(2):
                        step(2 * i + u, i, u)
                turn(NT - 1, 1)
                route(NT - 1, 1)


def plan_experts(nc, s, b2):
    with ExitStack() as ctx:
        def sb(name, shape, dt=F32):
            return ctx.enter_context(nc.sbuf_tensor(name, shape, dt))

        def sem(name):
            return ctx.enter_context(nc.semaphore(name))

        ahead = sb("ahead", [P, NT * G, EG, EG], BF16)
        tied = sb("tied", [P, NT * G, EG, EG], BF16)
        before_b = sb("before_b", [P, EG, EG], BF16)
        before = sb("before", [P, EG, EG])
        g_ahead = sb("g_ahead", [P, NT, G, G], BF16)
        g_tied = sb("g_tied", [P, NT, G, G], BF16)
        rank = sb("rank", [P, NT * G, EG])
        sel = sb("sel", [P, NT * G, EG])
        g_rank = sb("g_rank", [P, NT, G])
        g_sel = sb("g_sel", [P, NT, G])
        peak = sb("peak", [P, NT * G])
        g_peak = sb("g_peak", [P, NT])
        weight = sb("weight", [P, NT * G, EG])
        g_weight = sb("g_weight", [P, NT, G])
        total = sb("total", [P, NT * G])
        g_total = sb("g_total", [P, NT])
        chosen = sb("chosen", [P, NT, E])
        chosen_b = sb("chosen_b", [P, NT, E], BF16)
        passed = sb("passed", [P, NT + 1, E])
        passed_b = sb("passed_b", [P, NT + 1, E], BF16)
        gates = sb("gates", [P, NT, E])
        b2_all = sb("b2_all", [E, D])
        pad_rows = sb("pad_rows", [P, TW])
        list_part = sb("list_part", [P, 2, LIST])
        list_f = sb("list_f", [P, LIST])
        padding = sb("padding", [P, LIST])
        pad_at = sb("pad_at", [P, 1])
        upper = sb("upper", [P, P])
        upper_b = sb("upper_b", [P, P], BF16)
        ones_b = sb("ones_b", [P, P], BF16)
        place_i = sb("place_i", [P, 3, NT, E], I32)
        row_at = sb("row_at", [P, NT, E])
        row_b = sb("row_b", [P, NT, E], BF16)
        lane_b = sb("lane_b", [P, P], BF16)
        tile_at = sb("tile_at", [P, NT, E], BF16)
        tile_no = sb("tile_no", [P, NT], I16)
        tile_bf = sb("tile_bf", [P, NT], BF16)
        in_tile = sb("in_tile", [P, NT, E, NT], BF16)
        token = sb("token", [P, NT, E, 2, NT], BF16)
        lane_i = sb("lane_i", [P, 1], I32)
        lane = sb("lane", [P, 1])
        is_node = sb("is_node", [P, 1])
        one_row = sb("one_row", [P, 2, NT, P], BF16)
        level = sb("level", [1, NT])
        level_i = sb("level_i", [1, NT], I32)
        over = sb("over", [1, E, NT])
        tiles_f = sb("tiles_f", [1, 2, E])
        sums = sb("sums", [1, 2, E])

        ps_p = ctx.enter_context(nc.psum_tensor("ps_place", [P, 512], F32))
        ps_n = ctx.enter_context(nc.psum_tensor("ps_counts", [P, 512], F32))
        ps_t = ctx.enter_context(nc.psum_tensor("ps_gates_t", [P, 3, 512], F32))
        ps_l = [ctx.enter_context(nc.psum_tensor(f"ps_list{u}", [P, 512], F32)) for u in range(2)]

        consts, step, shifted, exped = sem("g_consts"), sem("g_step"), sem("g_shifted"), sem("g_exped")
        routed, chosen_set, placed = sem("routed"), sem("chosen_set"), sem("placed")
        turned, kept, out_done = sem("gates_turned"), sem("gates_kept"), sem("tab_out")
        rows_made, listed, list_read, values_made = sem("rows_made"), sem("listed"), sem("list_read"), sem("values")
        started, b2_in = sem("started"), sem("b2_in")

        with nc.Block() as block:
            @block.gpsimd
            def _(pool):
                nc.gpsimd.memset(before[:, :, :], 1.0).then_inc(consts, 1)
                nc.gpsimd.memset(upper[:, :], 1.0).then_inc(consts, 1)
                nc.gpsimd.memset(pad_rows[:, :], 0.0).then_inc(consts, 1)
                nc.gpsimd.iota(tile_no[:, :], [[1, NT]], base=0, channel_multiplier=0).then_inc(consts, 1)
                nc.gpsimd.iota(lane_i[:, 0:1], [[1, 1]], base=1, channel_multiplier=1).then_inc(consts, 1)
                nc.gpsimd.iota(level_i[:, :], [[P, NT]], base=0, channel_multiplier=0).then_inc(consts, 1)
                nc.gpsimd.memset(ones_b[:, :], 1.0).then_inc(consts, 1)
                nc.gpsimd.memset(list_part[:, :, :], 0.0).then_inc(consts, 1)
                pool.wait_ge(consts, 8)
                nc.gpsimd.affine_select(out=before[:, :, :], in_=before[:, :, :], compare_op=ALU.is_gt, fill=0.0,
                                        base=0, pattern=[[1, EG], [-1, EG]], channel_multiplier=0).then_inc(consts, 1)
                nc.gpsimd.affine_select(out=upper[:, :], in_=upper[:, :], compare_op=ALU.is_gt, fill=0.0,
                                        base=0, pattern=[[1, P]], channel_multiplier=-1).then_inc(consts, 1)

            @block.sync
            def _(sp):
                sp.dma_start(b2_all[:, :], b2).then_inc(b2_in, 16)
                sp.wait_ge(consts, 10)
                sp.dma_start(s.table.ap()[NP:ROWS, :], pad_rows[:, :]).then_inc(out_done, 16)
                sp.dma_start(s.sum_dram.ap()[NP:ROWS, :], pad_rows[:, 0:D]).then_inc(out_done, 16)
                sp.wait_ge(routed, 1)
                sp.dma_start(s.table.ap()[0:NP, D:TW].rearrange("(t p) c -> p t c", p=P),
                             gates[:, :, :]).then_inc(out_done, 16)
                sp.wait_ge(out_done, 48)

            @block.scalar
            def _(act):
                act.wait_ge(shifted, 1)
                nc.scalar.activation(weight[:, :, :], weight[:, :, :], ACT.Exp)
                nc.scalar.activation(g_weight[:, :, :], g_weight[:, :, :], ACT.Exp).then_inc(exped, 1)
                for c, (at, width) in enumerate(PARTS):
                    act.wait_ge(turned, c + 1)
                    nc.scalar.activation(s.gates_hi[:, at:at + width], ps_t[0:E, c, 0:width],
                                         ACT.Copy).then_inc(kept, 1)
                act.wait_ge(b2_in, 16)
                nc.scalar.activation(s.b2_hi[:, :], b2_all[:, :], ACT.Copy).then_inc(kept, 1)
                act.wait_ge(started, 1)
                with act.Fori(0, E // 2) as i:
                    for u in range(2):
                        e = 2 * i + u
                        start = act.value_load(s.starts[0:1, bass.ds(e, 1)], min_val=LEAD, max_val=LIST - NT)
                        act.wait_ge(listed, e + 3)
                        nc.scalar.activation(list_part[:, :, bass.ds(start, NT)],
                                             ps_l[u][:, 0:2 * NT].rearrange("p (b a) -> p b a", b=2),
                                             ACT.Copy).then_inc(list_read, 1)
                        act.wait_ge(list_read, e + 1)

            @block.vector
            def _(dve):
                n = [0]

                def then(ins):
                    n[0] += 1
                    ins.then_inc(step, 1)
                    dve.wait_ge(step, n[0])

                el = s.el[:, :, :].rearrange("p t (g e) -> p (t g) e", g=G)
                gl = s.gl[:, :, :]
                dve.wait_ge(consts, 10)
                nc.vector.tensor_copy(before_b[:, :, :], before[:, :, :])
                nc.vector.tensor_copy(lane_b[:, :], s.column[:, 0:P])
                then(nc.vector.tensor_copy(lane[:, :], lane_i[:, :]))
                nc.vector.tensor_scalar(is_node[:, :], lane[:, 0:1], float(TAIL), None, ALU.is_le)
                nc.vector.tensor_reduce(peak[:, :], el, AX.X, ALU.max)
                then(nc.vector.tensor_reduce(g_peak[:, :], gl, AX.X, ALU.max))
                nc.vector.tensor_tensor(weight[:, :, :], el, peak[:, :].unsqueeze(2).broadcast_to([P, NT * G, EG]),
                                        ALU.subtract)
                nc.vector.tensor_tensor(g_weight[:, :, :], gl, g_peak[:, :].unsqueeze(2).broadcast_to([P, NT, G]),
                                        ALU.subtract).then_inc(shifted, 1)
                wide = [P, NT * G, EG, EG]
                nc.vector.tensor_tensor(ahead[:, :, :, :], el.unsqueeze(2).broadcast_to(wide),
                                        el.unsqueeze(3).broadcast_to(wide), ALU.is_gt)
                nc.vector.tensor_tensor(tied[:, :, :, :], el.unsqueeze(2).broadcast_to(wide),
                                        el.unsqueeze(3).broadcast_to(wide), ALU.is_equal)
                g_wide = [P, NT, G, G]
                nc.vector.tensor_tensor(g_ahead[:, :, :, :], gl.unsqueeze(2).broadcast_to(g_wide),
                                        gl.unsqueeze(3).broadcast_to(g_wide), ALU.is_gt)
                then(nc.vector.tensor_tensor(g_tied[:, :, :, :], gl.unsqueeze(2).broadcast_to(g_wide),
                                             gl.unsqueeze(3).broadcast_to(g_wide), ALU.is_equal))
                nc.vector.tensor_tensor(tied[:, :, :, :], tied[:, :, :, :],
                                        before_b[:, :, :].unsqueeze(1).broadcast_to(wide), ALU.mult)
                then(nc.vector.tensor_tensor(g_tied[:, :, :, :], g_tied[:, :, :, :],
                                             before_b[:, 0:G, 0:G].unsqueeze(1).broadcast_to(g_wide), ALU.mult))
                nc.vector.tensor_tensor(ahead[:, :, :, :], ahead[:, :, :, :], tied[:, :, :, :], ALU.add)
                then(nc.vector.tensor_tensor(g_ahead[:, :, :, :], g_ahead[:, :, :, :], g_tied[:, :, :, :], ALU.add))
                nc.vector.tensor_reduce(rank[:, :, :], ahead[:, :, :, :], AX.X, ALU.add)
                then(nc.vector.tensor_reduce(g_rank[:, :, :], g_ahead[:, :, :, :], AX.X, ALU.add))
                nc.vector.tensor_scalar(sel[:, :, :], rank[:, :, :], float(KE), None, ALU.is_lt)
                then(nc.vector.tensor_scalar(g_sel[:, :, :], g_rank[:, :, :], float(KG), None, ALU.is_lt))
                all_g = g_sel[:, :, :].rearrange("p t g -> p (t g)").unsqueeze(2).broadcast_to([P, NT * G, EG])
                then(nc.vector.tensor_tensor(chosen[:, :, :].rearrange("p t (g e) -> p (t g) e", g=G),
                                             sel[:, :, :], all_g, ALU.mult))
                then(nc.vector.tensor_scalar(chosen[:, NT - 1, :], chosen[:, NT - 1, :], is_node[:, 0:1], None,
                                             ALU.mult))
                nc.vector.tensor_copy(chosen_b[:, :, :], chosen[:, :, :])
                nc.vector.tensor_copy(upper_b[:, :], upper[:, :])
                then(nc.vector.memset(passed[:, 0, :], 0.0))
                for t in range(NT):
                    then(nc.vector.tensor_tensor(passed[:, t + 1, :], passed[:, t, :], chosen[:, t, :], ALU.add))
                nc.vector.tensor_copy(passed_b[:, :, :], passed[:, :, :]).then_inc(chosen_set, 1)
                nc.vector.tensor_copy(tile_bf[:, :], tile_no[:, :])
                then(nc.vector.tensor_copy(level[:, :], level_i[:, :]))
                dve.wait_ge(exped, 1)
                nc.vector.tensor_tensor(weight[:, :, :], weight[:, :, :], sel[:, :, :], ALU.mult)
                then(nc.vector.tensor_tensor(g_weight[:, :, :], g_weight[:, :, :], g_sel[:, :, :], ALU.mult))
                nc.vector.tensor_reduce(total[:, :], weight[:, :, :], AX.X, ALU.add)
                then(nc.vector.tensor_reduce(g_total[:, :], g_weight[:, :, :], AX.X, ALU.add))
                nc.vector.reciprocal(total[:, :], total[:, :])
                then(nc.vector.reciprocal(g_total[:, :], g_total[:, :]))
                nc.vector.tensor_tensor(weight[:, :, :], weight[:, :, :],
                                        total[:, :].unsqueeze(2).broadcast_to([P, NT * G, EG]), ALU.mult)
                then(nc.vector.tensor_tensor(g_weight[:, :, :], g_weight[:, :, :],
                                             g_total[:, :].unsqueeze(2).broadcast_to([P, NT, G]), ALU.mult))
                nc.vector.scalar_tensor_tensor(weight[:, :, :], weight[:, :, :], GATE_MIN, weight[:, :, :],
                                               ALU.is_ge, ALU.mult)
                then(nc.vector.scalar_tensor_tensor(g_weight[:, :, :], g_weight[:, :, :], GATE_MIN,
                                                    g_weight[:, :, :], ALU.is_ge, ALU.mult))
                all_g = g_weight[:, :, :].rearrange("p t g -> p (t g)").unsqueeze(2).broadcast_to([P, NT * G, EG])
                then(nc.vector.tensor_tensor(weight[:, :, :], weight[:, :, :], all_g, ALU.mult))
                nc.vector.tensor_copy(gates[:, :, :],
                                      weight[:, :, :].rearrange("p (t g) e -> p t (g e)", g=G)).then_inc(routed, 1)
                dve.wait_ge(placed, 1)
                then(nc.vector.tensor_copy(place_i[:, 0], ps_p[:, 0:NT * E].rearrange("p (t e) -> p t e", e=E)))
                nc.vector.tensor_scalar(place_i[:, 1], place_i[:, 0], 7, None, ALU.arith_shift_right)
                then(nc.vector.tensor_scalar(place_i[:, 2], place_i[:, 0], P - 1, None, ALU.bitwise_and))
                nc.vector.tensor_copy(tile_at[:, :, :], place_i[:, 1])
                then(nc.vector.tensor_copy(row_at[:, :, :], place_i[:, 2]))
                then(nc.vector.scalar_tensor_tensor(row_at[:, :, :], row_at[:, :, :], 1.0, chosen[:, :, :],
                                                    ALU.add, ALU.mult))
                nc.vector.tensor_scalar(row_b[:, :, :], row_at[:, :, :], -1.0, None, ALU.add)
                then(nc.vector.tensor_tensor(
                    in_tile[:, :, :, :].rearrange("p t e a -> p (t e) a"),
                    tile_at[:, :, :].rearrange("p t e -> p (t e)").unsqueeze(2).broadcast_to([P, NT * E, NT]),
                    tile_bf[:, :].unsqueeze(1).broadcast_to([P, NT * E, NT]), ALU.is_equal))
                nc.vector.tensor_scalar(token[:, :, :, 0, :], in_tile[:, :, :, :], lane[:, 0:1], None, ALU.mult)
                for t in range(NT):
                    last = nc.vector.tensor_scalar(token[:, t, :, 1, :], in_tile[:, t, :, :], float(P * t), None,
                                                   ALU.mult)
                last.then_inc(values_made, 1)
                nc.vector.tensor_tensor(over[:, :, :], ps_n[0:1, 0:E].unsqueeze(2).broadcast_to([1, E, NT]),
                                        level[:, :].unsqueeze(1).broadcast_to([1, E, NT]), ALU.is_gt)
                then(nc.vector.memset(sums[:, :, :], 0.0))
                then(nc.vector.tensor_reduce(tiles_f[:, 0, :], over[:, :, :], AX.X, ALU.add))
                then(nc.vector.tensor_scalar(tiles_f[:, 1, :], tiles_f[:, 0, :], float(MIN_TILES), None, ALU.max))
                nc.vector.tensor_copy(s.tiles[:, :], tiles_f[:, 1, :])
                then(nc.vector.tensor_copy(sums[:, 0, 1:E], tiles_f[:, 1, 0:E - 1]))
                reach, u = 1, 0
                while reach < E:
                    nc.vector.tensor_copy(sums[:, 1 - u, 0:reach], sums[:, u, 0:reach])
                    then(nc.vector.tensor_tensor(sums[:, 1 - u, reach:E], sums[:, u, reach:E],
                                                 sums[:, u, 0:E - reach], ALU.add))
                    reach, u = 2 * reach, 1 - u
                nc.vector.tensor_scalar(s.starts[:, :], sums[:, u, :], float(LEAD), None,
                                        ALU.add).then_inc(started, 1)
                for c, (at, width) in enumerate(PARTS):
                    dve.wait_ge(kept, c + 1)
                    nc.vector.tensor_tensor(s.gates_lo[:, at:at + width], ps_t[0:E, c, 0:width],
                                            s.gates_hi[:, at:at + width].bitcast(F32), ALU.subtract)
                dve.wait_ge(kept, 4)
                nc.vector.tensor_tensor(s.b2_lo[:, :], b2_all[:, :], s.b2_hi[:, :].bitcast(F32), ALU.subtract)
                def match(e, u):
                    wide = [P, NT, P]
                    nc.vector.tensor_tensor(one_row[:, u], lane_b[:, :].unsqueeze(1).broadcast_to(wide),
                                            row_b[:, :, bass.ds(e, 1)].broadcast_to(wide),
                                            ALU.is_equal).then_inc(rows_made, 1)

                with dve.Fori(0, E // 2) as i:
                    for u in range(2):
                        e = 2 * i + u
                        dve.wait_ge(listed, e + 1)
                        match(e, u)
                dve.wait_ge(list_read, E)
                nc.vector.tensor_tensor(list_f[:, :], list_part[:, 0], list_part[:, 1], ALU.add)
                nc.vector.tensor_scalar(pad_at[:, :], lane[:, :], float(NP), None, ALU.add).then_inc(step, 1)
                dve.wait_ge(step, n[0] + 1)
                n[0] += 1
                then(nc.vector.tensor_scalar(padding[:, :], list_f[:, :], 0.0, None, ALU.is_equal))
                then(nc.vector.scalar_tensor_tensor(list_f[:, :], padding[:, :], pad_at[:, :], list_f[:, :],
                                                    ALU.mult, ALU.add))
                nc.vector.tensor_scalar(s.list_i[:, :], list_f[:, :], -1.0, None, ALU.add)

            @block.tensor
            def _(pe):
                pe.wait_ge(chosen_set, 1)
                nc.tensor.matmul(ps_n[:, 0:E], ones_b[:, :], passed_b[:, NT, :], start=True, stop=True)
                nc.tensor.matmul(ps_p[:, 0:NT * E], upper_b[:, :], chosen_b[:, :, :].rearrange("p t e -> p (t e)"),
                                 start=True, stop=False)
                nc.tensor.matmul(ps_p[:, 0:NT * E], ones_b[:, :],
                                 passed_b[:, 0:NT, :].rearrange("p t e -> p (t e)"),
                                 start=False, stop=True).then_inc(placed, 1)
                pe.wait_ge(routed, 1)
                for c, (at, width) in enumerate(PARTS):
                    for t in range(at // P, (at + width) // P):
                        last = nc.tensor.transpose(ps_t[0:E, c, t * P - at:(t + 1) * P - at], gates[:, t, :],
                                                   s.ident[:, :])
                    last.then_inc(turned, 1)
                pe.wait_ge(values_made, 1)
                pe.sem_inc(listed, 2)

                def list_expert(e, u, first=False):
                    pe.wait_ge(rows_made, e + 1)
                    if not first:
                        pe.wait_ge(list_read, e - 1)
                    for t in range(NT):
                        last = nc.tensor.matmul(ps_l[u][:, 0:2 * NT], one_row[:, u, t, :],
                                                token[:, t, bass.ds(e, 1), :, :]
                                                .rearrange("p o b a -> p (o b a)"),
                                                start=(t == 0), stop=(t == NT - 1))
                    last.then_inc(listed, 1)

                for u in range(2):
                    list_expert(u, u, first=True)
                with pe.Fori(1, E // 2) as i:
                    for u in range(2):
                        list_expert(2 * i + u, u)


def run_experts(nc, s, w1, b1, w2):
    with ExitStack() as ctx:
        def sb(name, shape, dt=F32):
            return ctx.enter_context(nc.sbuf_tensor(name, shape, dt))

        def sem(name):
            return ctx.enter_context(nc.semaphore(name))

        ROW = KD * HID
        PIECE = ROW // 3
        raw1 = sb("raw1", [P, 2, ROW])
        raw2 = sb("raw2", [P, 2, ROW])
        w1_hi, w1_lo = sb("e1_hi", [P, 2, ROW], F32R), sb("e1_lo", [P, 2, ROW], F32R)
        w2_hi, w2_lo = sb("e2_hi", [P, 2, ROW], F32R), sb("e2_lo", [P, 2, ROW], F32R)
        b1_all = sb("b1_all", [P, RING, HID])
        rows = sb("rows", [P, TW])
        index = sb("index", [P, 1], I32)
        to_index = sb("to_index", [P, 1], I32)
        gate = sb("gate", [P, RING, 1])
        xt_hi, xt_lo = sb("e_xt_hi", [P, KD, P], F32R), sb("e_xt_lo", [P, KD, P], F32R)
        h_in = sb("h_in", [P, HID])
        h_act = sb("h_act", [P, HID])
        ht_hi, ht_lo = sb("e_ht_hi", [P, KH, P], F32R), sb("e_ht_lo", [P, KH, P], F32R)
        y = sb("y", [P, D])

        ps_h = ctx.enter_context(nc.psum_tensor("ps_h_2", [P, 512], F32))
        ps_x = ctx.enter_context(nc.psum_tensor("ps_xt", [P, 2, 512], F32))
        ps_y = ctx.enter_context(nc.psum_tensor("ps_y", [P, 2, 512], F32))
        ps_t = ctx.enter_context(nc.psum_tensor("ps_ht", [P, 512], F32))

        w1_in, w2_in, b1_in = sem("e_w1_in"), sem("e_w2_in"), sem("e_b1_in")
        w1_hi_made, w1_lo_made, w2_hi_made, w2_lo_made = (sem("e_w1_hi"), sem("e_w1_lo"), sem("e_w2_hi"),
                                                          sem("e_w2_lo"))
        gathered, turned, x_hi_made, x_lo_made = sem("gathered"), sem("x_turned"), sem("x_hi"), sem("x_lo")
        h_summed, biased, gelued, h_turned = sem("h_summed_2"), sem("biased"), sem("gelued"), sem("h_turned")
        h_hi_made, h_lo_made, y_summed, y_made = sem("h_hi"), sem("h_lo"), sem("y_summed"), sem("y_made")
        gate_kept, index_set, to_set, scattered, ready = (sem("gate_kept"), sem("index_set"), sem("to_set"),
                                                            sem("scattered"), sem("h_ready"))

        def tiles_of(eng, e):
            return eng.value_load(s.tiles[0:1, bass.ds(e, 1)], min_val=MIN_TILES, max_val=NT)

        def over_tiles(eng, name, tile):
            count = eng.alloc_register(name)
            eng.reg_mov(count, 0)

            def one(e, head, start=False, last=False):
                k = eng.snap(count)
                tile(k, e, head, start, last)
                eng.reg_add(count, count, 1)

            def expert(e, start=False, last=False):
                one(e, True, start, last)
                tiles = tiles_of(eng, e)
                with eng.If(tiles > 1):
                    with eng.Fori(1, tiles):
                        one(e, False)

            expert(0, start=True)
            with eng.Fori(1, E - 1) as e:
                expert(e)
            expert(E - 1, last=True)
            return eng.snap(count)

        with nc.Block() as block:
            @block.sync
            def _(sp):
                def load(e, u):
                    sp.dma_start(raw1[:, u, :].rearrange("p (k m) -> p k m", k=KD),
                                 w1[bass.ds(e * D, D), :].rearrange("(k p) m -> p k m", p=P)).then_inc(w1_in, 16)
                    sp.dma_start(raw2[:, u, :].rearrange("p (k d) -> p k d", k=KH),
                                 w2[bass.ds(e * HID, HID), :].rearrange("(k p) d -> p k d", p=P)) \
                      .then_inc(w2_in, 16)
                    sp.dma_start(b1_all[:, bass.ds(e % RING, 1), :].rearrange("p o m -> p (o m)"),
                                 b1[bass.ds(e, 1), :].broadcast_to([P, HID])).then_inc(b1_in, 16)

                def loaded(e):
                    sp.wait_ge(w1_in, 16 * e + 16)
                    sp.wait_ge(w2_in, 16 * e + 16)
                    sp.wait_ge(b1_in, 16 * e + 16)

                load(0, 0)
                loaded(0)
                load(1, 1)
                with sp.Fori(1, E // 2) as i:
                    for u in range(2):
                        e = 2 * i + u
                        loaded(e - 1)
                        sp.wait_ge(w1_lo_made, 3 * e - 3)
                        sp.wait_ge(w2_lo_made, 3 * e - 3)
                        load(e, u)
                loaded(E - 1)

            @block.gpsimd
            def _(pool):
                def gather(k):
                    nc.gpsimd.tensor_copy(index[:, :], s.list_i[:, bass.ds(k + LEAD, 1)]).then_inc(index_set, 1)
                    pool.reg_add(gathers, gathers, 1)
                    this = pool.snap(gathers)
                    pool.wait_ge(ready, 1)
                    pool.wait_ge(index_set, this)
                    nc.gpsimd.indirect_dma_start(rows[:, :], None, s.table.ap(),
                                                 bass.IndirectOffsetOnAxis(index[:, 0:1], 0),
                                                 bounds_check=ROWS - 1).then_inc(gathered, 16)

                def add(k, start=False):
                    pool.wait_ge(y_made, k + 1)
                    if not start:
                        pool.wait_ge(ready, 1)
                        pool.wait_ge(scattered, 16 * k)
                    nc.gpsimd.tensor_copy(to_index[:, :], s.list_i[:, bass.ds(k, 1)]).then_inc(to_set, 1)
                    pool.wait_ge(ready, 1)
                    pool.wait_ge(to_set, k + 1)
                    nc.gpsimd.indirect_dma_start(s.sum_dram.ap(), bass.IndirectOffsetOnAxis(to_index[:, 0:1], 0),
                                                 y[:, :], None, bounds_check=ROWS - 1,
                                                 compute_op=ALU.add).then_inc(scattered, 16)

                def tile(k, e, head, start, last):
                    pool.wait_ge(ready, 1)
                    pool.wait_ge(turned, k + 1)
                    nc.gpsimd.tensor_copy(gate[:, bass.ds(k % RING, 1), :].rearrange("p o c -> p (o c)"),
                                          rows[:, bass.ds(e + D, 1)]).then_inc(gate_kept, 1)
                    pool.wait_ge(ready, 1)
                    pool.wait_ge(gate_kept, k + 1)
                    gather(k + 1)
                    add(k, start)

                pool.sem_inc(ready, 1)
                gathers = pool.alloc_register("gathers")
                pool.reg_mov(gathers, 0)
                gather(0)
                n = over_tiles(pool, "pool_tiles", tile)
                for after in range(2):
                    add(n + after)
                pool.wait_ge(gathered, 16 * n + 16)
                pool.wait_ge(scattered, 16 * n + 32)

            @block.scalar
            def _(act):
                def split(raw, hi, piece, u, made):
                    at = piece * PIECE
                    nc.scalar.activation(hi[:, u, at:at + PIECE], raw[:, u, at:at + PIECE],
                                         ACT.Copy).then_inc(made, 1)

                def split_x(k):
                    act.wait_ge(turned, k + 1)
                    nc.scalar.activation(xt_hi[:, :, :].rearrange("p (b k) n -> p b (k n)", b=2),
                                         ps_x[:, :, 0:HALF], ACT.Copy).then_inc(x_hi_made, 1)

                def weights(e, which):
                    raw, hi, arrived, made = ((raw1, w1_hi, w1_in, w1_hi_made), (raw2, w2_hi, w2_in, w2_hi_made))[which]
                    act.wait_ge(arrived, 16 * e + 16)
                    for piece in range(3):
                        at = piece * PIECE
                        u = bass.ds(e % 2, 1)
                        nc.scalar.activation(hi[:, u, at:at + PIECE], raw[:, u, at:at + PIECE],
                                             ACT.Copy).then_inc(made, 1)

                def tile(k, e, head, start, last):
                    act.wait_ge(biased, k + 1)
                    if not start:
                        act.wait_ge(h_turned, k)
                    nc.scalar.activation(h_act[:, :], h_in[:, :], ACT.Gelu).then_inc(gelued, 1)
                    split_x(k + 1)
                    if head and not last:
                        weights(e + 1, 0)
                    act.wait_ge(h_turned, k + 1)
                    nc.scalar.activation(ht_hi[:, :, :].rearrange("p k n -> p (k n)"), ps_t[:, 0:HID],
                                         ACT.Copy).then_inc(h_hi_made, 1)
                    if head and not last:
                        weights(e + 1, 1)

                weights(0, 0)
                split_x(0)
                weights(0, 1)
                over_tiles(act, "act_tiles", tile)

            @block.vector
            def _(dve):
                def split_x(k):
                    dve.wait_ge(x_hi_made, k + 1)
                    nc.vector.tensor_tensor(xt_lo[:, :, :].rearrange("p (b k) n -> p b (k n)", b=2),
                                            ps_x[:, :, 0:HALF],
                                            xt_hi[:, :, :].bitcast(F32).rearrange("p (b k) n -> p b (k n)", b=2),
                                            ALU.subtract).then_inc(x_lo_made, 1)

                def weights(e, which):
                    raw, hi, lo, halved, made = ((raw1, w1_hi, w1_lo, w1_hi_made, w1_lo_made),
                                                 (raw2, w2_hi, w2_lo, w2_hi_made, w2_lo_made))[which]
                    for piece in range(3):
                        at = piece * PIECE
                        u = bass.ds(e % 2, 1)
                        dve.wait_ge(halved, 3 * e + piece + 1)
                        nc.vector.tensor_tensor(lo[:, u, at:at + PIECE], raw[:, u, at:at + PIECE],
                                                hi[:, u, at:at + PIECE].bitcast(F32),
                                                ALU.subtract).then_inc(made, 1)

                def keep_y(k):
                    dve.wait_ge(y_summed, k)
                    dve.wait_ge(gate_kept, k)
                    dve.wait_ge(scattered, 16 * k + 16)
                    nc.vector.tensor_scalar(y[:, :].rearrange("p (b d) -> p b d", b=2), ps_y[:, :, 0:HALF],
                                            gate[:, bass.ds((k + (RING - 1)) % RING, 1), :].rearrange("p o c -> p (o c)"),
                                            None, ALU.mult).then_inc(y_made, 1)

                def tile(k, e, head, start, last):
                    dve.wait_ge(h_summed, k + 1)
                    if head:
                        dve.wait_ge(b1_in, 16 * e + 16)
                    if not start:
                        dve.wait_ge(gelued, k)
                    nc.vector.tensor_tensor(h_in[:, :], ps_h[:, 0:HID],
                                            b1_all[:, bass.ds(e % RING, 1), :].rearrange("p o m -> p (o m)"),
                                            ALU.add).then_inc(biased, 1)
                    split_x(k + 1)
                    if head and not last:
                        weights(e + 1, 0)
                    if not start:
                        keep_y(k)
                    dve.wait_ge(h_hi_made, k + 1)
                    nc.vector.tensor_tensor(ht_lo[:, :, :].rearrange("p k n -> p (k n)"), ps_t[:, 0:HID],
                                            ht_hi[:, :, :].bitcast(F32).rearrange("p k n -> p (k n)"),
                                            ALU.subtract).then_inc(h_lo_made, 1)
                    if head and not last:
                        weights(e + 1, 1)

                nc.vector.memset(y[:, :], 0.0).then_inc(y_made, 1)
                dve.wait_ge(y_made, 1)
                dve.sem_inc(y_made, 1)
                weights(0, 0)
                split_x(0)
                weights(0, 1)
                n = over_tiles(dve, "dve_tiles", tile)
                keep_y(n)

            @block.tensor
            def _(pe):
                def turn_x(k):
                    pe.wait_ge(gathered, 16 * k + 16)
                    for c in range(KD):
                        last = nc.tensor.transpose(ps_x[:, c // 3, (c % 3) * P:(c % 3 + 1) * P],
                                                   rows[:, c * P:(c + 1) * P], s.ident[:, :])
                    last.then_inc(turned, 1)

                def down(k, u):
                    pe.wait_ge(h_lo_made, k)
                    pe.wait_ge(y_made, k + 1)
                    for half in range(2):
                        for c in range(KH):
                            at = c * D + half * HALF
                            hi, lo = ht_hi[:, c, :], ht_lo[:, c, :]
                            for n, (a, b) in enumerate(((hi, w2_hi), (hi, w2_lo), (lo, w2_hi))):
                                last = nc.tensor.matmul(ps_y[:, half, 0:HALF], a,
                                                        b[:, bass.ds(u, 1), at:at + HALF]
                                                        .rearrange("p o d -> p (o d)"),
                                                        start=(c == 0 and n == 0),
                                                        stop=(c == KH - 1 and n == 2))
                    last.then_inc(y_summed, 1)

                def tile(k, e, head, start, last):
                    if head:
                        pe.wait_ge(w1_lo_made, 3 * e + 3)
                    pe.wait_ge(x_lo_made, k + 1)
                    if not start:
                        pe.wait_ge(biased, k)
                    for c in range(KD):
                        hi, lo = xt_hi[:, c, :], xt_lo[:, c, :]
                        for n, (a, b) in enumerate(((hi, w1_hi), (hi, w1_lo), (lo, w1_hi))):
                            summed = nc.tensor.matmul(ps_h[:, 0:HID], a,
                                                      b[:, bass.ds(e % 2, 1), c * HID:(c + 1) * HID]
                                                      .rearrange("p o m -> p (o m)"),
                                                      start=(c == 0 and n == 0), stop=(c == KD - 1 and n == 2))
                    summed.then_inc(h_summed, 1)
                    turn_x(k + 1)
                    if not head:
                        pe.wait_ge(w2_lo_made, 3 * e + 3)
                        down(k, e % 2)
                    elif not start:
                        pe.wait_ge(w2_lo_made, 3 * e)
                        down(k, (e + 1) % 2)
                    pe.wait_ge(gelued, k + 1)
                    if not start:
                        pe.wait_ge(h_lo_made, k)
                    for c in range(KH):
                        last_t = nc.tensor.transpose(ps_t[:, c * P:(c + 1) * P], h_act[:, c * P:(c + 1) * P],
                                                     s.ident[:, :])
                    last_t.then_inc(h_turned, 1)

                turn_x(0)
                n = over_tiles(pe, "pe_tiles", tile)
                down(n, (E - 1) % 2)


def finish(nc, s, out):
    with ExitStack() as ctx:
        def sb(name, shape, dt=F32):
            return ctx.enter_context(nc.sbuf_tensor(name, shape, dt))

        def sem(name):
            return ctx.enter_context(nc.semaphore(name))

        total = sb("total_rows", [P, NT, D])
        ps = [ctx.enter_context(nc.psum_tensor(f"ps_bias{u}", [P, 2, 512], F32)) for u in range(2)]
        biased, added, out_done = sem("bias_summed"), sem("added"), sem("node_out")
        sums_in = [sem(f"sums_in{q}") for q in range(NT)]

        def size(t):
            return P if t < NT - 1 else TAIL

        with nc.Block() as block:
            @block.sync
            def _(sp):
                for t in range(NT):
                    sp.dma_start(total[:, t, :], s.sum_dram.ap()[t * P:(t + 1) * P, :]).then_inc(sums_in[t], 16)

            @block.scalar
            def _(act):
                for t in range(NT):
                    act.wait_ge(added, t + 1)
                    act.dma_start(out[t * P:t * P + size(t), :], total[0:size(t), t, :]).then_inc(out_done, 16)
                act.wait_ge(out_done, 16 * NT)

            @block.tensor
            def _(pe):
                for t in range(NT):
                    if t >= 2:
                        pe.wait_ge(added, t - 1)
                    for half in range(2):
                        parts = ((s.gates_hi, s.b2_hi), (s.gates_hi, s.b2_lo), (s.gates_lo, s.b2_hi))
                        for n, (a, b) in enumerate(parts):
                            last = nc.tensor.matmul(ps[t % 2][:, half, 0:HALF], a[:, t * P:(t + 1) * P],
                                                    b[:, half * HALF:(half + 1) * HALF],
                                                    start=(n == 0), stop=(n == 2))
                    last.then_inc(biased, 1)

            @block.vector
            def _(dve):
                for t in range(NT):
                    dve.wait_ge(biased, t + 1)
                    dve.wait_ge(sums_in[t], 16)
                    rows = total[:, t, :].rearrange("p (b d) -> p b d", b=2)
                    nc.vector.tensor_tensor(rows, ps[t % 2][:, :, 0:HALF], rows, ALU.add).then_inc(added, 1)


def program(nc, x, edge_src, edge_dst, w1, att1, bias1, w2, att2, bias2, wg, we, bg, be, ew1, eb1, ew2, eb2, out):
    s = Shared()
    s.early = []
    with ExitStack() as ctx:
        def sb(name, shape, dt=F32, where=ctx, side="left"):
            return where.enter_context(nc.sbuf_tensor(name, shape, dt, side=side))

        s.al_dram = nc.dram_tensor("al_dram", [2 * H1, NP], F32)
        s.mask_dram = nc.dram_tensor("mask_dram", [NT, P, NP], BF16)
        s.rel_dram = nc.dram_tensor("rel_dram", [2 * H1, NP], F32)
        s.z_dram = nc.dram_tensor("z_dram", [H1, N], F32)
        s.zi_dram = nc.dram_tensor("zi_dram", [H1, N], F32)
        s.count_dram = nc.dram_tensor("count_dram", [P, NT, NP], U16)
        s.sum_dram = nc.dram_tensor("sum_dram", [ROWS, D], F32)
        s.table = nc.dram_tensor("table", [ROWS, TW], F32)
        s.ident = sb("ident", [P, P])
        s.column = sb("column", [P, NP], I16)
        s.al_col = sb("al_col", [P, NT, 2 * H1])
        s.al2_col = sb("al2_col", [P, NT, 2])
        s.gl = sb("gl", [P, NT, G])
        s.el = sb("el", [P, NT, E])
        s.al_max = sb("al_max", [P, NT, H1])
        with ExitStack() as layer1:
            with ExitStack() as inputs1:
                s.ranges = sb("ranges", [1, 2 * NT], I32, where=inputs1)
                s.block_col = sb("block_col", [P, NT], where=inputs1)
                s.src_f = sb("src_f", [P, ET], where=inputs1)
                s.dst_f = sb("dst_f", [P, ET], where=inputs1)
                s.x_t = sb("x_t", [P, NT, KD, P], where=inputs1)
                s.w1_hi = sb("w1_hi", [P, KD, D], F32R, where=inputs1)
                s.w1_lo = sb("w1_lo", [P, KD, D], F32R, where=inputs1)
                node_features(nc, s, x, w1, edge_src, edge_dst, att1)
                nc.clear_and_free_semaphores(s.early)
                nc.all_engine_barrier()
                s.count = sb("count", [P, NT, NP], U16, where=layer1, side="right")
                s.h_ext = sb("h_ext", [P, NT, H1, C1 + 1], where=layer1, side="right")
                transform_and_count(nc, s)
            g_held = ExitStack()
            s.g_t = sb("g_t", [C1, H1, NP], where=g_held)
            attend_by_head(nc, s, bias1)
        with ExitStack() as layer2:
            s.h2_hi = sb("h2_hi", [P, NT, D + 4], F32R, where=layer2, side="right")
            s.h2_lo = sb("h2_lo", [P, NT, D + 4], F32R, where=layer2, side="right")
            transform_again(nc, s, w2, att2)
            g_held.close()
            s.prob2 = sb("prob2", [P, NT, NP], where=layer2, side="right")
            attention_again(nc, s)
            mix_and_route(nc, s, x, bias2, wg, we, bg, be)
        with ExitStack() as routing:
            s.tiles = sb("tiles", [1, E], I32, where=routing)
            s.starts = sb("starts", [1, E], I32, where=routing)
            s.list_i = sb("list_i", [P, LIST], I32, where=routing)
            s.gates_hi = sb("gates_hi", [E, NP], F32R, where=routing)
            s.gates_lo = sb("gates_lo", [E, NP], F32R, where=routing)
            s.b2_hi = sb("b2_hi", [E, D], F32R, where=routing)
            s.b2_lo = sb("b2_lo", [E, D], F32R, where=routing)
            plan_experts(nc, s, eb2)
            run_experts(nc, s, ew1, eb1, ew2)
            finish(nc, s, out)


def kernel(**inputs):
    import numpy as np
    import concourse.bacc as bacc
    from concourse.bass_utils import run_bass_kernel_spmd

    def edges(ends):
        padded = np.full(ET * P, -1, np.int32)
        padded[:EDGES] = ends
        return padded.reshape(ET, P).T

    def columns(a):
        return a.reshape(KD, P).T

    a = {name: np.asarray(value) for name, value in inputs.items()}
    gnn = {name[7:]: value for name, value in a.items() if name.startswith("L0_gnn_")}
    ffn = {name[7:]: value for name, value in a.items() if name.startswith("L0_ffn_")}
    x = np.zeros((NP, D), np.float32)
    x[:N] = a["x"]
    laid = {
        "x": x,
        "edge_src": edges(a["src"]),
        "edge_dst": edges(a["dst"]),
        "w1": gnn["W1"],
        "att1": np.stack([columns(gnn["a_src1"]), columns(gnn["a_dst1"])], 1),
        "bias1": gnn["b1"].reshape(H1, C1).T,
        "w2": gnn["W2"],
        "att2": np.concatenate([gnn["a_src2"], gnn["a_dst2"]], 1),
        "bias2": gnn["b2"].reshape(1, D),
        "wg": ffn["Wg"],
        "we": ffn["We"],
        "bg": ffn["bg"].reshape(1, G),
        "be": ffn["be"].reshape(1, E),
        "ew1": ffn["W1"].reshape(E * D, HID),
        "eb1": ffn["b1"].reshape(E, HID),
        "ew2": ffn["W2"].reshape(E * HID, D),
        "eb2": ffn["b2"].reshape(E, D),
    }
    laid = {f"in_{name}": np.ascontiguousarray(value) for name, value in laid.items()}
    nc = bacc.Bacc("TRN2", target_bir_lowering=False, num_devices=1)
    args = [nc.dram_tensor(name, value.shape, mybir.dt.from_np(value.dtype), kind="ExternalInput").ap()
            for name, value in laid.items()]
    out = nc.dram_tensor("out_nodes", (N, D), F32, kind="ExternalOutput")
    program(nc, *args, out.ap())
    ran = run_bass_kernel_spmd(nc, [laid], core_ids=[0])
    return ran.results[0]["out_nodes"]
```

```python
import concourse.bass as bass
from concourse import mybir
from contextlib import ExitStack

F32 = mybir.dt.float32
F32R = mybir.dt.float32r
BF16 = mybir.dt.bfloat16
I32 = mybir.dt.int32
I16 = mybir.dt.int16
U16 = mybir.dt.uint16
ALU = mybir.AluOpType
ACT = mybir.ActivationFunctionType
AX = mybir.AxisListType

P = 128
N = 1250
NT = -(-N // P)
NP = NT * P
TAIL = N - (NT - 1) * P
D = 768
KD = D // P
HALF = D // 2
EDGES = 20000
EP = -(-EDGES // (2 * P))
ET = 2 * EP
H1 = 8
C1 = D // H1
G = 4
EG = 8
E = G * EG
RC = G + E
TW = D + E
ROWS = NP + P
KG = 2
KE = 4
PAIRS = N * KG * KE
GATE_MIN = 1e-6
MIN_TILES = 1
LEAD = 2
AHEAD = 4
EL = E + AHEAD
LISTED = LEAD + PAIRS // P + 1 + MIN_TILES * E + NT
LIST = LISTED + NT
HID = 384
KH = HID // P
ROW = KD * HID
PIECE = ROW // 3
RING = 4
SLOPE = 0.2
LN_EPS = 1e-5
NOT_A_NEIGHBOUR = -1e30
BANK = 512
PARTS = tuple((at, min(BANK, NP - at)) for at in range(0, NP, BANK))


class Shared:
    pass


def semaphore(nc, s, name):
    s.early.append(nc.alloc_semaphore(name=name))
    return s.early[-1]


def node_features(nc, s, x, w1, edge_src, edge_dst, att1):
    with ExitStack() as ctx:
        def sb(name, shape, dt=F32):
            return ctx.enter_context(nc.sbuf_tensor(name, shape, dt))

        def sem(name):
            return semaphore(nc, s, name)

        xs = sb("xs", [P, NT, D])
        w1_raw = sb("w1_raw", [P, KD, D])
        w1_t = sb("w1_t", [P, KD, D])
        att_col = sb("att_col", [P, 2, KD])
        att_low = sb("att_low", [P, 2, KD, H1])
        att_diag = sb("att_diag", [P, KD, 2, H1])
        wa = sb("wa", [P, KD, 2 * H1])
        stats = sb("stats", [P, NT, 2, 6])
        mv = sb("mv", [P, NT, 2])
        veps = sb("veps", [P, NT])
        rstd = sb("rstd", [P, 4, NT])
        xn = sb("xn", [P, 2, D])
        al_rows = sb("al_rows", [2 * H1, NP])
        edge_i = sb("edge_i", [P, 2, ET], I32)
        dst_hi = sb("dst_hi", [P, ET])
        tile_ids_i = sb("tile_ids_i", [P, 2], I32)
        tile_ids = sb("tile_ids", [P, 2])
        tile_rev = sb("tile_rev", [P, 2])
        block_i = sb("block_i", [P, NT], I32)
        block_lo = s.block_col
        block_hi = sb("block_hi", [P, NT])
        tmax = sb("tmax", [P, 2])
        tmin = sb("tmin", [P, 2])
        hit = sb("hit", [P, 2, NT])
        ge = sb("ge", [P, 2, NT])
        span = sb("span", [P, 2, 2 * NT])
        span_col = sb("span_col", [2 * NT, 1])
        span_row = sb("span_row", [1, 2 * NT])
        span_fix = sb("span_fix", [1, 2 * NT])
        span_i = sb("span_i", [1, 2 * NT], I32)

        ps_x = ctx.enter_context(nc.psum_tensor("ps_x", [P, 2, 2, 512], F32))
        ps_al = ctx.enter_context(nc.psum_tensor("ps_al", [P, 3, 512], F32))
        ps_m = ctx.enter_context(nc.psum_tensor("ps_m", [P, 512], F32))

        x_in, w_in, e_in, a_in = sem("x_in"), sem("w_in"), sem("e_in"), sem("a_in")
        consts, dve_step, edge_step = sem("consts"), sem("dve_step"), sem("edge_step")
        pe_edges, pe_w1t, w1t_kept = sem("pe_edges"), sem("pe_w1t"), sem("w1t_kept")
        diag_low = sem("diag_low")
        diag, pe_wa, wa_kept = sem("diag"), sem("pe_wa"), sem("wa_kept")
        sqrt_done, normed, pe_xt, xt_kept = sem("sqrt_done"), sem("normed"), sem("pe_xt"), sem("xt_kept")
        pe_al, al_kept, pe_alc, stored = sem("pe_al"), sem("al_kept"), sem("pe_alc"), sem("stored")
        split_hi = sem("split_hi")
        id_done, stat_done = sem("id_done"), sem("stat_done")

        with nc.Block() as block:
            @block.sync
            def _(sp):
                sp.dma_start(edge_i[:, 0], edge_src).then_inc(e_in, 16)
                sp.dma_start(edge_i[:, 1], edge_dst).then_inc(e_in, 16)
                sp.dma_start(xs[:, :, :], x.rearrange("(t p) d -> p t d", p=P)).then_inc(x_in, 16)
                sp.wait_ge(al_kept, 3)
                sp.dma_start(s.al_dram.ap(), al_rows[:, :]).then_inc(stored, 16)
                sp.wait_ge(stored, 16)

            @block.gpsimd
            def _(pool):
                pool.dma_start(att_col[:, :, :], att1).then_inc(a_in, 16)
                nc.gpsimd.memset(s.ident[:, :], 0.0).then_inc(id_done, 1)
                nc.gpsimd.iota(tile_ids_i[:, :], [[P, 2]], base=0, channel_multiplier=1).then_inc(consts, 1)
                nc.gpsimd.iota(block_i[:, :], [[P, NT]], base=0, channel_multiplier=0).then_inc(consts, 1)
                nc.gpsimd.iota(s.column[:, :], [[1, NP]], base=0, channel_multiplier=0).then_inc(consts, 1)
                pool.wait_ge(id_done, 1)
                nc.gpsimd.affine_select(out=s.ident[:, :], in_=s.ident[:, :], compare_op=ALU.not_equal,
                                        fill=1.0, base=0, pattern=[[-1, P]],
                                        channel_multiplier=1).then_inc(consts, 1)
                pool.wait_ge(a_in, 16)
                for a in range(2):
                    nc.gpsimd.affine_select(out=att_low[:, a], compare_op=ALU.is_ge, fill=0.0,
                                            in_=att_col[:, a].unsqueeze(2).broadcast_to([P, KD, H1]),
                                            base=0, pattern=[[P, KD], [-C1, H1]],
                                            channel_multiplier=1).then_inc(diag_low, 1)
                pool.wait_ge(diag_low, 2)
                for a in range(2):
                    nc.gpsimd.affine_select(out=att_diag[:, :, a, :], in_=att_low[:, a], compare_op=ALU.is_ge,
                                            fill=0.0, base=C1 - 1, pattern=[[-P, KD], [C1, H1]],
                                            channel_multiplier=-1).then_inc(diag, 1)

            @block.vector
            def _(dve):
                step = [0]

                def then(ins):
                    step[0] += 1
                    ins.then_inc(dve_step, 1)
                    dve.wait_ge(dve_step, step[0])

                nc.vector.memset(tmax[:, :], -1.0)
                then(nc.vector.memset(tmin[:, :], 2.0 * NP))
                dve.wait_ge(e_in, 32)
                nc.vector.tensor_copy(s.src_f[:, :], edge_i[:, 0])
                then(nc.vector.tensor_copy(s.dst_f[:, :], edge_i[:, 1]))
                nc.vector.tensor_scalar(dst_hi[:, :], s.dst_f[:, :], 0.0, 4.0 * NP, ALU.is_lt, ALU.mult)
                dve.wait_ge(consts, 4)
                nc.vector.tensor_copy(tile_ids[:, :], tile_ids_i[:, :])
                nc.vector.tensor_copy(block_lo[:, :], block_i[:, :])
                then(nc.vector.memset(span[:, :, :], 0.0))
                nc.vector.tensor_scalar(block_hi[:, :], block_lo[:, :], float(P - 1), None, ALU.add)
                nc.vector.tensor_scalar(tile_rev[:, :], tile_ids[:, :], -1.0, float(ET), ALU.mult, ALU.add)
                nc.vector.tensor_scalar(tile_ids[:, :], tile_ids[:, :], 1.0, None, ALU.add)
                nc.vector.tensor_tensor(dst_hi[:, :], dst_hi[:, :], s.dst_f[:, :],
                                        ALU.add).then_inc(edge_step, 1)
                dve.wait_ge(pe_edges, 1)
                rest = ET - P
                nc.vector.tensor_reduce(tmax[:, 0:1], ps_m[:, 0:P], AX.X, ALU.max)
                nc.vector.tensor_reduce(tmax[0:rest, 1:2], ps_m[0:rest, P:2 * P], AX.X, ALU.max)
                nc.vector.tensor_reduce(tmin[:, 0:1], ps_m[:, 2 * P:3 * P], AX.X, ALU.min)
                then(nc.vector.tensor_reduce(tmin[0:rest, 1:2], ps_m[0:rest, 3 * P:4 * P], AX.X, ALU.min))
                for c in range(2):
                    nc.vector.tensor_scalar(ge[:, c], block_lo[:, :], tmax[:, c:c + 1], None, ALU.is_le)
                then(nc.vector.memset(veps[:, :], 0.0))
                for c in range(2):
                    nc.vector.scalar_tensor_tensor(hit[:, c], block_hi[:, :], tmin[:, c:c + 1], ge[:, c],
                                                   ALU.is_ge, ALU.mult)
                then(nc.vector.memset(veps[:, :], 0.0))
                for c in range(2):
                    nc.vector.tensor_scalar(span[:, c, 0:NT], hit[:, c], tile_ids[:, c:c + 1], None, ALU.mult)
                    last = nc.vector.tensor_scalar(span[:, c, NT:2 * NT], hit[:, c], tile_rev[:, c:c + 1],
                                                   None, ALU.mult)
                last.then_inc(edge_step, 1)
                dve.wait_ge(pe_edges, 2)
                nc.vector.tensor_reduce(span_col[:, :], ps_m[0:2 * NT, 0:2 * P], AX.X,
                                        ALU.max).then_inc(edge_step, 1)
                dve.wait_ge(pe_edges, 3)
                then(nc.vector.tensor_scalar(span_row[:, :], ps_m[0:1, 0:2 * NT], 1.0, None, ALU.max))
                then(nc.vector.tensor_scalar(span_fix[:, 0:NT], ps_m[0:1, NT:2 * NT], -1.0, float(ET),
                                             ALU.mult, ALU.add))
                then(nc.vector.tensor_scalar(span_fix[:, NT:2 * NT], span_row[:, 0:NT], -1.0, None, ALU.add))
                then(nc.vector.tensor_tensor(span_fix[:, 0:NT], span_fix[:, 0:NT], span_fix[:, NT:2 * NT],
                                             ALU.min))
                nc.vector.tensor_copy(span_i[:, 0:NT], span_fix[:, 0:NT])
                then(nc.vector.tensor_scalar(span_i[:, NT:2 * NT], span_row[:, 0:NT], 1.0, None, ALU.add))
                nc.vector.tensor_scalar(s.ranges[:, :], span_i[:, :], 1, None, ALU.arith_shift_right)
                for j in range(KD):
                    dve.wait_ge(pe_w1t, j + 1)
                    nc.vector.tensor_copy(w1_t[:, j, :].rearrange("p (b d) -> p b d", b=2),
                                          ps_x[:, j % 2, :, 0:HALF]).then_inc(w1t_kept, 1)
                dve.wait_ge(x_in, 16)
                with dve.Fori(0, NT) as t:
                    for half in range(2):
                        nc.vector.bn_stats(stats[:, bass.ds(t, 1), half, :],
                                           xs[:, bass.ds(t, 1), half * HALF:(half + 1) * HALF]).then_inc(stat_done, 1)
                dve.wait_ge(stat_done, 2 * NT)
                for t in range(NT):
                    last = nc.vector.bn_aggr(mv[:, t, :], stats[:, t, :, :].rearrange("p a b -> p (a b)"))
                then(last)
                nc.vector.tensor_scalar(veps[:, :], mv[:, :, 1], LN_EPS, None, ALU.add).then_inc(stat_done, 1)
                dve.wait_ge(sqrt_done, 1)
                then(nc.vector.reciprocal(rstd[:, 1], rstd[:, 0]))
                then(nc.vector.tensor_tensor(rstd[:, 2], rstd[:, 1], rstd[:, 1], ALU.mult))
                then(nc.vector.tensor_tensor(rstd[:, 2], rstd[:, 2], veps[:, :], ALU.mult))
                then(nc.vector.tensor_scalar(rstd[:, 2], rstd[:, 2], -0.5, 1.5, ALU.mult, ALU.add))
                then(nc.vector.tensor_tensor(rstd[:, 3], rstd[:, 1], rstd[:, 2], ALU.mult))
                with dve.Fori(0, NT // 2) as i:
                    for u in range(2):
                        t = 2 * i + u
                        dve.wait_ge(xt_kept, t + 1)
                        nc.vector.tensor_scalar(xn[:, u, :], xs[:, bass.ds(t, 1), :].rearrange("p o d -> p (o d)"),
                                                mv[:, bass.ds(t, 1), 0:1].rearrange("p o d -> p (o d)"),
                                                rstd[:, 3, bass.ds(t, 1)], ALU.subtract, ALU.mult).then_inc(normed, 1)
                dve.wait_ge(split_hi, KD)
                for k in range(KD):
                    nc.vector.tensor_tensor(s.w1_lo[:, k, :], w1_raw[:, k, :], s.w1_hi[:, k, :].bitcast(F32),
                                            ALU.subtract)
                dve.wait_ge(pe_alc, 1)
                nc.vector.tensor_copy(s.al_col[:, :, :], ps_m[:, 0:NT * 16].rearrange("p (t c) -> p t c", c=16))

            @block.scalar
            def _(act):
                act.dma_start(w1_raw[:, :, :], w1.rearrange("(k p) c -> p k c", p=P)).then_inc(w_in, 16)
                act.sem_inc(xt_kept, 2)
                act.wait_ge(w_in, 16)
                for k in range(KD):
                    nc.scalar.activation(s.w1_hi[:, k, :], w1_raw[:, k, :], ACT.Copy).then_inc(split_hi, 1)
                act.wait_ge(pe_wa, 1)
                nc.scalar.activation(wa[:, :, :], ps_m[:, 0:KD * 16].rearrange("p (k c) -> p k c", c=16),
                                     ACT.Copy).then_inc(wa_kept, 1)
                act.wait_ge(stat_done, 2 * NT + 1)
                nc.scalar.activation(rstd[:, 0], veps[:, :], ACT.Sqrt).then_inc(sqrt_done, 1)
                with act.Fori(0, NT // 2) as i:
                    for u in range(2):
                        t = 2 * i + u
                        act.wait_ge(pe_xt, t + 1)
                        nc.scalar.activation(
                            s.x_t[:, bass.ds(t, 1), :, :].rearrange("p o (b k) n -> p (o b) (k n)", b=2),
                            ps_x[:, u, :, 0:HALF], ACT.Copy).then_inc(xt_kept, 1)
                for c, (at, width) in enumerate(PARTS):
                    act.wait_ge(pe_al, c + 1)
                    nc.scalar.activation(al_rows[:, at:at + width], ps_al[0:16, c, 0:width],
                                         ACT.Copy).then_inc(al_kept, 1)

            @block.tensor
            def _(pe):
                pe.wait_ge(consts, 4)
                pe.wait_ge(edge_step, 1)
                for c, src in enumerate((s.dst_f, dst_hi)):
                    nc.tensor.transpose(ps_m[:, 2 * c * P:(2 * c + 1) * P], src[:, 0:P], s.ident[:, :])
                    last = nc.tensor.transpose(ps_m[0:ET - P, (2 * c + 1) * P:(2 * c + 2) * P], src[:, P:ET],
                                               s.ident[:, :])
                last.then_inc(pe_edges, 1)
                pe.wait_ge(edge_step, 2)
                for c in range(2):
                    last = nc.tensor.transpose(ps_m[0:2 * NT, c * P:(c + 1) * P], span[:, c, :], s.ident[:, :])
                last.then_inc(pe_edges, 1)
                pe.wait_ge(edge_step, 3)
                nc.tensor.transpose(ps_m[0:1, 0:2 * NT], span_col[:, :],
                                    s.ident[0:2 * NT, 0:2 * NT]).then_inc(pe_edges, 1)
                pe.wait_ge(w_in, 16)
                for j in range(KD):
                    if j >= 2:
                        pe.wait_ge(w1t_kept, j - 1)
                    for k in range(KD):
                        last = nc.tensor.transpose(ps_x[:, j % 2, k // 3, (k % 3) * P:(k % 3 + 1) * P],
                                                   w1_raw[:, k, j * P:(j + 1) * P], s.ident[:, :])
                    last.then_inc(pe_w1t, 1)
                pe.wait_ge(w1t_kept, KD)
                pe.wait_ge(diag, 2)
                for k in range(KD):
                    for j in range(KD):
                        last = nc.tensor.matmul(ps_m[:, k * 16:(k + 1) * 16], w1_t[:, j, k * P:(k + 1) * P],
                                                att_diag[:, j, :, :].rearrange("p s h -> p (s h)"),
                                                start=(j == 0), stop=(j == KD - 1))
                last.then_inc(pe_wa, 1)
                with pe.Fori(0, NT // 2) as i:
                    for u in range(2):
                        t = 2 * i + u
                        pe.wait_ge(normed, t + 1)
                        pe.wait_ge(xt_kept, t + 1)
                        for k in range(KD):
                            last = nc.tensor.transpose(ps_x[:, u, k // 3, (k % 3) * P:(k % 3 + 1) * P],
                                                       xn[:, u, k * P:(k + 1) * P], s.ident[:, :])
                        last.then_inc(pe_xt, 1)
                pe.wait_ge(wa_kept, 1)
                pe.wait_ge(xt_kept, NT + 2)
                for c, (at, width) in enumerate(PARTS):
                    for k in range(KD):
                        last = nc.tensor.matmul(ps_al[0:16, c, 0:width], wa[:, k, :],
                                                s.x_t[:, at // P:(at + width) // P, k, :],
                                                start=(k == 0), stop=(k == KD - 1))
                    last.then_inc(pe_al, 1)
                pe.wait_ge(al_kept, 3)
                for t in range(NT):
                    last = nc.tensor.transpose(ps_m[:, t * 16:(t + 1) * 16], al_rows[:, t * P:(t + 1) * P],
                                               s.ident[0:16, 0:16])
                last.then_inc(pe_alc, 1)


def transform_and_count(nc, s):
    with ExitStack() as ctx:
        def sb(name, shape, dt=F32):
            return ctx.enter_context(nc.sbuf_tensor(name, shape, dt))

        def sem(name):
            return ctx.enter_context(nc.semaphore(name))

        HOTS = 2

        al_src = sb("al_src", [P, H1, NP])
        xt_hi = sb("xt_hi", [P, 2, D], F32R)
        xt_lo = sb("xt_lo", [P, 2, D], F32R)
        counts = sb("counts", [P, NP])
        mask = sb("mask", [P, 2, NP], BF16)
        junk = sb("junk", [P, 2, NP], BF16)
        one_src = sb("one_src", [P, HOTS, 2, NP], BF16)
        one_dst = sb("one_dst", [P, HOTS, 2, P], BF16)
        dst_rel = sb("dst_rel", [P, 2, ET])
        zeros = sb("zeros", [P, P], BF16)
        best = sb("best", [P, 2, H1])
        ps_h = ctx.enter_context(nc.psum_tensor("ps_h", [P, 2, 512], F32))
        ps_c = ctx.enter_context(nc.psum_tensor("ps_c", [P, 3, 512], F32))
        ps_t = ctx.enter_context(nc.psum_tensor("ps_t", [P, 3, 512], F32))

        al_in, zeroed, ones_set = sem("al_in"), sem("zeroed"), sem("ones_set")
        xhi_made, xlo_made, h_summed, h_kept = sem("xhi_made"), sem("xlo_made"), sem("h_summed"), sem("h_kept")
        onehot_made, onehot_used, rel_made = sem("onehot_made"), sem("onehot_used"), sem("rel_made")
        counted, counts_kept = sem("counted"), sem("counts_kept")
        turned, turned_kept = sem("turned"), sem("turned_kept")
        mask_made, maxed, best_kept = sem("mask_made"), sem("maxed"), sem("best_kept")
        mask_out = [sem("mask_out0"), sem("mask_out1")]

        with nc.Block() as block:
            @block.sync
            def _(sp):
                sp.dma_start(al_src[:, :, :].rearrange("p h n -> p (h n)"),
                             s.al_dram.ap()[0:H1, :].rearrange("(o h) n -> o (h n)", o=1)
                             .broadcast_to([P, H1 * NP])).then_inc(al_in, 16)
                with sp.Fori(0, NT // 2) as i:
                    for u in range(2):
                        t = 2 * i + u
                        sp.wait_ge(mask_made, t + 2)
                        sp.dma_start(s.mask_dram.ap()[bass.ds(t, 1), :, :].rearrange("o p n -> (o p) n"),
                                     mask[:, u, :]).then_inc(mask_out[u], 16)
                for u in range(2):
                    sp.wait_ge(mask_out[u], 16 * (NT // 2))

            @block.gpsimd
            def _(pool):
                nc.gpsimd.memset(s.h_ext[:, :, :, C1:C1 + 1], 1.0).then_inc(ones_set, 1)
                with pool.Fori(0, NT // 2) as i:
                    for u in range(2):
                        t = 2 * i + u
                        pool.wait_ge(xhi_made, t + 1)
                        nc.gpsimd.tensor_tensor(
                            xt_lo[:, u, :], s.x_t[:, bass.ds(t, 1), :, :].rearrange("p o k n -> p (o k n)"),
                            xt_hi[:, u, :].bitcast(F32), ALU.subtract).then_inc(xlo_made, 1)

            @block.scalar
            def _(act):
                act.sem_inc(h_kept, 2)
                act.sem_inc(turned_kept, 1)
                act.sem_inc(counts_kept, 1)
                with act.Fori(0, NT // 2) as i:
                    for u in range(2):
                        t = 2 * i + u
                        act.wait_ge(h_kept, t + 2)
                        nc.scalar.activation(
                            xt_hi[:, u, :], s.x_t[:, bass.ds(t, 1), :, :].rearrange("p o k n -> p (o k n)"),
                            ACT.Copy).then_inc(xhi_made, 1)
                        act.wait_ge(counted, t + 1)
                        act.wait_ge(mask_made, t + 1)
                        act.wait_ge(turned_kept, t + 1)
                        nc.scalar.activation(counts[:, 0:1024], ps_c[:, 0:2, :].rearrange("p a n -> p (a n)"),
                                             ACT.Copy)
                        nc.scalar.activation(counts[:, 1024:NP], ps_c[:, 2, 0:256], ACT.Copy).then_inc(counts_kept, 1)
                        act.wait_ge(h_summed, t + 1)
                        for half in range(2):
                            last = nc.scalar.activation(
                                s.h_ext[:, bass.ds(t, 1), 4 * half:4 * half + 4, 0:C1]
                                .rearrange("p o h c -> p (o h) c"),
                                ps_h[:, half, 0:HALF].rearrange("p (h c) -> p h c", c=C1), ACT.Copy)
                        last.then_inc(h_kept, 1)
                        act.wait_ge(turned, t + 1)
                        nc.scalar.activation(
                            s.count[:, 0:8, bass.ds(t * P, P)],
                            ps_t[:, 0:2, :].rearrange("p a (b n) -> p (a b) n", n=P), ACT.Copy)
                        nc.scalar.activation(
                            s.count[:, 8:NT, bass.ds(t * P, P)],
                            ps_t[:, 2, 0:2 * P].rearrange("p (b n) -> p b n", n=P),
                            ACT.Copy).then_inc(turned_kept, 1)

            @block.vector
            def _(dve):
                nc.vector.memset(zeros[:, :], 0.0).then_inc(zeroed, 1)
                dve.sem_inc(mask_made, 1)
                made = dve.alloc_register("made_dve")
                dve.reg_mov(made, 0)
                freed = dve.alloc_register("freed")
                dve.reg_mov(freed, 0)

                def one_hots(t, u):
                    nc.vector.tensor_scalar(dst_rel[:, u, :], s.dst_f[:, :], s.block_col[:, bass.ds(t, 1)],
                                            None, ALU.subtract).then_inc(rel_made, 1)
                    dve.wait_ge(rel_made, t + 1)
                    first = dve.value_load(s.ranges[0:1, bass.ds(t, 1)], min_val=0, max_val=EP - 1)
                    end = dve.value_load(s.ranges[0:1, bass.ds(t + NT, 1)], min_val=1, max_val=EP)
                    with dve.Fori(first, end) as e:
                        m = dve.snap(made)
                        dve.wait_ge(onehot_used, m + 1)
                        for q in range(2):
                            nc.vector.tensor_scalar(one_src[:, m % HOTS, q, :], s.column[:, :],
                                                    s.src_f[:, bass.ds(2 * e + q, 1)], None, ALU.is_equal)
                            last = nc.vector.tensor_scalar(one_dst[:, m % HOTS, q, :], s.column[:, 0:P],
                                                           dst_rel[:, u, bass.ds(2 * e + q, 1)], None,
                                                           ALU.is_equal)
                        last.then_inc(onehot_made, 1)
                        dve.reg_add(made, made, 1)

                def largest(t, i, u, first=False):
                    dve.wait_ge(counts_kept, t + 2)
                    if not first:
                        dve.wait_ge(mask_out[u], 16 * i)
                    nc.vector.tensor_scalar(mask[:, u, :], counts[:, :], 0.0, NOT_A_NEIGHBOUR,
                                            ALU.is_equal, ALU.mult).then_inc(mask_made, 1)
                    dve.wait_ge(al_in, 16)
                    dve.wait_ge(mask_made, t + 2)
                    for h in range(H1):
                        if h >= 2:
                            dve.reg_add(freed, freed, 1)
                            now = dve.snap(freed)
                            dve.wait_ge(al_in, 16)
                            dve.wait_ge(maxed, now)
                        nc.vector.tensor_tensor_reduce(
                            junk[:, h % 2, :], mask[:, u, :], al_src[:, h, :], 1.0,
                            2.0 * NOT_A_NEIGHBOUR, ALU.add, ALU.max, best[:, u, h:h + 1]).then_inc(maxed, 1)
                    dve.reg_add(freed, freed, 2)
                    dve.wait_ge(maxed, (t + 1) * H1)
                    nc.vector.tensor_copy(s.al_max[:, bass.ds(t, 1), :].rearrange("p o h -> p (o h)"),
                                          best[:, u, :]).then_inc(best_kept, 1)
                    dve.wait_ge(best_kept, t + 1)

                one_hots(0, 0)
                one_hots(1, 1)
                largest(0, 0, 0, first=True)
                one_hots(2, 0)
                largest(1, 0, 1, first=True)
                with dve.Fori(1, NT // 2 - 1) as i:
                    one_hots(2 * i + 1, 1)
                    largest(2 * i, i, 0)
                    one_hots(2 * i + 2, 0)
                    largest(2 * i + 1, i, 1)
                one_hots(NT - 1, 1)
                largest(NT - 2, NT // 2 - 1, 0)
                largest(NT - 1, NT // 2 - 1, 1)

            @block.tensor
            def _(pe):
                pe.sem_inc(onehot_used, HOTS)
                pe.wait_ge(zeroed, 1)
                made = pe.alloc_register("made_pe")
                pe.reg_mov(made, 0)
                with pe.Fori(0, NT // 2) as i:
                    for u in range(2):
                        t = 2 * i + u
                        first = pe.value_load(s.ranges[0:1, bass.ds(t, 1)], min_val=0, max_val=EP - 1)
                        end = pe.value_load(s.ranges[0:1, bass.ds(t + NT, 1)], min_val=1, max_val=EP)
                        pe.wait_ge(counts_kept, t + 1)
                        for c, (at, width) in enumerate(PARTS):
                            nc.tensor.matmul(ps_c[:, c, 0:width], zeros[:, :], zeros[:, 0:1].broadcast_to([P, width]),
                                             start=True, stop=False)
                        with pe.Fori(first, end) as e:
                            m = pe.snap(made)
                            pe.wait_ge(onehot_made, m + 1)
                            for q in range(2):
                                for c, (at, width) in enumerate(PARTS):
                                    last = nc.tensor.matmul(ps_c[:, c, 0:width], one_dst[:, m % HOTS, q, :],
                                                            one_src[:, m % HOTS, q, at:at + width],
                                                            start=False, stop=False)
                            last.then_inc(onehot_used, 1)
                            pe.reg_add(made, made, 1)
                        for c, (at, width) in enumerate(PARTS):
                            last = nc.tensor.matmul(ps_c[:, c, 0:width], zeros[:, :],
                                                    zeros[:, 0:1].broadcast_to([P, width]),
                                                    start=False, stop=True)
                        last.then_inc(counted, 1)
                        pe.wait_ge(xlo_made, t + 1)
                        pe.wait_ge(h_kept, t + 2)
                        for half in range(2):
                            at = half * HALF
                            for k in range(KD):
                                hi, lo = (w[:, u, k * P:(k + 1) * P] for w in (xt_hi, xt_lo))
                                for n, (a, b) in enumerate(((hi, s.w1_hi), (hi, s.w1_lo), (lo, s.w1_hi))):
                                    last = nc.tensor.matmul(ps_h[:, half, 0:HALF], a, b[:, k, at:at + HALF],
                                                            start=(k == 0 and n == 0),
                                                            stop=(k == KD - 1 and n == 2))
                        last.then_inc(h_summed, 1)
                        pe.wait_ge(counts_kept, t + 2)
                        pe.wait_ge(turned_kept, t + 1)
                        for b in range(NT):
                            last = nc.tensor.transpose(ps_t[:, b // 4, (b % 4) * P:(b % 4 + 1) * P],
                                                       counts[:, b * P:(b + 1) * P], s.ident[:, :])
                        last.then_inc(turned, 1)

def attend_by_head(nc, s, bias1):
    with ExitStack() as ctx:
        def sb(name, shape, dt=F32):
            return ctx.enter_context(nc.sbuf_tensor(name, shape, dt))

        def sem(name):
            return ctx.enter_context(nc.semaphore(name))

        rel = sb("rel", [P, NT, 2, H1])
        top = sb("top", [P, 2, NT, H1])
        src_small = sb("src_small", [P, NT, H1])
        rel_rows = sb("rel_rows", [2 * H1, NP])
        bias_col = sb("bias_col", [C1, H1])
        bias_now = sb("bias_now", [C1, 1])
        h_head = sb("h_head", [P, 2, NT, C1 + 1])
        steep = sb("steep", [P, 2, NP])
        flat = sb("flat", [P, 2, NP])
        ex = sb("ex", [P, 2, NP])
        ey = sb("ey", [P, 2, NP])
        prob = sb("prob", [P, 2, NP])
        out_t = sb("out_t", [C1 + 1, 2, NP])
        scale_t = sb("scale_t", [C1, 2, NP])
        neg_t = sb("neg_t", [C1, NP])
        z_rows = sb("z_rows", [NT, 2, N // NT])

        ps_o = [ctx.enter_context(nc.psum_tensor(f"ps_o{u}", [P, 3, 512], F32)) for u in range(2)]
        ps_r = ctx.enter_context(nc.psum_tensor("ps_r", [P, 512], F32))

        step, rel_made, rel_turned, rel_kept, rel_out = (sem("c_step"), sem("rel_made_2"), sem("rel_turned"),
                                                         sem("rel_kept"), sem("rel_out"))
        rows_in = [sem("rows_in0"), sem("rows_in1")]
        head_set, exped, joined, mixed = sem("head_set"), sem("exped"), sem("joined"), sem("mixed")
        out_kept, z_out, z_in, z_done, zi_out = (sem("out_kept"), sem("z_out"), sem("z_in"), sem("z_done"),
                                                 sem("zi_out"))
        scale_in = [sem("scale_in0"), sem("scale_in1")]
        neg_made, neg_exped, elued = sem("neg_made"), sem("neg_exped"), sem("elued")
        pool_step, bias_in, count_out = sem("pool_step"), sem("bias_in"), sem("count_out")
        WID = [min(width, N - at) for at, width in PARTS]

        with nc.Block() as block:
            @block.sync
            def _(sp):
                sp.dma_start(bias_col[:, :], bias1).then_inc(bias_in, 16)
                sp.dma_start(s.count_dram.ap(), s.count[:, :, :]).then_inc(count_out, 16)
                sp.wait_ge(rel_kept, 3)
                sp.dma_start(s.rel_dram.ap(), rel_rows[:, :]).then_inc(rel_out, 16)
                sp.wait_ge(rel_out, 16)

                def load_rows(h, u):
                    sp.dma_start(steep[:, u, :], s.rel_dram.ap()[bass.ds(h, 1), :].broadcast_to([P, NP])) \
                      .then_inc(rows_in[u], 16)
                    sp.dma_start(flat[:, u, :], s.rel_dram.ap()[bass.ds(h + H1, 1), :].broadcast_to([P, NP])) \
                      .then_inc(rows_in[u], 16)

                def reciprocal_sums(h, u):
                    sp.wait_ge(out_kept, h + 1)
                    sp.dma_start(s.z_dram.ap()[bass.ds(h, 1), :], out_t[C1:C1 + 1, u, 0:N]).then_inc(z_out, 16)
                    sp.wait_ge(z_out, 16 * h + 16)
                    sp.dma_start(z_rows[:, u, :], s.z_dram.ap()[bass.ds(h, 1), :]
                                 .rearrange("o (a b) -> (o a) b", a=NT)).then_inc(z_in, 16)
                    sp.wait_ge(z_done, 2 * h + 2)
                    sp.dma_start(s.zi_dram.ap()[bass.ds(h, 1), :].rearrange("o (a b) -> (o a) b", a=NT),
                                 z_rows[:, u, :]).then_inc(zi_out, 16)
                    sp.wait_ge(zi_out, 16 * h + 16)
                    sp.dma_start(scale_t[:, u, 0:N], s.zi_dram.ap()[bass.ds(h, 1), :].broadcast_to([C1, N])) \
                      .then_inc(scale_in[u], 16)

                load_rows(0, 0)
                load_rows(1, 1)
                reciprocal_sums(0, 0)
                with sp.Fori(0, H1 // 2 - 1) as i:
                    for u in range(2):
                        h = 2 * i + u
                        load_rows(h + 2, u)
                        sp.wait_ge(elued, h + 1)
                        reciprocal_sums(h + 1, 1 - u)
                reciprocal_sums(H1 - 1, 1)
                for u in range(2):
                    sp.wait_ge(scale_in[u], 16 * (H1 // 2))
                sp.wait_ge(count_out, 16)

            @block.gpsimd
            def _(pool):
                def stage_head(h, u):
                    nc.gpsimd.tensor_copy(h_head[:, u], s.h_ext[:, :, bass.ds(h, 1), :]
                                          .rearrange("p t o c -> p (t o) c")).then_inc(head_set, 1)

                steps = pool.alloc_register("pool_steps")
                pool.reg_mov(steps, 0)

                def then(ins):
                    ins.then_inc(pool_step, 1)
                    pool.reg_add(steps, steps, 1)
                    done = pool.snap(steps)
                    pool.wait_ge(bias_in, 16)
                    pool.wait_ge(pool_step, done)

                def finish(h, i, u):
                    pool.wait_ge(scale_in[u], 16 * i + 16)
                    then(nc.gpsimd.tensor_copy(bias_now[:, :], bias_col[:, bass.ds(h, 1)]))
                    then(nc.gpsimd.tensor_tensor(out_t[0:C1, u, 0:N], out_t[0:C1, u, 0:N], scale_t[:, u, 0:N],
                                                 ALU.mult))
                    then(nc.gpsimd.tensor_scalar(out_t[0:C1, u, 0:N], out_t[0:C1, u, 0:N], bias_now[:, 0:1],
                                                 None, ALU.add))
                    nc.gpsimd.tensor_scalar(neg_t[:, 0:N], out_t[0:C1, u, 0:N], 0.0, None,
                                            ALU.min).then_inc(neg_made, 1)
                    then(nc.gpsimd.tensor_scalar(scale_t[:, u, 0:N], out_t[0:C1, u, 0:N], 0.0, -1.0,
                                                 ALU.max, ALU.add))
                    pool.wait_ge(neg_exped, h + 1)
                    nc.gpsimd.tensor_tensor(s.g_t[:, bass.ds(h, 1), 0:N].rearrange("p o n -> p (o n)"),
                                            scale_t[:, u, 0:N], neg_t[:, 0:N], ALU.add).then_inc(elued, 1)
                    pool.wait_ge(elued, h + 2)

                nc.gpsimd.memset(s.g_t[:, :, N:NP], 0.0)
                pool.sem_inc(elued, 1)
                pool.wait_ge(bias_in, 16)
                stage_head(0, 0)
                stage_head(1, 1)
                with pool.Fori(0, H1 // 2 - 1) as i:
                    for u in range(2):
                        h = 2 * i + u
                        pool.wait_ge(mixed, (h + 1) * NT + 2)
                        stage_head(h + 2, u)
                        finish(h, i, u)

            @block.scalar
            def _(act):
                act.wait_ge(rel_turned, 1)
                for c, (at, width) in enumerate(PARTS):
                    act.wait_ge(rel_turned, c + 1)
                    nc.scalar.activation(rel_rows[:, at:at + width], ps_r[0:16, 0:width],
                                         ACT.Copy).then_inc(rel_kept, 1)
                act.wait_ge(step, 1)

                def keep_out(h, u):
                    act.wait_ge(mixed, (h + 1) * NT + 2)
                    if not (isinstance(h, int) and h == 0):
                        act.wait_ge(elued, h)
                    nc.scalar.activation(out_t[:, u, 0:1024].rearrange("p (a n) -> p a n", a=2),
                                         ps_o[u][0:C1 + 1, 0:2, :], ACT.Copy)
                    nc.scalar.activation(out_t[:, u, 1024:N], ps_o[u][0:C1 + 1, 2, 0:WID[2]],
                                         ACT.Copy).then_inc(out_kept, 1)

                def exp_negative(h):
                    act.wait_ge(neg_made, h + 1)
                    nc.scalar.activation(neg_t[:, 0:N], neg_t[:, 0:N], ACT.Exp).then_inc(neg_exped, 1)

                def exps(h, i, u, first):
                    act.wait_ge(rows_in[u], 32 * i + 32)
                    for t in range(NT):
                        act.wait_ge(joined, h * NT + t + 1)
                        nc.scalar.activation(ex[:, t % 2, 0:N], steep[:, u, 0:N], ACT.Exp,
                                             bias=s.al_col[:, t, bass.ds(h, 1)])
                        nc.scalar.activation(ey[:, t % 2, 0:N], flat[:, u, 0:N], ACT.Exp,
                                             bias=src_small[:, t, bass.ds(h, 1)]).then_inc(exped, 1)
                        if t == 2 and not first:
                            keep_out(h - 1, 1 - u)

                def head(h, i, u, first=False, second=False):
                    exps(h, i, u, first)
                    if not first and not second:
                        exp_negative(h - 2)

                head(0, 0, 0, first=True)
                head(1, 0, 1, second=True)
                with act.Fori(1, H1 // 2) as i:
                    for u in range(2):
                        head(2 * i + u, i, u)
                keep_out(H1 - 1, 1)
                exp_negative(H1 - 2)
                exp_negative(H1 - 1)

            @block.vector
            def _(dve):
                n = [0]

                def then(ins):
                    n[0] += 1
                    ins.then_inc(rel_made, 1)
                    dve.wait_ge(rel_made, n[0])

                src, dst = s.al_col[:, :, 0:H1], s.al_col[:, :, H1:2 * H1]
                then(nc.vector.tensor_tensor(top[:, 0], s.al_max[:, :, :], dst, ALU.add))
                then(nc.vector.scalar_tensor_tensor(top[:, 1], top[:, 0], SLOPE, top[:, 0], ALU.mult, ALU.max))
                then(nc.vector.scalar_tensor_tensor(top[:, 1], s.al_max[:, :, :], 0.5 * NOT_A_NEIGHBOUR, top[:, 1],
                                                    ALU.is_gt, ALU.mult))
                nc.vector.tensor_tensor(rel[:, :, 0, :], dst, top[:, 1], ALU.subtract)
                nc.vector.scalar_tensor_tensor(rel[:, :, 1, :], dst, SLOPE, top[:, 1], ALU.mult, ALU.subtract)
                nc.vector.tensor_scalar(src_small[:, :, :], src, SLOPE, None, ALU.mult).then_inc(step, 1)
                dve.wait_ge(step, 1)
                dve.sem_inc(joined, 2)

                def invert_sums(h, u):
                    dve.wait_ge(z_in, 16 * h + 16)
                    nc.vector.tensor_scalar(z_rows[:, u, :], z_rows[:, u, :], 1e-16, None,
                                            ALU.add).then_inc(z_done, 1)
                    dve.wait_ge(z_done, 2 * h + 1)
                    nc.vector.reciprocal(z_rows[:, u, :], z_rows[:, u, :]).then_inc(z_done, 1)

                def head(h, u, first=False):
                    for t in range(NT):
                        dve.wait_ge(exped, h * NT + t + 1)
                        nc.vector.scalar_tensor_tensor(ex[:, t % 2, 0:N], ey[:, t % 2, 0:N], 1.0,
                                                       ex[:, t % 2, 0:N], ALU.min, ALU.max).then_inc(step, 1)
                        dve.wait_ge(step, h * NT + t + 2)
                        dve.wait_ge(mixed, h * NT + t + 1)
                        nc.vector.scalar_tensor_tensor(prob[:, t % 2, 0:N], ex[:, t % 2, 0:N], 1.0,
                                                       s.count[:, t, 0:N], ALU.min,
                                                       ALU.mult).then_inc(joined, 1)
                        if t == 6 and not first:
                            invert_sums(h - 1, 1 - u)

                head(0, 0, first=True)
                head(1, 1)
                with dve.Fori(1, H1 // 2) as i:
                    for u in range(2):
                        head(2 * i + u, u)

                def finish(h, u):
                    v, e = out_t[0:C1, u, 0:N], neg_t[:, 0:N]
                    dve.wait_ge(scale_in[u], 16 * (H1 // 2))
                    then(nc.vector.tensor_tensor(v, v, scale_t[:, u, 0:N], ALU.mult))
                    then(nc.vector.tensor_scalar(v, v, bias_col[:, h:h + 1], None, ALU.add))
                    dve.wait_ge(elued, h + 1)
                    nc.vector.tensor_scalar(e, v, 0.0, None, ALU.min).then_inc(neg_made, 1)
                    dve.wait_ge(neg_exped, h + 1)
                    nc.vector.scalar_tensor_tensor(s.g_t[:, h, 0:N], e, -1.0, v, ALU.add,
                                                   ALU.max).then_inc(elued, 1)

                dve.wait_ge(bias_in, 16)
                finish(H1 - 2, 0)
                invert_sums(H1 - 1, 1)
                finish(H1 - 1, 1)

            @block.tensor
            def _(pe):
                pe.sem_inc(mixed, 2)
                pe.wait_ge(step, 1)
                for c, (at, width) in enumerate(PARTS):
                    if c:
                        pe.wait_ge(rel_kept, c)
                    for t in range(at // P, (at + width) // P):
                        last = nc.tensor.transpose(ps_r[0:16, t * P - at:(t + 1) * P - at],
                                                   rel[:, t, :, :].rearrange("p a h -> p (a h)"), s.ident[:, :])
                    last.then_inc(rel_turned, 1)

                def head(h, u, early=False):
                    pe.wait_ge(head_set, h + 1)
                    if not early:
                        pe.wait_ge(out_kept, h - 1)
                    for t in range(NT):
                        pe.wait_ge(joined, h * NT + t + 3)
                        for c in range(3):
                            last = nc.tensor.matmul(ps_o[u][0:C1 + 1, c, 0:WID[c]], h_head[:, u, t, :],
                                                    prob[:, t % 2, 512 * c:512 * c + WID[c]],
                                                    start=(t == 0), stop=(t == NT - 1))
                        last.then_inc(mixed, 1)

                head(0, 0, early=True)
                head(1, 1, early=True)
                with pe.Fori(1, H1 // 2) as i:
                    for u in range(2):
                        head(2 * i + u, u)

def transform_again(nc, s, w2, att2):
    with ExitStack() as ctx:
        def sb(name, shape, dt=F32):
            return ctx.enter_context(nc.sbuf_tensor(name, shape, dt))

        def sem(name):
            return ctx.enter_context(nc.semaphore(name))

        RAW = 4
        w2_raw = sb("w2_raw", [C1, RAW, D])
        w2_hi = sb("w2_hi", [C1, H1, D], F32R)
        w2_lo = sb("w2_lo", [C1, H1, D], F32R)
        g_hi = sb("g_hi", [C1, 2, H1, P], F32R)
        g_lo = sb("g_lo", [C1, 2, H1, P], F32R)
        att = sb("att", [P, 2, D])
        junk = sb("junk2", [P, 2, 2, HALF], BF16)
        al_now = sb("al_now", [P, 2, 2])
        ps = [ctx.enter_context(nc.psum_tensor(f"ps_h2{u}", [P, 2, 512], F32)) for u in range(2)]

        w_in = [sem(f"w2_in{q}") for q in range(RAW)]
        a_in, w_hi, w_lo, ones_set = sem("a2_in"), sem("w2_hi_made"), sem("w2_lo_made"), sem("ones2_set")
        ghi_made, glo_made, summed, h_hi, al_made, al_kept = (
            sem("ghi_made"), sem("glo_made"), sem("h2_summed"), sem("h2_hi_made"), sem("al2_made"),
            sem("al2_kept"))

        with nc.Block() as block:
            @block.sync
            def _(sp):
                for k in range(H1):
                    if k >= RAW:
                        sp.wait_ge(w_lo, k - RAW + 1)
                    sp.dma_start(w2_raw[:, k % RAW, :], w2[k * C1:(k + 1) * C1, :]).then_inc(w_in[k % RAW], 16)
                sp.dma_start(att[:, :, :].rearrange("p a d -> p (a d)"), att2.broadcast_to([P, 2 * D])) \
                  .then_inc(a_in, 16)

            @block.gpsimd
            def _(pool):
                nc.gpsimd.memset(s.h2_hi[:, :, D:D + 4].bitcast(F32), 0.0).then_inc(ones_set, 1)
                nc.gpsimd.memset(s.h2_lo[:, :, D:D + 4].bitcast(F32), 0.0)
                pool.wait_ge(ones_set, 1)
                nc.gpsimd.memset(s.h2_hi[:, :, D:D + 1].bitcast(F32), 1.0).then_inc(ones_set, 1)
                with pool.Fori(0, NT // 2) as i:
                    for u in range(2):
                        t = 2 * i + u
                        pool.wait_ge(ghi_made, t + 1)
                        nc.gpsimd.tensor_tensor(g_lo[:, u], s.g_t[:, :, bass.ds(t * P, P)],
                                                g_hi[:, u].bitcast(F32), ALU.subtract).then_inc(glo_made, 1)
                pool.wait_ge(ones_set, 2)

            @block.scalar
            def _(act):
                def split_g(t, u):
                    nc.scalar.activation(g_hi[:, u], s.g_t[:, :, bass.ds(t * P, P)], ACT.Copy).then_inc(ghi_made, 1)

                split_g(0, 0)
                for k in range(H1):
                    act.wait_ge(w_in[k % RAW], 16 * (k // RAW + 1))
                    nc.scalar.activation(w2_hi[:, k, :], w2_raw[:, k % RAW, :], ACT.Copy).then_inc(w_hi, 1)
                act.sem_inc(h_hi, 2)
                split_g(1, 1)
                with act.Fori(0, NT // 2) as i:
                    for u in range(2):
                        t = 2 * i + u
                        act.wait_ge(summed, t + 1)
                        nc.scalar.activation(
                            s.h2_hi[:, bass.ds(t, 1), 0:D].rearrange("p o (b d) -> p (o b) d", b=2),
                            ps[u][:, :, 0:HALF], ACT.Copy).then_inc(h_hi, 1)
                        nc.scalar.activation(g_hi[:, u], s.g_t[:, :, bass.ds((t + 2) % NT * P, P)],
                                             ACT.Copy).then_inc(ghi_made, 1)

            @block.vector
            def _(dve):
                for k in range(H1):
                    dve.wait_ge(w_hi, k + 1)
                    nc.vector.tensor_tensor(w2_lo[:, k, :], w2_raw[:, k % RAW, :], w2_hi[:, k, :].bitcast(F32),
                                            ALU.subtract).then_inc(w_lo, 1)
                dve.wait_ge(a_in, 16)
                dve.sem_inc(al_made, 2)
                with dve.Fori(0, NT // 2) as i:
                    for u in range(2):
                        t = 2 * i + u
                        dve.wait_ge(h_hi, t + 3)
                        out = s.h2_lo[:, bass.ds(t, 1), 0:D].rearrange("p o (b d) -> p (o b) d", b=2)
                        hi = s.h2_hi[:, bass.ds(t, 1), 0:D].bitcast(F32).rearrange("p o (b d) -> p (o b) d", b=2)
                        nc.vector.tensor_tensor(out, ps[u][:, :, 0:HALF], hi, ALU.subtract)
                        for a in range(2):
                            last = nc.vector.scalar_tensor_tensor(
                                junk[:, a], ps[u][:, :, 0:HALF], 1.0,
                                att[:, a, :].rearrange("p (b d) -> p b d", b=2),
                                ALU.mult, ALU.mult, accum_out=al_now[:, u, a:a + 1])
                        last.then_inc(al_made, 1)
                        dve.wait_ge(al_made, t + 3)
                        nc.vector.tensor_copy(s.al2_col[:, bass.ds(t, 1), :].rearrange("p o a -> p (o a)"),
                                              al_now[:, u, :]).then_inc(al_kept, 1)
                        dve.wait_ge(al_kept, t + 1)

            @block.tensor
            def _(pe):
                with pe.Fori(0, NT // 2) as i:
                    for u in range(2):
                        t = 2 * i + u
                        pe.wait_ge(glo_made, t + 1)
                        pe.wait_ge(al_made, t + 1)
                        for half in range(2):
                            at = half * HALF
                            for k in range(H1):
                                hi, lo = g_hi[:, u, k, :], g_lo[:, u, k, :]
                                if half == 0 and u == 0:
                                    pe.wait_ge(w_lo, k + 1)
                                for n, (a, b) in enumerate(((hi, w2_hi), (hi, w2_lo), (lo, w2_hi))):
                                    last = nc.tensor.matmul(ps[u][:, half, 0:HALF], a, b[:, k, at:at + HALF],
                                                            start=(k == 0 and n == 0),
                                                            stop=(k == H1 - 1 and n == 2))
                        last.then_inc(summed, 1)


def attention_again(nc, s):
    with ExitStack() as ctx:
        def sb(name, shape, dt=F32):
            return ctx.enter_context(nc.sbuf_tensor(name, shape, dt))

        def sem(name):
            return ctx.enter_context(nc.semaphore(name))

        MS = NT // 2
        count = sb("count2", [P, NT, NP], U16)
        mask = sb("mask2", [P, MS, NP], BF16)
        al_rows = sb("al2_rows", [2, NP])
        junk = sb("junk3", [P, 2, NP], BF16)
        best = sb("best2", [P, NT])
        top = sb("top2", [P, 2, NT])
        rel = sb("rel2", [P, NT, 2])
        rel_rows = sb("rel2_rows", [2, NP])
        small = sb("small2", [P, NT])
        ex = sb("ex2", [P, 2, NP])
        ey = sb("ey2", [P, 2, NP])
        ps = ctx.enter_context(nc.psum_tensor("ps_rows", [P, 3, 512], F32))
        ps_all = ctx.enter_context(nc.psum_tensor("ps_all", [P, 3, 512], F32))
        count_in, al_turned, al_kept, al_spread = (sem("count_in"), sem("al2_turned"), sem("al2_rows_kept"),
                                                   sem("al2_spread"))
        mask_in = [sem(f"mask2_in{q}") for q in range(MS)]
        maxed, step, rel_turned, rel_kept, rel_spread = (sem("max2"), sem("e_step"), sem("rel2_turned"),
                                                         sem("rel2_kept"), sem("rel2_spread"))
        everywhere = [rows[:, :, :].rearrange("p a n -> p (a n)")[:, 0:NP] for rows in (ps_all, ps)]
        exped, joined, made = sem("exped2"), sem("joined2"), sem("made2")

        with nc.Block() as block:
            @block.sync
            def _(sp):
                for t in range(MS):
                    sp.dma_start(mask[:, t, :], s.mask_dram.ap()[t]).then_inc(mask_in[t], 16)
                sp.dma_start(count[:, :, :], s.count_dram.ap()).then_inc(count_in, 16)
                for t in range(MS, NT):
                    sp.wait_ge(maxed, t - MS + 1)
                    sp.dma_start(mask[:, t - MS, :], s.mask_dram.ap()[t]).then_inc(mask_in[t - MS], 16)

            @block.tensor
            def _(pe):
                def turn(src, turned):
                    for c, (at, width) in enumerate(PARTS):
                        for t in range(at // P, (at + width) // P):
                            last = nc.tensor.transpose(ps[0:2, c, t * P - at:(t + 1) * P - at], src[:, t, :],
                                                       s.ident[:, :])
                        last.then_inc(turned, 1)

                def spread(rows, a, to):
                    for c, (at, width) in enumerate(PARTS):
                        last = nc.tensor.matmul(to[:, c, 0:width], s.ident[0:2, a:a + 1].broadcast_to([2, P]),
                                                rows[:, at:at + width], start=True, stop=True)
                    return last

                turn(s.al2_col, al_turned)
                pe.wait_ge(al_kept, 3)
                spread(al_rows, 0, ps_all).then_inc(al_spread, 1)
                pe.wait_ge(step, 5)
                turn(rel, rel_turned)
                pe.wait_ge(rel_kept, 3)
                spread(rel_rows, 0, ps_all)
                spread(rel_rows, 1, ps).then_inc(rel_spread, 1)

            @block.scalar
            def _(act):
                for rows_to, turned, kept in ((al_rows, al_turned, al_kept), (rel_rows, rel_turned, rel_kept)):
                    for c, (at, width) in enumerate(PARTS):
                        act.wait_ge(turned, c + 1)
                        nc.scalar.activation(rows_to[:, at:at + width], ps[0:2, c, 0:width],
                                             ACT.Copy).then_inc(kept, 1)
                act.wait_ge(rel_spread, 1)
                for t in range(NT):
                    if t >= 2:
                        act.wait_ge(made, t - 1)
                    nc.scalar.activation(ex[:, t % 2, :], everywhere[0], ACT.Exp, bias=s.al2_col[:, t, 0:1])
                    nc.scalar.activation(ey[:, t % 2, :], everywhere[1], ACT.Exp,
                                         bias=small[:, t:t + 1]).then_inc(exped, 1)

            @block.vector
            def _(dve):
                n = [0]

                def then(ins):
                    n[0] += 1
                    ins.then_inc(step, 1)
                    dve.wait_ge(step, n[0])

                dve.wait_ge(al_spread, 1)
                for t in range(NT):
                    dve.wait_ge(mask_in[t % MS], 16 * (t // MS + 1))
                    if t >= 2:
                        dve.wait_ge(maxed, t - 1)
                    nc.vector.tensor_tensor_reduce(junk[:, t % 2, :], mask[:, t % MS, :], everywhere[0], 1.0,
                                                   2.0 * NOT_A_NEIGHBOUR, ALU.add, ALU.max,
                                                   best[:, t:t + 1]).then_inc(maxed, 1)
                dve.wait_ge(maxed, NT)
                src, dst = s.al2_col[:, :, 0], s.al2_col[:, :, 1]
                then(nc.vector.tensor_tensor(top[:, 0], best[:, :], dst, ALU.add))
                then(nc.vector.scalar_tensor_tensor(top[:, 1], top[:, 0], SLOPE, top[:, 0], ALU.mult, ALU.max))
                then(nc.vector.scalar_tensor_tensor(top[:, 1], best[:, :], 0.5 * NOT_A_NEIGHBOUR, top[:, 1],
                                                    ALU.is_gt, ALU.mult))
                nc.vector.tensor_scalar(small[:, :], src, SLOPE, None, ALU.mult)
                then(nc.vector.tensor_tensor(rel[:, :, 0], dst, top[:, 1], ALU.subtract))
                then(nc.vector.scalar_tensor_tensor(rel[:, :, 1], dst, SLOPE, top[:, 1], ALU.mult, ALU.subtract))
                dve.wait_ge(count_in, 16)
                for t in range(NT):
                    dve.wait_ge(exped, t + 1)
                    nc.vector.scalar_tensor_tensor(ex[:, t % 2, :], ey[:, t % 2, :], 1.0, ex[:, t % 2, :],
                                                   ALU.min, ALU.max).then_inc(joined, 1)
                    dve.wait_ge(joined, t + 1)
                    nc.vector.scalar_tensor_tensor(s.prob2[:, t, :], ex[:, t % 2, :], 1.0, count[:, t, :],
                                                   ALU.min, ALU.mult).then_inc(made, 1)


def mix_and_route(nc, s, x, bias2, wg, we, bg, be):
    with ExitStack() as ctx:
        def sb(name, shape, dt=F32):
            return ctx.enter_context(nc.sbuf_tensor(name, shape, dt))

        def sem(name):
            return ctx.enter_context(nc.semaphore(name))

        p_hi = sb("p_hi", [P, 2, NT, P], F32R)
        p_lo = sb("p_lo", [P, 2, NT, P], F32R)
        x_in_t = sb("x_in_t", [P, 2, D])
        x2 = sb("x2", [P, 2, D])
        xf = sb("xf", [P, 2, D])
        xf_t = sb("xf_t", [P, 2, KD, P])
        b_row = sb("b_row", [P, D])
        wr = sb("wr", [P, KD, RC])
        br = sb("br", [P, RC])
        zi = sb("zi", [P, 2, 2])
        stats = sb("stats2", [P, 2, 2, 6])
        mv = sb("mv2", [P, 2, 2])
        veps = sb("veps2", [P, 2, 1])
        half_neg = sb("half_neg", [P, 1])
        ahead = sb("ahead", [P, G, EG, EG], BF16)
        tied = sb("tied", [P, G, EG, EG], BF16)
        before = sb("before", [P, EG, EG], BF16)
        rstd = sb("rstd2", [P, 2, 1])
        ps_o = [ctx.enter_context(nc.psum_tensor(f"ps_mix{u}", [P, 2, 512], F32)) for u in range(2)]
        ps_x = ctx.enter_context(nc.psum_tensor("ps_xf", [P, 2, 512], F32))
        ps_l = ctx.enter_context(nc.psum_tensor("ps_logit", [P, 512], F32))
        W2H = (D + 4) // 2

        wr_in, br_in = sem("wr_in"), sem("br_in")
        x_in = [sem("xt_in0"), sem("xt_in1")]
        phi_made, plo_made, mixed, x_biased = (sem("phi_made"), sem("plo_made"), sem("mixed2"),
                                               sem("x_biased"))
        x2_made, stat, var_made, rooted, xf_made = (sem("x2_made"), sem("stat2"), sem("var_made"),
                                                    sem("rooted"), sem("xf_made"))
        turned, xft_kept, logged, logits_kept = sem("xf_turned"), sem("xft_kept"), sem("logged"), sem("logits_kept")
        x2_out = [sem("x2_out0"), sem("x2_out1")]
        xf_out = [sem("xf_out0"), sem("xf_out1")]
        consts = sem("f_consts")

        with nc.Block() as block:
            @block.sync
            def _(sp):
                sp.dma_start(b_row[:, :], bias2.broadcast_to([P, D])).then_inc(br_in, 16)
                sp.dma_start(br[:, 0:G], bg.broadcast_to([P, G])).then_inc(br_in, 16)
                sp.dma_start(br[:, G:RC], be.broadcast_to([P, E])).then_inc(br_in, 16)
                sp.dma_start(wr[:, :, 0:G], wg.rearrange("(k p) g -> p k g", p=P)).then_inc(wr_in, 16)
                for g in range(G):
                    sp.dma_start(wr[:, :, G + g * EG:G + (g + 1) * EG],
                                 we[g].rearrange("(k p) e -> p k e", p=P)).then_inc(wr_in, 16)
                for u in range(2):
                    sp.dma_start(x_in_t[:, u, :], x[u * P:(u + 1) * P, :]).then_inc(x_in[u], 16)

                def out(t, i, u):
                    sp.wait_ge(x2_made, t + 1)
                    sp.dma_start(s.sum_dram.ap()[bass.ds(t * P, P), :], x2[:, u, :]).then_inc(x2_out[u], 16)
                    sp.wait_ge(xf_made, t + 1)
                    sp.dma_start(s.table.ap()[bass.ds(t * P, P), 0:D], xf[:, u, :]).then_inc(xf_out[u], 16)

                with sp.Fori(0, NT // 2 - 1) as i:
                    for u in range(2):
                        t = 2 * i + u
                        sp.wait_ge(x2_made, t + 1)
                        sp.dma_start(x_in_t[:, u, :], x[bass.ds((t + 2) * P, P), :]).then_inc(x_in[u], 16)
                        out(t, i, u)
                for u in range(2):
                    out(NT - 2 + u, NT // 2 - 1, u)
                for u in range(2):
                    sp.wait_ge(x2_out[u], 16 * (NT // 2))
                    sp.wait_ge(xf_out[u], 16 * (NT // 2))

            @block.gpsimd
            def _(pool):
                nc.gpsimd.memset(half_neg[:, :], -0.5).then_inc(consts, 1)
                nc.gpsimd.memset(before[:, :, :], 1.0).then_inc(consts, 1)
                pool.wait_ge(consts, 2)
                nc.gpsimd.affine_select(out=before[:, :, :], in_=before[:, :, :], compare_op=ALU.is_gt, fill=0.0,
                                        base=0, pattern=[[1, EG], [-1, EG]],
                                        channel_multiplier=0).then_inc(consts, 1)
                pool.wait_ge(br_in, 48)
                with pool.Fori(0, NT // 2) as i:
                    for u in range(2):
                        t = 2 * i + u
                        pool.wait_ge(x_in[u], 16 * i + 16)
                        nc.gpsimd.tensor_tensor(x_in_t[:, u, :], x_in_t[:, u, :], b_row[:, :],
                                                ALU.add).then_inc(x_biased, 1)
                        pool.wait_ge(var_made, t + 1)
                        nc.gpsimd.tensor_tensor(rstd[:, u, :], veps[:, u, :], half_neg[:, :],
                                                ALU.pow).then_inc(rooted, 1)

            @block.scalar
            def _(act):
                def split(t, u):
                    nc.scalar.activation(p_hi[:, u], s.prob2[:, :, bass.ds(t * P, P)], ACT.Copy).then_inc(phi_made, 1)

                split(0, 0)
                split(1, 1)
                with act.Fori(0, NT // 2) as i:
                    for u in range(2):
                        t = 2 * i + u
                        act.wait_ge(mixed, t + 1)
                        nc.scalar.activation(p_hi[:, u], s.prob2[:, :, bass.ds((t + 2) % NT * P, P)],
                                             ACT.Copy).then_inc(phi_made, 1)
                        act.wait_ge(turned, t + 1)
                        nc.scalar.activation(xf_t[:, u].rearrange("p (b k) n -> p b (k n)", b=2),
                                             ps_x[:, :, 0:HALF], ACT.Copy).then_inc(xft_kept, 1)

            @block.vector
            def _(dve):
                def split(u):
                    nc.vector.tensor_tensor(p_lo[:, u], s.prob2[:, :, bass.ds(low_at[0], P)],
                                            p_hi[:, u].bitcast(F32), ALU.subtract).then_inc(plo_made, 1)

                low_at = [0]
                for t in range(2):
                    dve.wait_ge(phi_made, t + 1)
                    low_at[0] = t * P
                    split(t)
                steps = dve.alloc_register("f_steps")
                dve.reg_mov(steps, 0)

                def then(ins):
                    ins.then_inc(stat, 1)
                    dve.reg_add(steps, steps, 1)
                    done = dve.snap(steps)
                    dve.wait_ge(br_in, 48)
                    dve.wait_ge(stat, done)

                def rank_experts(t):
                    el = s.el[:, bass.ds(t, 1), :].rearrange("p o (g e) -> p (o g) e", g=G)
                    wide = [P, G, EG, EG]
                    rival, own = el.unsqueeze(2).broadcast_to(wide), el.unsqueeze(3).broadcast_to(wide)
                    nc.vector.tensor_tensor(ahead[:, :, :, :], rival, own, ALU.is_gt)
                    then(nc.vector.tensor_tensor(tied[:, :, :, :], rival, own, ALU.is_equal))
                    then(nc.vector.tensor_tensor(tied[:, :, :, :], tied[:, :, :, :],
                                                 before[:, :, :].unsqueeze(1).broadcast_to(wide), ALU.mult))
                    then(nc.vector.tensor_tensor(ahead[:, :, :, :], ahead[:, :, :, :], tied[:, :, :, :], ALU.add))
                    then(nc.vector.tensor_reduce(s.rank[:, bass.ds(t, 1), :]
                                                 .rearrange("p o (g e) -> p (o g) e", g=G),
                                                 ahead[:, :, :, :], AX.X, ALU.add))

                dve.wait_ge(consts, 3)

                def normalize(t, i, u, first=False):
                    dve.wait_ge(mixed, t + 1)
                    then(nc.vector.tensor_scalar(zi[:, u, 0:1], ps_o[u][:, 1, D - W2H:D - W2H + 1], 1e-16,
                                                 None, ALU.add))
                    then(nc.vector.reciprocal(zi[:, u, 1:2], zi[:, u, 0:1]))
                    dve.wait_ge(x_biased, t + 1)
                    if not first:
                        dve.wait_ge(x2_out[u], 16 * i)
                    nc.vector.scalar_tensor_tensor(x2[:, u, 0:W2H], ps_o[u][:, 0, 0:W2H], zi[:, u, 1:2],
                                                   x_in_t[:, u, 0:W2H], ALU.mult, ALU.add)
                    nc.vector.scalar_tensor_tensor(x2[:, u, W2H:D], ps_o[u][:, 1, 0:D - W2H], zi[:, u, 1:2],
                                                   x_in_t[:, u, W2H:D], ALU.mult,
                                                   ALU.add).then_inc(x2_made, 1)
                    dve.wait_ge(x2_made, t + 1)
                    nc.vector.bn_stats(stats[:, u, 0, :], x2[:, u, 0:HALF])
                    then(nc.vector.bn_stats(stats[:, u, 1, :], x2[:, u, HALF:D]))
                    then(nc.vector.bn_aggr(mv[:, u, :], stats[:, u, :, :].rearrange("p a b -> p (a b)")))
                    nc.vector.tensor_scalar(veps[:, u, :], mv[:, u, 1:2], LN_EPS, None,
                                            ALU.add).then_inc(var_made, 1)
                    dve.wait_ge(rooted, t + 1)
                    if not first:
                        dve.wait_ge(xf_out[u], 16 * i)
                    nc.vector.tensor_scalar(xf[:, u, :], x2[:, u, :], mv[:, u, 0:1], rstd[:, u, :],
                                            ALU.subtract, ALU.mult).then_inc(xf_made, 1)
                    dve.wait_ge(phi_made, t + 3)
                    low_at[0] = (t + 2) % NT * P
                    split(u)

                def logits(t):
                    dve.wait_ge(logged, t + 1)
                    nc.vector.tensor_tensor(s.gl[:, bass.ds(t, 1), :].rearrange("p o g -> p (o g)"),
                                            ps_l[:, 0:G], br[:, 0:G], ALU.add)
                    nc.vector.tensor_tensor(s.el[:, bass.ds(t, 1), :].rearrange("p o g -> p (o g)"),
                                            ps_l[:, G:RC], br[:, G:RC], ALU.add).then_inc(logits_kept, 1)
                    dve.wait_ge(logits_kept, t + 1)
                    rank_experts(t)

                normalize(0, 0, 0, first=True)
                normalize(1, 0, 1, first=True)
                logits(0)
                with dve.Fori(1, NT // 2) as i:
                    for u in range(2):
                        normalize(2 * i + u, i, u)
                        logits(2 * i + u - 1)
                logits(NT - 1)

            @block.tensor
            def _(pe):
                pe.wait_ge(wr_in, 16 * (1 + G))

                def mix(t, u, half, first=False):
                    if not first:
                        pe.wait_ge(x2_made, t - 1)
                    at = half * W2H
                    for k in range(NT):
                        hi, lo = p_hi[:, u, k, :], p_lo[:, u, k, :]
                        for n, (a, b) in enumerate(((hi, s.h2_hi), (hi, s.h2_lo), (lo, s.h2_hi))):
                            last = nc.tensor.matmul(ps_o[u][:, half, 0:W2H], a, b[:, k, at:at + W2H],
                                                    start=(k == 0 and n == 0),
                                                    stop=(k == NT - 1 and n == 2))
                    if half == 1:
                        last.then_inc(mixed, 1)

                def turn(t, u, first=False):
                    pe.wait_ge(xf_made, t + 1)
                    if not first:
                        pe.wait_ge(xft_kept, t)
                    for k in range(KD):
                        last = nc.tensor.transpose(ps_x[:, k // 3, (k % 3) * P:(k % 3 + 1) * P],
                                                   xf[:, u, k * P:(k + 1) * P], s.ident[:, :])
                    last.then_inc(turned, 1)

                def route(t, u, first=False):
                    pe.wait_ge(xft_kept, t + 1)
                    if not first:
                        pe.wait_ge(logits_kept, t)
                    for k in range(KD):
                        last = nc.tensor.matmul(ps_l[:, 0:RC], xf_t[:, u, k, :], wr[:, k, :],
                                                start=(k == 0), stop=(k == KD - 1))
                    last.then_inc(logged, 1)

                def step(t, u, first=False, second=False):
                    pe.wait_ge(plo_made, t + 1)
                    mix(t, u, 0, first or second)
                    if not first:
                        turn(t - 1, 1 - u, second)
                    mix(t, u, 1, first or second)
                    if not first:
                        route(t - 1, 1 - u, second)

                step(0, 0, first=True)
                step(1, 1, second=True)
                with pe.Fori(1, NT // 2) as i:
                    for u in range(2):
                        step(2 * i + u, u)
                turn(NT - 1, 1)
                route(NT - 1, 1)


def match_rows(nc, s, e):
    wide = [P, NT, P]
    nc.vector.tensor_copy(s.token_now[:, :, :], s.token[:, :, bass.ds(e, 1), :, :]
                          .rearrange("p t o b a -> p t (o b a)"))
    return nc.vector.tensor_tensor(s.one_row[:, :, :], s.lane[:, :].unsqueeze(1).broadcast_to(wide),
                                   s.row_at[:, :, bass.ds(e, 1)].broadcast_to(wide), ALU.is_equal)


def list_tokens(nc, s, ps):
    for t in range(NT):
        last = nc.tensor.matmul(ps[:, 0:2 * NT], s.one_row[:, t, :],
                                s.token_now[:, t, :], start=(t == 0), stop=(t == NT - 1))
    return last


def sum_list(nc, s, ps):
    return nc.vector.tensor_reduce(s.found[:, 0], ps[:, 0:2 * NT].rearrange("p (b a) -> p a b", b=2),
                                   AX.X, ALU.add)


def mark_padding(nc, s):
    return nc.vector.tensor_scalar(s.found[:, 1], s.found[:, 0], 0.0, s.pad_at[:, :], ALU.is_equal, ALU.mult)


def keep_list(nc, s, start):
    return nc.vector.scalar_tensor_tensor(s.list_i[:, bass.ds(start, NT)], s.found[:, 0], -1.0, s.found[:, 1],
                                          ALU.add, ALU.add)


def plan_experts(nc, s, w1, b1, w2, b2):
    with ExitStack() as ctx:
        def sb(name, shape, dt=F32):
            return ctx.enter_context(nc.sbuf_tensor(name, shape, dt))

        def sem(name):
            return ctx.enter_context(nc.semaphore(name))

        before_b = sb("g_before_b", [P, G, G], BF16)
        before = sb("g_before", [P, G, G])
        g_ahead = sb("g_ahead", [P, NT, G, G], BF16)
        g_tied = sb("g_tied", [P, NT, G, G], BF16)
        sel = sb("sel", [P, NT * G, EG])
        g_rank = sb("g_rank", [P, NT, G])
        g_sel = sb("g_sel", [P, NT, G])
        peak = sb("peak", [P, NT * G])
        g_peak = sb("g_peak", [P, NT])
        weight = sb("weight", [P, NT * G, EG])
        g_weight = sb("g_weight", [P, NT, G])
        total = sb("total", [P, NT * G])
        g_total = sb("g_total", [P, NT])
        chosen = sb("chosen", [P, NT, E])
        chosen_b = sb("chosen_b", [P, NT, E], BF16)
        passed = sb("passed", [P, NT + 1, E])
        passed_b = sb("passed_b", [P, NT + 1, E], BF16)
        gates = sb("gates", [P, NT, E])
        b2_all = sb("b2_all", [E, D])
        pad_rows = sb("pad_rows", [P, TW])
        upper = sb("upper", [P, P])
        upper_b = sb("upper_b", [P, P], BF16)
        ones_b = sb("ones_b", [P, P], BF16)
        place_i = sb("place_i", [P, 3, NT, E], I32)
        row_at = sb("row_at", [P, NT, E])
        tile_at = sb("tile_at", [P, NT, E], BF16)
        tile_no = sb("tile_no", [P, NT], I16)
        tile_bf = sb("tile_bf", [P, NT], BF16)
        in_tile = sb("in_tile", [P, NT, E, NT], BF16)
        lane_i = sb("lane_i", [P, 1], I32)
        lane = sb("lane", [P, 1])
        is_node = sb("is_node", [P, 1])
        level = sb("level", [1, NT])
        level_i = sb("level_i", [1, NT], I32)
        over = sb("over", [1, E, NT])
        tiles_f = sb("tiles_f", [1, 2, E])
        sums = sb("sums", [1, 2, E])

        ps_p = ctx.enter_context(nc.psum_tensor("ps_place", [P, 512], F32))
        ps_n = ctx.enter_context(nc.psum_tensor("ps_counts", [P, 512], F32))
        ps_t = ctx.enter_context(nc.psum_tensor("ps_gates_t", [P, 3, 512], F32))
        ps_l = ctx.enter_context(nc.psum_tensor("ps_list", [P, 512], F32))

        consts, step, shifted, exped = sem("g_consts"), sem("g_step"), sem("g_shifted"), sem("g_exped")
        routed, chosen_set, placed = sem("routed"), sem("chosen_set"), sem("placed")
        turned, kept, out_done = sem("gates_turned"), sem("gates_kept"), sem("tab_out")
        rows_made, listed, values_made = sem("rows_made"), sem("listed"), sem("values")
        b2_in = sem("b2_in")

        with nc.Block() as block:
            @block.gpsimd
            def _(pool):
                nc.gpsimd.memset(before[:, :, :], 1.0).then_inc(consts, 1)
                nc.gpsimd.memset(upper[:, :], 1.0).then_inc(consts, 1)
                nc.gpsimd.memset(pad_rows[:, :], 0.0).then_inc(consts, 1)
                nc.gpsimd.iota(tile_no[:, :], [[1, NT]], base=0, channel_multiplier=0).then_inc(consts, 1)
                nc.gpsimd.iota(lane_i[:, 0:1], [[1, 1]], base=1, channel_multiplier=1).then_inc(consts, 1)
                nc.gpsimd.iota(level_i[:, :], [[P, NT]], base=0, channel_multiplier=0).then_inc(consts, 1)
                nc.gpsimd.memset(ones_b[:, :], 1.0).then_inc(consts, 1)
                nc.gpsimd.memset(s.row_at[:, :, :], -1.0).then_inc(consts, 1)
                nc.gpsimd.memset(s.token[:, :, E:EL, :, :], 0.0).then_inc(consts, 1)
                nc.gpsimd.memset(s.starts[:, :], LISTED).then_inc(consts, 1)
                pool.wait_ge(consts, 10)
                nc.gpsimd.affine_select(out=before[:, :, :], in_=before[:, :, :], compare_op=ALU.is_gt, fill=0.0,
                                        base=0, pattern=[[1, G], [-1, G]], channel_multiplier=0).then_inc(consts, 1)
                nc.gpsimd.affine_select(out=upper[:, :], in_=upper[:, :], compare_op=ALU.is_gt, fill=0.0,
                                        base=0, pattern=[[1, P]], channel_multiplier=-1).then_inc(consts, 1)

            @block.sync
            def _(sp):
                sp.dma_start(b2_all[:, :], b2).then_inc(b2_in, 16)
                for piece in range(3):
                    if piece:
                        sp.wait_ge(s.w1_in, 16 * piece)
                        sp.wait_ge(s.w2_in, 16 * piece)
                    load_piece(sp, s, w1, b1, w2, 0, 0, piece)
                sp.wait_ge(s.w1_in, 48)
                sp.wait_ge(s.w2_in, 48)
                sp.wait_ge(s.b1_in, 16)
                sp.wait_ge(consts, 12)
                sp.dma_start(s.table.ap()[NP:ROWS, :], pad_rows[:, :]).then_inc(out_done, 16)
                sp.dma_start(s.sum_dram.ap()[NP:ROWS, :], pad_rows[:, 0:D]).then_inc(out_done, 16)
                sp.wait_ge(routed, 1)
                sp.dma_start(s.table.ap()[0:NP, D:TW].rearrange("(t p) c -> p t c", p=P),
                             gates[:, :, :]).then_inc(out_done, 16)
                sp.wait_ge(out_done, 48)

            @block.scalar
            def _(act):
                act.wait_ge(shifted, 1)
                nc.scalar.activation(weight[:, :, :], weight[:, :, :], ACT.Exp)
                nc.scalar.activation(g_weight[:, :, :], g_weight[:, :, :], ACT.Exp).then_inc(exped, 1)
                for c, (at, width) in enumerate(PARTS):
                    act.wait_ge(turned, c + 1)
                    nc.scalar.activation(s.gates_hi[:, at:at + width], ps_t[0:E, c, 0:width],
                                         ACT.Copy).then_inc(kept, 1)
                act.wait_ge(b2_in, 16)
                nc.scalar.activation(s.b2_hi[:, :], b2_all[:, :], ACT.Copy).then_inc(kept, 1)

            @block.vector
            def _(dve):
                n = [0]

                def then(ins):
                    n[0] += 1
                    ins.then_inc(step, 1)
                    dve.wait_ge(step, n[0])

                el = s.el[:, :, :].rearrange("p t (g e) -> p (t g) e", g=G)
                gl = s.gl[:, :, :]
                dve.wait_ge(consts, 12)
                nc.vector.tensor_copy(before_b[:, :, :], before[:, :, :])
                nc.vector.tensor_copy(s.lane[:, :], s.column[:, 0:P])
                then(nc.vector.tensor_copy(lane[:, :], lane_i[:, :]))
                nc.vector.tensor_scalar(is_node[:, :], lane[:, 0:1], float(TAIL), None, ALU.is_le)
                nc.vector.tensor_reduce(peak[:, :], el, AX.X, ALU.max)
                then(nc.vector.tensor_reduce(g_peak[:, :], gl, AX.X, ALU.max))
                nc.vector.tensor_tensor(weight[:, :, :], el, peak[:, :].unsqueeze(2).broadcast_to([P, NT * G, EG]),
                                        ALU.subtract)
                nc.vector.tensor_tensor(g_weight[:, :, :], gl, g_peak[:, :].unsqueeze(2).broadcast_to([P, NT, G]),
                                        ALU.subtract).then_inc(shifted, 1)
                g_wide = [P, NT, G, G]
                nc.vector.tensor_tensor(g_ahead[:, :, :, :], gl.unsqueeze(2).broadcast_to(g_wide),
                                        gl.unsqueeze(3).broadcast_to(g_wide), ALU.is_gt)
                then(nc.vector.tensor_tensor(g_tied[:, :, :, :], gl.unsqueeze(2).broadcast_to(g_wide),
                                             gl.unsqueeze(3).broadcast_to(g_wide), ALU.is_equal))
                then(nc.vector.tensor_tensor(g_tied[:, :, :, :], g_tied[:, :, :, :],
                                             before_b[:, :, :].unsqueeze(1).broadcast_to(g_wide), ALU.mult))
                then(nc.vector.tensor_tensor(g_ahead[:, :, :, :], g_ahead[:, :, :, :], g_tied[:, :, :, :], ALU.add))
                then(nc.vector.tensor_reduce(g_rank[:, :, :], g_ahead[:, :, :, :], AX.X, ALU.add))
                nc.vector.tensor_scalar(sel[:, :, :], s.rank[:, :, :].rearrange("p t (g e) -> p (t g) e", g=G),
                                        float(KE), None, ALU.is_lt)
                then(nc.vector.tensor_scalar(g_sel[:, :, :], g_rank[:, :, :], float(KG), None, ALU.is_lt))
                all_g = g_sel[:, :, :].rearrange("p t g -> p (t g)").unsqueeze(2).broadcast_to([P, NT * G, EG])
                then(nc.vector.tensor_tensor(chosen[:, :, :].rearrange("p t (g e) -> p (t g) e", g=G),
                                             sel[:, :, :], all_g, ALU.mult))
                then(nc.vector.tensor_scalar(chosen[:, NT - 1, :], chosen[:, NT - 1, :], is_node[:, 0:1], None,
                                             ALU.mult))
                nc.vector.tensor_copy(chosen_b[:, :, :], chosen[:, :, :])
                nc.vector.tensor_copy(upper_b[:, :], upper[:, :])
                then(nc.vector.memset(passed[:, 0, :], 0.0))
                for t in range(NT):
                    then(nc.vector.tensor_tensor(passed[:, t + 1, :], passed[:, t, :], chosen[:, t, :], ALU.add))
                nc.vector.tensor_copy(passed_b[:, :, :], passed[:, :, :]).then_inc(chosen_set, 1)
                nc.vector.tensor_copy(tile_bf[:, :], tile_no[:, :])
                then(nc.vector.tensor_copy(level[:, :], level_i[:, :]))
                dve.wait_ge(exped, 1)
                nc.vector.tensor_tensor(weight[:, :, :], weight[:, :, :], sel[:, :, :], ALU.mult)
                then(nc.vector.tensor_tensor(g_weight[:, :, :], g_weight[:, :, :], g_sel[:, :, :], ALU.mult))
                nc.vector.tensor_reduce(total[:, :], weight[:, :, :], AX.X, ALU.add)
                then(nc.vector.tensor_reduce(g_total[:, :], g_weight[:, :, :], AX.X, ALU.add))
                nc.vector.reciprocal(total[:, :], total[:, :])
                then(nc.vector.reciprocal(g_total[:, :], g_total[:, :]))
                nc.vector.tensor_tensor(weight[:, :, :], weight[:, :, :],
                                        total[:, :].unsqueeze(2).broadcast_to([P, NT * G, EG]), ALU.mult)
                then(nc.vector.tensor_tensor(g_weight[:, :, :], g_weight[:, :, :],
                                             g_total[:, :].unsqueeze(2).broadcast_to([P, NT, G]), ALU.mult))
                nc.vector.scalar_tensor_tensor(weight[:, :, :], weight[:, :, :], GATE_MIN, weight[:, :, :],
                                               ALU.is_ge, ALU.mult)
                then(nc.vector.scalar_tensor_tensor(g_weight[:, :, :], g_weight[:, :, :], GATE_MIN,
                                                    g_weight[:, :, :], ALU.is_ge, ALU.mult))
                all_g = g_weight[:, :, :].rearrange("p t g -> p (t g)").unsqueeze(2).broadcast_to([P, NT * G, EG])
                then(nc.vector.tensor_tensor(weight[:, :, :], weight[:, :, :], all_g, ALU.mult))
                nc.vector.tensor_copy(gates[:, :, :],
                                      weight[:, :, :].rearrange("p (t g) e -> p t (g e)", g=G)).then_inc(routed, 1)
                dve.wait_ge(placed, 1)
                then(nc.vector.tensor_copy(place_i[:, 0], ps_p[:, 0:NT * E].rearrange("p (t e) -> p t e", e=E)))
                nc.vector.tensor_scalar(place_i[:, 1], place_i[:, 0], 7, None, ALU.arith_shift_right)
                then(nc.vector.tensor_scalar(place_i[:, 2], place_i[:, 0], P - 1, None, ALU.bitwise_and))
                nc.vector.tensor_copy(tile_at[:, :, :], place_i[:, 1])
                then(nc.vector.tensor_copy(row_at[:, :, :], place_i[:, 2]))
                then(nc.vector.scalar_tensor_tensor(row_at[:, :, :], row_at[:, :, :], 1.0, chosen[:, :, :],
                                                    ALU.add, ALU.mult))
                nc.vector.tensor_scalar(s.row_at[:, :, 0:E], row_at[:, :, :], -1.0, None, ALU.add)
                then(nc.vector.tensor_tensor(
                    in_tile[:, :, :, :].rearrange("p t e a -> p (t e) a"),
                    tile_at[:, :, :].rearrange("p t e -> p (t e)").unsqueeze(2).broadcast_to([P, NT * E, NT]),
                    tile_bf[:, :].unsqueeze(1).broadcast_to([P, NT * E, NT]), ALU.is_equal))
                nc.vector.tensor_scalar(s.token[:, :, 0:E, 0, :], in_tile[:, :, :, :], lane[:, 0:1], None, ALU.mult)
                for t in range(NT):
                    last = nc.vector.tensor_scalar(s.token[:, t, 0:E, 1, :], in_tile[:, t, :, :], float(P * t), None,
                                                   ALU.mult)
                last.then_inc(values_made, 1)
                nc.vector.tensor_tensor(over[:, :, :], ps_n[0:1, 0:E].unsqueeze(2).broadcast_to([1, E, NT]),
                                        level[:, :].unsqueeze(1).broadcast_to([1, E, NT]), ALU.is_gt)
                then(nc.vector.memset(sums[:, :, :], 0.0))
                then(nc.vector.tensor_reduce(tiles_f[:, 0, :], over[:, :, :], AX.X, ALU.add))
                then(nc.vector.tensor_scalar(tiles_f[:, 1, :], tiles_f[:, 0, :], float(MIN_TILES), None, ALU.max))
                nc.vector.tensor_copy(s.tiles[:, :], tiles_f[:, 1, :])
                then(nc.vector.tensor_copy(sums[:, 0, 1:E], tiles_f[:, 1, 0:E - 1]))
                reach, u = 1, 0
                while reach < E:
                    nc.vector.tensor_copy(sums[:, 1 - u, 0:reach], sums[:, u, 0:reach])
                    then(nc.vector.tensor_tensor(sums[:, 1 - u, reach:E], sums[:, u, reach:E],
                                                 sums[:, u, 0:E - reach], ALU.add))
                    reach, u = 2 * reach, 1 - u
                then(nc.vector.tensor_scalar(s.starts[:, 0:E], sums[:, u, :], float(LEAD), None, ALU.add))
                for c, (at, width) in enumerate(PARTS):
                    dve.wait_ge(kept, c + 1)
                    nc.vector.tensor_tensor(s.gates_lo[:, at:at + width], ps_t[0:E, c, 0:width],
                                            s.gates_hi[:, at:at + width].bitcast(F32), ALU.subtract)
                dve.wait_ge(kept, 4)
                nc.vector.tensor_tensor(s.b2_lo[:, :], b2_all[:, :], s.b2_hi[:, :].bitcast(F32), ALU.subtract)
                then(nc.vector.tensor_scalar(s.pad_at[:, :], lane[:, :], float(NP), None, ALU.add))
                then(nc.vector.tensor_scalar(s.list_i[:, :], s.column[:, 0:LIST], 0.0, s.pad_at[:, :],
                                             ALU.mult, ALU.add))
                then(nc.vector.tensor_scalar(s.list_i[:, :], s.list_i[:, :], -1.0, None, ALU.add))
                for e in range(AHEAD - 1):
                    match_rows(nc, s, e).then_inc(rows_made, 1)
                    dve.wait_ge(listed, e + 1)
                    then(sum_list(nc, s, ps_l))
                    then(mark_padding(nc, s))
                    start = dve.value_load(s.starts[0:1, e:e + 1], min_val=LEAD, max_val=LIST - NT)
                    then(keep_list(nc, s, start))

            @block.tensor
            def _(pe):
                pe.wait_ge(chosen_set, 1)
                nc.tensor.matmul(ps_n[:, 0:E], ones_b[:, :], passed_b[:, NT, :], start=True, stop=True)
                nc.tensor.matmul(ps_p[:, 0:NT * E], upper_b[:, :], chosen_b[:, :, :].rearrange("p t e -> p (t e)"),
                                 start=True, stop=False)
                nc.tensor.matmul(ps_p[:, 0:NT * E], ones_b[:, :],
                                 passed_b[:, 0:NT, :].rearrange("p t e -> p (t e)"),
                                 start=False, stop=True).then_inc(placed, 1)
                pe.wait_ge(routed, 1)
                for c, (at, width) in enumerate(PARTS):
                    for t in range(at // P, (at + width) // P):
                        last = nc.tensor.transpose(ps_t[0:E, c, t * P - at:(t + 1) * P - at], gates[:, t, :],
                                                   s.ident[:, :])
                    last.then_inc(turned, 1)
                pe.wait_ge(values_made, 1)
                for e in range(AHEAD - 1):
                    pe.wait_ge(rows_made, e + 1)
                    if e:
                        pe.wait_ge(listed, e)
                    list_tokens(nc, s, ps_l).then_inc(listed, 1)


def load_piece(eng, s, w1, b1, w2, e, u, piece):
    if piece == 0:
        eng.dma_start(s.b1_all[:, bass.ds(e % RING, 1), :].rearrange("p o m -> p (o m)"),
                      b1[bass.ds(e, 1), :].broadcast_to([P, HID])).then_inc(s.b1_in, 16)
    at = piece * PIECE
    eng.dma_start(s.raw1[:, u, at:at + PIECE].rearrange("p (k m) -> p k m", m=HID),
                  w1[bass.ds(e * D + piece * (D // 3), D // 3), :].rearrange("(k p) m -> p k m", p=P)) \
       .then_inc(s.w1_in, 16)
    eng.dma_start(s.raw2[:, u, at:at + PIECE], w2[bass.ds(e * HID + piece * P, P), :]).then_inc(s.w2_in, 16)


def run_experts(nc, s, w1, b1, w2):
    with ExitStack() as ctx:
        def sb(name, shape, dt=F32):
            return ctx.enter_context(nc.sbuf_tensor(name, shape, dt))

        def sem(name):
            return ctx.enter_context(nc.semaphore(name))

        raw1, raw2, b1_all = s.raw1, s.raw2, s.b1_all
        w1_hi, w1_lo = sb("e1_hi", [P, 2, ROW], F32R), sb("e1_lo", [P, 2, ROW], F32R)
        w2_hi, w2_lo = sb("e2_hi", [P, 2, ROW], F32R), sb("e2_lo", [P, 2, ROW], F32R)
        rows = sb("rows", [P, TW])
        index = sb("index", [P, 1], I32)
        to_index = sb("to_index", [P, 1], I32)
        gate = sb("gate", [P, RING, 1])
        xt_hi, xt_lo = sb("e_xt_hi", [P, KD, P], F32R), sb("e_xt_lo", [P, KD, P], F32R)
        h_in = sb("h_in", [P, HID])
        h_act = sb("h_act", [P, HID])
        ht_hi, ht_lo = sb("e_ht_hi", [P, KH, P], F32R), sb("e_ht_lo", [P, KH, P], F32R)
        y = sb("y", [P, D])

        ps_h = ctx.enter_context(nc.psum_tensor("ps_h_2", [P, 512], F32))
        ps_x = ctx.enter_context(nc.psum_tensor("ps_xt", [P, 2, 512], F32))
        ps_y = ctx.enter_context(nc.psum_tensor("ps_y", [P, 2, 512], F32))
        ps_t = ctx.enter_context(nc.psum_tensor("ps_ht", [P, 512], F32))

        ps_l = ctx.enter_context(nc.psum_tensor("ps_lists", [P, 512], F32))
        rows_made, listed, list_step, list_kept = (sem("e_rows_made"), sem("e_listed"), sem("list_step"),
                                                   sem("list_kept"))
        w1_in, w2_in, b1_in = s.w1_in, s.w2_in, s.b1_in
        w1_hi_made, w1_lo_made, w2_hi_made, w2_lo_made = (sem("e_w1_hi"), sem("e_w1_lo"), sem("e_w2_hi"),
                                                          sem("e_w2_lo"))
        gathered, turned, x_hi_made, x_lo_made = sem("gathered"), sem("x_turned"), sem("x_hi"), sem("x_lo")
        h_summed, biased, gelued, h_turned = sem("h_summed_2"), sem("biased"), sem("gelued"), sem("h_turned")
        h_hi_made, h_lo_made, y_summed, y_made = sem("h_hi"), sem("h_lo"), sem("y_summed"), sem("y_made")
        gate_kept, index_set, to_set, scattered, ready = (sem("gate_kept"), sem("index_set"), sem("to_set"),
                                                            sem("scattered"), sem("h_ready"))

        def tiles_of(eng, e):
            return eng.value_load(s.tiles[0:1, bass.ds(e, 1)], min_val=MIN_TILES, max_val=NT)

        def over_tiles(eng, name, tile, alone=None):
            count = eng.alloc_register(name)
            eng.reg_mov(count, 0)

            def one(e, which, start=False, last=False):
                k = eng.snap(count)
                tile(k, e, which, start, last)
                eng.reg_add(count, count, 1)

            def expert(e, start=False, last=False):
                one(e, 0, start, last)
                tiles = tiles_of(eng, e)
                if alone and not last:
                    with eng.If(tiles > 1):
                        one(e, 1)
                    with eng.If(tiles < 2):
                        alone(e)
                    with eng.If(tiles > 2):
                        with eng.Fori(2, tiles):
                            one(e, 2)
                else:
                    with eng.If(tiles > 1):
                        with eng.Fori(1, tiles):
                            one(e, 2)

            expert(0, start=True)
            with eng.Fori(1, E - 1) as e:
                expert(e)
            expert(E - 1, last=True)
            return eng.snap(count)

        with nc.Block() as block:
            @block.sync
            def _(sp):
                def load(e, u, before):
                    for piece in range(3):
                        sp.reg_add(arrived, arrived, 16)
                        now = sp.snap(arrived)
                        sp.wait_ge(w1_in, 16)
                        sp.wait_ge(w1_in, now)
                        sp.wait_ge(w2_in, now)
                        if piece == 0:
                            before()
                        load_piece(sp, s, w1, b1, w2, e, u, piece)

                arrived = sp.alloc_register("arrived")
                sp.reg_mov(arrived, 32)
                load(1, 1, before=lambda: sp.wait_ge(b1_in, 16))
                biases = sp.alloc_register("biases")
                sp.reg_mov(biases, 16)
                split = sp.alloc_register("split")
                sp.reg_mov(split, 0)
                with sp.Fori(1, E // 2) as i:
                    for u in range(2):
                        e = 2 * i + u

                        def free():
                            sp.reg_add(split, split, 3)
                            now = sp.snap(split)
                            sp.wait_ge(w1_in, 16)
                            sp.wait_ge(w1_lo_made, now)
                            sp.wait_ge(w2_lo_made, now)
                            sp.reg_add(biases, biases, 16)
                            now = sp.snap(biases)
                            sp.wait_ge(w1_in, 16)
                            sp.wait_ge(b1_in, now)

                        load(e, u, before=free)
                sp.wait_ge(w1_in, 48 * E)
                sp.wait_ge(w2_in, 48 * E)
                sp.wait_ge(b1_in, 16 * E)

            @block.gpsimd
            def _(pool):
                def gather(k):
                    nc.gpsimd.tensor_copy(index[:, :], s.list_i[:, bass.ds(k + LEAD, 1)]).then_inc(index_set, 1)
                    pool.reg_add(gathers, gathers, 1)
                    this = pool.snap(gathers)
                    pool.wait_ge(ready, 1)
                    pool.wait_ge(index_set, this)
                    nc.gpsimd.indirect_dma_start(rows[:, :], None, s.table.ap(),
                                                 bass.IndirectOffsetOnAxis(index[:, 0:1], 0),
                                                 bounds_check=ROWS - 1).then_inc(gathered, 16)

                def add(k, start=False):
                    pool.wait_ge(y_made, k + 1)
                    if not start:
                        pool.wait_ge(ready, 1)
                        pool.wait_ge(scattered, 16 * k)
                    nc.gpsimd.tensor_copy(to_index[:, :], s.list_i[:, bass.ds(k, 1)]).then_inc(to_set, 1)
                    pool.wait_ge(ready, 1)
                    pool.wait_ge(to_set, k + 1)
                    nc.gpsimd.indirect_dma_start(s.sum_dram.ap(), bass.IndirectOffsetOnAxis(to_index[:, 0:1], 0),
                                                 y[:, :], None, bounds_check=ROWS - 1,
                                                 compute_op=ALU.add).then_inc(scattered, 16)

                def tile(k, e, which, start, last):
                    head = which == 0
                    if head and not last:
                        pool.wait_ge(list_kept, e + 1)
                    pool.wait_ge(ready, 1)
                    pool.wait_ge(turned, k + 1)
                    nc.gpsimd.tensor_copy(gate[:, bass.ds(k % RING, 1), :].rearrange("p o c -> p (o c)"),
                                          rows[:, bass.ds(e + D, 1)]).then_inc(gate_kept, 1)
                    pool.wait_ge(ready, 1)
                    pool.wait_ge(gate_kept, k + 1)
                    gather(k + 1)
                    add(k, start)

                pool.sem_inc(ready, 1)
                gathers = pool.alloc_register("gathers")
                pool.reg_mov(gathers, 0)
                gather(0)
                n = over_tiles(pool, "pool_tiles", tile)
                for after in range(2):
                    add(n + after)
                pool.wait_ge(gathered, 16 * n + 16)
                pool.wait_ge(scattered, 16 * n + 32)

            @block.scalar
            def _(act):
                def split(raw, hi, piece, u, made):
                    at = piece * PIECE
                    nc.scalar.activation(hi[:, u, at:at + PIECE], raw[:, u, at:at + PIECE],
                                         ACT.Copy).then_inc(made, 1)

                def split_x(k):
                    act.wait_ge(turned, k + 1)
                    nc.scalar.activation(xt_hi[:, :, :].rearrange("p (b k) n -> p b (k n)", b=2),
                                         ps_x[:, :, 0:HALF], ACT.Copy).then_inc(x_hi_made, 1)

                def weights(e, which):
                    raw, hi, arrived, made = ((raw1, w1_hi, w1_in, w1_hi_made), (raw2, w2_hi, w2_in, w2_hi_made))[which]
                    for piece in range(3):
                        act.wait_ge(arrived, 48 * e + 16 * (piece + 1))
                        at = piece * PIECE
                        u = bass.ds(e % 2, 1)
                        nc.scalar.activation(hi[:, u, at:at + PIECE], raw[:, u, at:at + PIECE],
                                             ACT.Copy).then_inc(made, 1)

                def tile(k, e, which, start, last):
                    head = which == 0
                    act.wait_ge(biased, k + 1)
                    if not start:
                        act.wait_ge(h_turned, k)
                    nc.scalar.activation(h_act[:, :], h_in[:, :], ACT.Gelu).then_inc(gelued, 1)
                    split_x(k + 1)
                    if head and not last:
                        weights(e + 1, 0)
                    act.wait_ge(h_turned, k + 1)
                    nc.scalar.activation(ht_hi[:, :, :].rearrange("p k n -> p (k n)"), ps_t[:, 0:HID],
                                         ACT.Copy).then_inc(h_hi_made, 1)
                    if head and not last:
                        weights(e + 1, 1)

                weights(0, 0)
                split_x(0)
                weights(0, 1)
                over_tiles(act, "act_tiles", tile)

            @block.vector
            def _(dve):
                def split_x(k):
                    dve.wait_ge(x_hi_made, k + 1)
                    nc.vector.tensor_tensor(xt_lo[:, :, :].rearrange("p (b k) n -> p b (k n)", b=2),
                                            ps_x[:, :, 0:HALF],
                                            xt_hi[:, :, :].bitcast(F32).rearrange("p (b k) n -> p b (k n)", b=2),
                                            ALU.subtract).then_inc(x_lo_made, 1)

                def weights(e, part, pieces):
                    raw, hi, lo, halved, made = ((raw1, w1_hi, w1_lo, w1_hi_made, w1_lo_made),
                                                 (raw2, w2_hi, w2_lo, w2_hi_made, w2_lo_made))[part]
                    for piece in pieces:
                        at = piece * PIECE
                        u = bass.ds(e % 2, 1)
                        dve.wait_ge(halved, 3 * e + piece + 1)
                        nc.vector.tensor_tensor(lo[:, u, at:at + PIECE], raw[:, u, at:at + PIECE],
                                                hi[:, u, at:at + PIECE].bitcast(F32),
                                                ALU.subtract).then_inc(made, 1)

                def keep_y(k):
                    dve.wait_ge(y_summed, k)
                    dve.wait_ge(gate_kept, k)
                    dve.wait_ge(scattered, 16 * k + 16)
                    nc.vector.tensor_scalar(y[:, :].rearrange("p (b d) -> p b d", b=2), ps_y[:, :, 0:HALF],
                                            gate[:, bass.ds((k + (RING - 1)) % RING, 1), :]
                                            .rearrange("p o c -> p (o c)"),
                                            None, ALU.mult).then_inc(y_made, 1)

                def tile(k, e, which, start, last):
                    head = which == 0
                    dve.wait_ge(h_summed, k + 1)
                    if head:
                        dve.wait_ge(b1_in, 16 * e + 16)
                    if not start:
                        dve.wait_ge(gelued, k)
                    nc.vector.tensor_tensor(h_in[:, :], ps_h[:, 0:HID],
                                            b1_all[:, bass.ds(e % RING, 1), :].rearrange("p o m -> p (o m)"),
                                            ALU.add).then_inc(biased, 1)
                    if which == 1:
                        weights(e + 1, 1, (0,))
                    elif head and not last:
                        keep(e)
                    split_x(k + 1)
                    if head and not last:
                        match_rows(nc, s, e + AHEAD).then_inc(rows_made, 1)
                    elif which == 1:
                        weights(e + 1, 1, (1,))
                    if not start:
                        keep_y(k)
                    dve.wait_ge(h_hi_made, k + 1)
                    nc.vector.tensor_tensor(ht_lo[:, :, :].rearrange("p k n -> p (k n)"), ps_t[:, 0:HID],
                                            ht_hi[:, :, :].bitcast(F32).rearrange("p k n -> p (k n)"),
                                            ALU.subtract).then_inc(h_lo_made, 1)
                    if head and not last:
                        weights(e + 1, 0, range(3))
                    elif which == 1:
                        weights(e + 1, 1, (2,))

                def keep(e):
                    start = dve.value_load(s.starts[0:1, bass.ds(e + (AHEAD - 1), 1)], min_val=LEAD,
                                           max_val=LIST - NT)
                    dve.wait_ge(listed, e + 1)
                    sum_list(nc, s, ps_l).then_inc(list_step, 1)
                    dve.wait_ge(list_step, 2 * e + 1)
                    mark_padding(nc, s).then_inc(list_step, 1)
                    dve.wait_ge(list_step, 2 * e + 2)
                    keep_list(nc, s, start).then_inc(list_kept, 1)
                    dve.wait_ge(list_kept, e + AHEAD - 1)

                def alone(e):
                    weights(e + 1, 1, range(3))

                dve.sem_inc(list_kept, AHEAD - 2)
                match_rows(nc, s, AHEAD - 1).then_inc(rows_made, 1)
                nc.vector.memset(y[:, :], 0.0).then_inc(y_made, 1)
                dve.wait_ge(y_made, 1)
                dve.sem_inc(y_made, 1)
                weights(0, 0, range(3))
                split_x(0)
                weights(0, 1, range(3))
                n = over_tiles(dve, "dve_tiles", tile, alone)
                keep_y(n)

            @block.tensor
            def _(pe):
                def turn_x(k):
                    pe.wait_ge(gathered, 16 * k + 16)
                    for c in range(KD):
                        last = nc.tensor.transpose(ps_x[:, c // 3, (c % 3) * P:(c % 3 + 1) * P],
                                                   rows[:, c * P:(c + 1) * P], s.ident[:, :])
                    last.then_inc(turned, 1)

                def down(k, u):
                    pe.wait_ge(h_lo_made, k)
                    pe.wait_ge(y_made, k + 1)
                    for half in range(2):
                        for c in range(KH):
                            at = c * D + half * HALF
                            hi, lo = ht_hi[:, c, :], ht_lo[:, c, :]
                            for n, (a, b) in enumerate(((hi, w2_hi), (hi, w2_lo), (lo, w2_hi))):
                                last = nc.tensor.matmul(ps_y[:, half, 0:HALF], a,
                                                        b[:, bass.ds(u, 1), at:at + HALF]
                                                        .rearrange("p o d -> p (o d)"),
                                                        start=(c == 0 and n == 0),
                                                        stop=(c == KH - 1 and n == 2))
                    last.then_inc(y_summed, 1)

                def tile(k, e, which, start, last):
                    head = which == 0
                    if head:
                        if not last:
                            pe.wait_ge(rows_made, e + 1)
                            list_tokens(nc, s, ps_l).then_inc(listed, 1)
                        pe.wait_ge(w1_lo_made, 3 * e + 3)
                    pe.wait_ge(x_lo_made, k + 1)
                    if not start:
                        pe.wait_ge(biased, k)
                    for c in range(KD):
                        hi, lo = xt_hi[:, c, :], xt_lo[:, c, :]
                        for n, (a, b) in enumerate(((hi, w1_hi), (hi, w1_lo), (lo, w1_hi))):
                            summed = nc.tensor.matmul(ps_h[:, 0:HID], a,
                                                      b[:, bass.ds(e % 2, 1), c * HID:(c + 1) * HID]
                                                      .rearrange("p o m -> p (o m)"),
                                                      start=(c == 0 and n == 0), stop=(c == KD - 1 and n == 2))
                    summed.then_inc(h_summed, 1)
                    turn_x(k + 1)
                    if not head:
                        pe.wait_ge(w2_lo_made, 3 * e + 3)
                        down(k, e % 2)
                    elif not start:
                        pe.wait_ge(w2_lo_made, 3 * e)
                        down(k, (e + 1) % 2)
                    pe.wait_ge(gelued, k + 1)
                    if not start:
                        pe.wait_ge(h_lo_made, k)
                    for c in range(KH):
                        last_t = nc.tensor.transpose(ps_t[:, c * P:(c + 1) * P], h_act[:, c * P:(c + 1) * P],
                                                     s.ident[:, :])
                    last_t.then_inc(h_turned, 1)

                turn_x(0)
                n = over_tiles(pe, "pe_tiles", tile)
                down(n, (E - 1) % 2)


def finish(nc, s, out):
    with ExitStack() as ctx:
        def sb(name, shape, dt=F32):
            return ctx.enter_context(nc.sbuf_tensor(name, shape, dt))

        def sem(name):
            return ctx.enter_context(nc.semaphore(name))

        total = sb("total_rows", [P, NT, D])
        ps = [ctx.enter_context(nc.psum_tensor(f"ps_bias{u}", [P, 2, 512], F32)) for u in range(2)]
        biased, added, out_done = sem("bias_summed"), sem("added"), sem("node_out")
        sums_in = [sem(f"sums_in{q}") for q in range(NT)]

        def size(t):
            return P if t < NT - 1 else TAIL

        with nc.Block() as block:
            @block.sync
            def _(sp):
                for t in range(NT):
                    sp.dma_start(total[:, t, :], s.sum_dram.ap()[t * P:(t + 1) * P, :]).then_inc(sums_in[t], 16)

            @block.scalar
            def _(act):
                for t in range(NT):
                    act.wait_ge(added, t + 1)
                    act.dma_start(out[t * P:t * P + size(t), :], total[0:size(t), t, :]).then_inc(out_done, 16)
                act.wait_ge(out_done, 16 * NT)

            @block.tensor
            def _(pe):
                for t in range(NT):
                    if t >= 2:
                        pe.wait_ge(added, t - 1)
                    for half in range(2):
                        parts = ((s.gates_hi, s.b2_hi), (s.gates_hi, s.b2_lo), (s.gates_lo, s.b2_hi))
                        for n, (a, b) in enumerate(parts):
                            last = nc.tensor.matmul(ps[t % 2][:, half, 0:HALF], a[:, t * P:(t + 1) * P],
                                                    b[:, half * HALF:(half + 1) * HALF],
                                                    start=(n == 0), stop=(n == 2))
                    last.then_inc(biased, 1)

            @block.vector
            def _(dve):
                for t in range(NT):
                    dve.wait_ge(biased, t + 1)
                    dve.wait_ge(sums_in[t], 16)
                    rows = total[:, t, :].rearrange("p (b d) -> p b d", b=2)
                    nc.vector.tensor_tensor(rows, ps[t % 2][:, :, 0:HALF], rows, ALU.add).then_inc(added, 1)


def program(nc, x, edge_src, edge_dst, w1, att1, bias1, w2, att2, bias2, wg, we, bg, be, ew1, eb1, ew2, eb2, out):
    s = Shared()
    s.early = []
    with ExitStack() as ctx:
        def sb(name, shape, dt=F32, where=ctx, side="left"):
            return where.enter_context(nc.sbuf_tensor(name, shape, dt, side=side))

        s.al_dram = nc.dram_tensor("al_dram", [2 * H1, NP], F32)
        s.mask_dram = nc.dram_tensor("mask_dram", [NT, P, NP], BF16)
        s.rel_dram = nc.dram_tensor("rel_dram", [2 * H1, NP], F32)
        s.z_dram = nc.dram_tensor("z_dram", [H1, N], F32)
        s.zi_dram = nc.dram_tensor("zi_dram", [H1, N], F32)
        s.count_dram = nc.dram_tensor("count_dram", [P, NT, NP], U16)
        s.sum_dram = nc.dram_tensor("sum_dram", [ROWS, D], F32)
        s.table = nc.dram_tensor("table", [ROWS, TW], F32)
        s.ident = sb("ident", [P, P])
        s.column = sb("column", [P, NP], I16)
        s.al_col = sb("al_col", [P, NT, 2 * H1])
        s.al2_col = sb("al2_col", [P, NT, 2])
        s.al_max = sb("al_max", [P, NT, H1])
        with ExitStack() as layer1:
            with ExitStack() as inputs1:
                s.ranges = sb("ranges", [1, 2 * NT], I32, where=inputs1)
                s.block_col = sb("block_col", [P, NT], where=inputs1)
                s.src_f = sb("src_f", [P, ET], where=inputs1)
                s.dst_f = sb("dst_f", [P, ET], where=inputs1)
                s.x_t = sb("x_t", [P, NT, KD, P], where=inputs1)
                s.w1_hi = sb("w1_hi", [P, KD, D], F32R, where=inputs1)
                s.w1_lo = sb("w1_lo", [P, KD, D], F32R, where=inputs1)
                node_features(nc, s, x, w1, edge_src, edge_dst, att1)
                nc.clear_and_free_semaphores(s.early)
                nc.all_engine_barrier()
                s.count = sb("count", [P, NT, NP], U16, where=layer1, side="right")
                s.h_ext = sb("h_ext", [P, NT, H1, C1 + 1], where=layer1, side="right")
                transform_and_count(nc, s)
            g_held = ExitStack()
            s.g_t = sb("g_t", [C1, H1, NP], where=g_held)
            attend_by_head(nc, s, bias1)
        s.gl = sb("gl", [P, NT, G], side="right")
        s.el = sb("el", [P, NT, E], side="right")
        s.rank = sb("rank", [P, NT, E], side="right")
        with ExitStack() as layer2:
            s.h2_hi = sb("h2_hi", [P, NT, D + 4], F32R, where=layer2, side="right")
            s.h2_lo = sb("h2_lo", [P, NT, D + 4], F32R, where=layer2, side="right")
            transform_again(nc, s, w2, att2)
            g_held.close()
            s.prob2 = sb("prob2", [P, NT, NP], where=layer2, side="right")
            attention_again(nc, s)
            mix_and_route(nc, s, x, bias2, wg, we, bg, be)
        with ExitStack() as routing:
            s.tiles = sb("tiles", [1, E], I32, where=routing)
            s.starts = sb("starts", [1, EL], I32, where=routing)
            s.row_at = sb("row_in_tile", [P, NT, EL], BF16, where=routing)
            s.token = sb("token", [P, NT, EL, 2, NT], BF16, where=routing)
            s.token_now = sb("token_now", [P, NT, 2 * NT], BF16, where=routing)
            s.one_row = sb("one_row", [P, NT, P], BF16, where=routing)
            s.lane = sb("lanes", [P, P], BF16, where=routing)
            s.pad_at = sb("pad_at", [P, 1], where=routing)
            s.found = sb("found", [P, 2, NT], where=routing)
            s.list_i = sb("list_i", [P, LIST], I32, where=routing)
            s.gates_hi = sb("gates_hi", [E, NP], F32R, where=routing)
            s.gates_lo = sb("gates_lo", [E, NP], F32R, where=routing)
            s.b2_hi = sb("b2_hi", [E, D], F32R, where=routing)
            s.b2_lo = sb("b2_lo", [E, D], F32R, where=routing)
            s.raw1 = sb("raw1", [P, 2, ROW], where=routing)
            s.raw2 = sb("raw2", [P, 2, ROW], where=routing)
            s.b1_all = sb("b1_all", [P, RING, HID], where=routing)
            s.w1_in, s.w2_in, s.b1_in = (routing.enter_context(nc.semaphore(name))
                                         for name in ("e_w1_in", "e_w2_in", "e_b1_in"))
            plan_experts(nc, s, ew1, eb1, ew2, eb2)
            run_experts(nc, s, ew1, eb1, ew2)
            finish(nc, s, out)


def kernel(**inputs):
    import numpy as np
    import concourse.bacc as bacc
    from concourse.bass_utils import run_bass_kernel_spmd

    def edges(ends):
        padded = np.full(ET * P, -1, np.int32)
        padded[:EDGES] = ends
        return padded.reshape(ET, P).T

    def columns(a):
        return a.reshape(KD, P).T

    a = {name: np.asarray(value) for name, value in inputs.items()}
    gnn = {name[7:]: value for name, value in a.items() if name.startswith("L0_gnn_")}
    ffn = {name[7:]: value for name, value in a.items() if name.startswith("L0_ffn_")}
    x = np.zeros((NP, D), np.float32)
    x[:N] = a["x"]
    laid = {
        "x": x,
        "edge_src": edges(a["src"]),
        "edge_dst": edges(a["dst"]),
        "w1": gnn["W1"],
        "att1": np.stack([columns(gnn["a_src1"]), columns(gnn["a_dst1"])], 1),
        "bias1": gnn["b1"].reshape(H1, C1).T,
        "w2": gnn["W2"],
        "att2": np.concatenate([gnn["a_src2"], gnn["a_dst2"]], 1),
        "bias2": gnn["b2"].reshape(1, D),
        "wg": ffn["Wg"],
        "we": ffn["We"],
        "bg": ffn["bg"].reshape(1, G),
        "be": ffn["be"].reshape(1, E),
        "ew1": ffn["W1"].reshape(E * D, HID),
        "eb1": ffn["b1"].reshape(E, HID),
        "ew2": ffn["W2"].reshape(E * HID, D),
        "eb2": ffn["b2"].reshape(E, D),
    }
    laid = {f"in_{name}": np.ascontiguousarray(value) for name, value in laid.items()}
    nc = bacc.Bacc("TRN2", target_bir_lowering=False, num_devices=1)
    args = [nc.dram_tensor(name, value.shape, mybir.dt.from_np(value.dtype), kind="ExternalInput").ap()
            for name, value in laid.items()]
    out = nc.dram_tensor("out_nodes", (N, D), F32, kind="ExternalOutput")
    program(nc, *args, out.ap())
    ran = run_bass_kernel_spmd(nc, [laid], core_ids=[0])
    return ran.results[0]["out_nodes"]
```
